# Optimizing a Trainium2 kernel written in Bass

```python
import numpy as np
import jax
import jax.numpy as jnp

def _softmax(x, axis=-1):
    return jax.nn.softmax(x, axis=axis)

def _gelu(x):
    return jax.nn.gelu(x, approximate=True)

def _silu(x):
    return jax.nn.silu(x)

def _sigmoid(x):
    return jax.nn.sigmoid(x)

def _layernorm(x, axis=-1, eps=1e-05):
    m = jnp.mean(x, axis=axis, keepdims=True)
    v = jnp.var(x, axis=axis, keepdims=True)
    return (x - m) / jnp.sqrt(v + eps)

def _scatter_add(tgt, idx, src, axis=0):
    return tgt.at[idx].add(src)

def _segment_sum(src, seg, n):
    return jax.ops.segment_sum(src, seg, n)
kernel_name = 'mk_perceiver_d4_seqx_r4_4fa2cb'

def setup_inputs(seed: int=0):
    np.random.seed(seed)
    _w = jnp.asarray

    def _rec_inputs():
        import jax
        import jax.numpy as jnp
        _rk = jax.random.key(seed)
        x = 7.22e-05 + 1 * jax.random.normal(jax.random.fold_in(_rk, 1), (2, 256, 256), jnp.float32)
        _lenS = 256 - jax.random.randint(jax.random.fold_in(_rk, 7), (2,), 0, max(1, 256 // 4) + 1, jnp.int32)
        _lenS2 = 4096 - jax.random.randint(jax.random.fold_in(_rk, 8), (2,), 0, max(1, 4096 // 4) + 1, jnp.int32)
        _ctx_1024P = jax.random.normal(jax.random.fold_in(_rk, 11), (2, 16, 256), jnp.float32)
        _ctx_1024c = jax.random.dirichlet(jax.random.fold_in(_rk, 511), 0.3 * jnp.ones((16,), jnp.float32), (2, 4096))
        _ctx_1024t = jnp.einsum('bsk,bkd->bsd', _ctx_1024c, _ctx_1024P)
        _ctx_1024t = _ctx_1024t * jax.lax.rsqrt(jnp.mean(jnp.square(_ctx_1024t)) + 1e-12) * 0.953939
        ctx_1024 = 4.13588e-05 + 0.999923 * (_ctx_1024t + 0.3 * jax.random.normal(jax.random.fold_in(_rk, 611), (2, 4096, 256), jnp.float32))
        _validS = jnp.arange(256)[None, :] < _lenS[:, None]
        _validS2 = jnp.arange(4096)[None, :] < _lenS2[:, None]
        _causal = jnp.tril(jnp.ones((256, 256), dtype=bool))
        mask_BxS2_ik0 = jnp.where(jnp.broadcast_to(_validS2[:, :], (2, 4096)), 0, 1).astype(jnp.int32)
        return (x, ctx_1024, mask_BxS2_ik0)
    x, ctx_1024, mask_BxS2_ik0 = _rec_inputs()

    def _L0_xattn_setup():
        import jax, jax.numpy as jnp
        import numpy as np
        B, LQ, LK, D = (4, 512, 512, 256)
        H = 16
        HD = D // H

        def _split_heads(x):
            b, l, _ = x.shape
            return x.reshape(b, l, H, HD).transpose(0, 2, 1, 3)
        key = jax.random.key(seed)
        ks = jax.random.split(key, 10)
        s = 0.02
        return {'hidden_states': jax.random.normal(ks[0], (B, LQ, D), jnp.float32), 'context': jax.random.normal(ks[1], (B, LK, D), jnp.float32), 'attention_mask': jax.random.randint(ks[2], (B, LK), 0, 2, jnp.int32), 'q_w': jax.random.normal(ks[3], (D, D), jnp.float32) * s, 'q_b': jnp.zeros((D,), jnp.float32), 'k_w': jax.random.normal(ks[4], (D, D), jnp.float32) * s, 'k_b': jnp.zeros((D,), jnp.float32), 'v_w': jax.random.normal(ks[5], (D, D), jnp.float32) * s, 'v_b': jnp.zeros((D,), jnp.float32)}
    _L0_xattn_all = _L0_xattn_setup()
    _L0_xattn_in = {k: v for k, v in _L0_xattn_all.items() if k in ('q_w', 'q_b', 'k_w', 'k_b', 'v_w', 'v_b')}
    del _L0_xattn_all

    def _L0_attn_setup():
        import jax, jax.numpy as jnp
        import numpy as np
        B, S, D = (2, 512, 256)
        H, DH = (16, 64)
        DQL, DKVL = (128, 128)
        DR = 64
        TOPK = 64
        LN_EPS = 1e-05
        ROPE_BASE = 10000.0

        def _rope_tables(seq_len, dim):
            inv_freq = 1.0 / ROPE_BASE ** (np.arange(0, dim, 2, dtype=np.float32) / dim)
            t = np.arange(seq_len, dtype=np.float32)
            freqs = np.outer(t, inv_freq)
            cos = np.concatenate([np.cos(freqs), np.cos(freqs)], -1)[:, ::2]
            sin = np.concatenate([np.sin(freqs), np.sin(freqs)], -1)[:, ::2]
            return (jnp.asarray(cos), jnp.asarray(sin))

        def _apply_rope_subspace(x, d_rope):
            s = x.shape[-2]
            cos, sin = _rope_tables(s, d_rope)
            xr, xp = (x[..., :d_rope], x[..., d_rope:])
            e, o = (xr[..., 0::2], xr[..., 1::2])
            rot = jnp.stack([e * cos - o * sin, e * sin + o * cos], axis=-1).reshape(xr.shape)
            return jnp.concatenate([rot, xp], axis=-1)

        def _reference_tuple_inner(x, w_down_q, w_down_kv, w_up_q, w_up_k, w_up_v, w_out, ln_scale, ln_bias):
            b, s, d = x.shape
            residual = x
            mu = jnp.mean(x, axis=-1, keepdims=True)
            var = jnp.mean((x - mu) ** 2, axis=-1, keepdims=True)
            h = (x - mu) * jax.lax.rsqrt(var + LN_EPS) * ln_scale + ln_bias
            c_q = h @ w_down_q.T
            c_kv = h @ w_down_kv.T
            q = (c_q @ w_up_q.T).reshape(b, s, H, DH).transpose(0, 2, 1, 3)
            k = (c_kv @ w_up_k.T).reshape(b, s, H, DH).transpose(0, 2, 1, 3)
            v = (c_kv @ w_up_v.T).reshape(b, s, H, DH).transpose(0, 2, 1, 3)
            q = _apply_rope_subspace(q, DR)
            k = _apply_rope_subspace(k, DR)
            scale = 1.0 / np.sqrt(DH).astype(np.float32)
            scores = jnp.einsum('bhqd,bhkd->bhqk', q, k) * scale
            _, indices = jax.lax.top_k(scores, min(TOPK, s))
            attn = jax.nn.softmax(scores, axis=-1)
            out = jnp.einsum('bhqk,bhkd->bhqd', attn, v)
            out = out.transpose(0, 2, 1, 3).reshape(b, s, H * DH)
            out = out @ w_out.T + residual
            return (out, indices.astype(jnp.int64))
        key = jax.random.key(seed)
        ks = jax.random.split(key, 7)
        init = lambda k, shape: jax.random.normal(k, shape, jnp.float32) * 0.02
        return {'x': jax.random.normal(ks[0], (B, S, D), jnp.float32), 'w_down_q': init(ks[1], (DQL, D)), 'w_down_kv': init(ks[2], (DKVL, D)), 'w_up_q': init(ks[3], (H * DH, DQL)), 'w_up_k': init(ks[4], (H * DH, DKVL)), 'w_up_v': init(ks[5], (H * DH, DKVL)), 'w_out': init(ks[6], (D, H * DH)), 'ln_scale': jnp.ones((D,), jnp.float32), 'ln_bias': jnp.zeros((D,), jnp.float32)}
    _L0_attn_all = _L0_attn_setup()
    _L0_attn_in = {k: v for k, v in _L0_attn_all.items() if k in ('w_down_q', 'w_down_kv', 'w_up_q', 'w_up_k', 'w_up_v', 'w_out', 'ln_scale', 'ln_bias')}
    del _L0_attn_all

    def _L0_ffn_setup():
        import jax, jax.numpy as jnp
        import numpy as np
        B, S, D_MODEL, D_HIDDEN = (4, 512, 256, 1024)

        def act_quant(x):
            scale = 127.0 / jnp.clip(jnp.max(jnp.abs(x), axis=-1, keepdims=True), 1e-05)
            return jnp.clip(jnp.round(x * scale), -128, 127) / scale

        def weight_quant(w):
            scale = 1.0 / jnp.clip(jnp.mean(jnp.abs(w)), 1e-05)
            return jnp.clip(jnp.round(w * scale), -1, 1) / scale

        def bit_linear(x, w):
            xq = x + jax.lax.stop_gradient(act_quant(x) - x)
            wq = w + jax.lax.stop_gradient(weight_quant(w) - w)
            return jnp.einsum('bsd,hd->bsh', xq, wq)

        def depthwise_conv1d(x_bcl, w, b):
            y = jax.lax.conv_general_dilated(x_bcl, w, window_strides=(1,), padding=[(1, 1)], dimension_numbers=('NCH', 'OIH', 'NCH'), feature_group_count=x_bcl.shape[1])
            return y + b[None, :, None]
        key = jax.random.key(seed)
        ks = jax.random.split(key, 5)
        lim1 = 1.0 / np.sqrt(D_MODEL)
        lim2 = 1.0 / np.sqrt(D_HIDDEN)
        limc = 1.0 / np.sqrt(3.0)
        return {'x': jax.random.normal(ks[0], (B, S, D_MODEL), dtype=jnp.float32), 'w1': jax.random.uniform(ks[1], (D_HIDDEN, D_MODEL), jnp.float32, -lim1, lim1), 'conv_w': jax.random.uniform(ks[2], (D_HIDDEN, 1, 3), jnp.float32, -limc, limc), 'conv_b': jax.random.uniform(ks[3], (D_HIDDEN,), jnp.float32, -limc, limc), 'w2': jax.random.uniform(ks[4], (D_MODEL, D_HIDDEN), jnp.float32, -lim2, lim2)}
    _L0_ffn_all = _L0_ffn_setup()
    _L0_ffn_in = {k: v for k, v in _L0_ffn_all.items() if k in ('w1', 'conv_w', 'conv_b', 'w2')}
    del _L0_ffn_all

    def _L1_xattn_setup():
        import jax, jax.numpy as jnp
        import numpy as np
        HEADS = 16
        DIM_Q = 256
        DIM_KV = 256
        INNER = 256
        key = jax.random.key(seed)
        k1, k2, k3, k4, k5, k6, k7 = jax.random.split(key, 7)
        B, Lq, Lkv = (2, 512, 1024)
        H = jax.random.normal(k1, (B, Lq, DIM_Q), dtype=jnp.float32)
        T = jax.random.normal(k2, (B, Lkv, DIM_KV), dtype=jnp.float32)
        mask = jax.random.randint(k3, (B, Lkv), 0, 2, dtype=jnp.int32)
        s = 0.02
        Wq = jax.random.normal(k4, (DIM_Q, INNER), dtype=jnp.float32) * s
        Wk = jax.random.normal(k5, (DIM_KV, INNER), dtype=jnp.float32) * s
        Wv = jax.random.normal(k6, (DIM_KV, INNER), dtype=jnp.float32) * s
        Wo = jax.random.normal(k7, (INNER, DIM_Q), dtype=jnp.float32) * s
        return {'H': H, 'T': T, 'mask': mask, 'Wq': Wq, 'Wk': Wk, 'Wv': Wv, 'Wo': Wo}
    _L1_xattn_all = _L1_xattn_setup()
    _L1_xattn_in = {k: v for k, v in _L1_xattn_all.items() if k in ('Wq', 'Wk', 'Wv', 'Wo')}
    del _L1_xattn_all

    def _L1_attn_setup():
        import jax, jax.numpy as jnp
        import numpy as np
        K = 256
        H = 16
        key = jax.random.key(seed)
        ks = jax.random.split(key, 6)
        s = 1.0 / np.sqrt(K)
        return {'x': jax.random.normal(ks[0], (2, 512, K), dtype=jnp.float32), 'Wq': jax.random.uniform(ks[1], (K, K), jnp.float32, -s, s), 'Wk': jax.random.uniform(ks[2], (K, K), jnp.float32, -s, s), 'Wv': jax.random.uniform(ks[3], (K, K), jnp.float32, -s, s), 'Wu': jax.random.uniform(ks[4], (K, K), jnp.float32, -s, s), 'bu': jax.random.uniform(ks[5], (K,), jnp.float32, -s, s)}
    _L1_attn_all = _L1_attn_setup()
    _L1_attn_in = {k: v for k, v in _L1_attn_all.items() if k in ('Wq', 'Wk', 'Wv', 'Wu', 'bu')}
    del _L1_attn_all

    def _L1_ffn_setup():
        import jax, jax.numpy as jnp
        import numpy as np
        B, S, D = (2, 512, 256)
        I = 128
        E = 16
        TOP_K = 2

        def _mlp(x, wg, wu, wd):
            return jnp.einsum('bsi,id->bsd', jax.nn.silu(x @ wg) * (x @ wu), wd)
        key = jax.random.key(seed)
        ks = jax.random.split(key, 10)
        sc_d = 1.0 / np.sqrt(D)
        sc_i = 1.0 / np.sqrt(I)
        return {'x': jax.random.normal(ks[0], (B, S, D), dtype=jnp.float32), 'gate_w': jax.random.normal(ks[1], (D, E), dtype=jnp.float32) * sc_d, 'gate_b': jnp.zeros((E,), dtype=jnp.float32), 'shared_wg': jax.random.normal(ks[2], (D, I), dtype=jnp.float32) * sc_d, 'shared_wu': jax.random.normal(ks[3], (D, I), dtype=jnp.float32) * sc_d, 'shared_wd': jax.random.normal(ks[4], (I, D), dtype=jnp.float32) * sc_i, 'experts_wg': jax.random.normal(ks[5], (E, D, I), dtype=jnp.float32) * sc_d, 'experts_wu': jax.random.normal(ks[6], (E, D, I), dtype=jnp.float32) * sc_d, 'experts_wd': jax.random.normal(ks[7], (E, I, D), dtype=jnp.float32) * sc_i}
    _L1_ffn_all = _L1_ffn_setup()
    _L1_ffn_in = {k: v for k, v in _L1_ffn_all.items() if k in ('gate_w', 'gate_b', 'shared_wg', 'shared_wu', 'shared_wd', 'experts_wg', 'experts_wu', 'experts_wd')}
    del _L1_ffn_all

    def _L2_xattn_setup():
        import jax, jax.numpy as jnp
        import numpy as np
        key = jax.random.key(seed)
        k1, k2 = jax.random.split(key)
        B, N, M, D = (32, 512, 64, 256)
        h_enc = jax.random.normal(k1, (B, N, D), dtype=jnp.float32)
        h_dec = jax.random.normal(k2, (B, M, D), dtype=jnp.float32)
        return {'h_enc': h_enc, 'h_dec': h_dec}
    _L2_xattn_all = _L2_xattn_setup()
    _L2_xattn_in = {k: v for k, v in _L2_xattn_all.items() if k in ()}
    del _L2_xattn_all

    def _L2_attn_setup():
        import jax, jax.numpy as jnp
        import numpy as np
        DIM = 256
        HEADS = 16
        DIM_HEAD = 64
        DIM_INNER = HEADS * DIM_HEAD
        SCALE = DIM_HEAD ** (-0.5)

        def rmsnorm(x, w):
            eps = jnp.asarray(jnp.finfo(x.dtype).eps, x.dtype)
            var = jnp.mean(jnp.square(x), axis=-1, keepdims=True)
            return x * jax.lax.rsqrt(var + eps) * w
        key = jax.random.key(seed)
        ks = jax.random.split(key, 6)
        tokens = jax.random.normal(ks[0], (2, 512, DIM), dtype=jnp.float32)
        norm_w = jnp.ones((DIM,), dtype=jnp.float32)
        Wq = jax.random.normal(ks[1], (DIM, DIM_INNER), dtype=jnp.float32) * 0.02
        Wkv = jax.random.normal(ks[2], (DIM, 2 * DIM_INNER), dtype=jnp.float32) * 0.02
        Wout = jax.random.normal(ks[3], (DIM_INNER, DIM), dtype=jnp.float32) * 0.02
        Wg = jax.random.normal(ks[4], (DIM, HEADS), dtype=jnp.float32) * 0.02
        return {'tokens': tokens, 'norm_w': norm_w, 'Wq': Wq, 'Wkv': Wkv, 'Wout': Wout, 'Wg': Wg}
    _L2_attn_all = _L2_attn_setup()
    _L2_attn_in = {k: v for k, v in _L2_attn_all.items() if k in ('norm_w', 'Wq', 'Wkv', 'Wout', 'Wg')}
    del _L2_attn_all

    def _L2_ffn_setup():
        import jax, jax.numpy as jnp
        import numpy as np
        DIM = 256

        def _reference_tuple_inner(x, W_r, W_k, W_v, mu_r, mu_k):
            B, T, C = x.shape
            x_prev = jnp.concatenate([jnp.zeros((B, 1, C), x.dtype), x[:, :-1, :]], axis=1)
            xr = mu_r * x + (1.0 - mu_r) * x_prev
            xk = mu_k * x + (1.0 - mu_k) * x_prev
            r = jax.nn.sigmoid(jnp.einsum('btc,dc->btd', xr, W_r))
            k = jnp.einsum('btc,dc->btd', xk, W_k)
            k_act = jnp.square(jax.nn.relu(k))
            out = r * jnp.einsum('btc,dc->btd', k_act, W_v)
            new_state = x[:, -1, :]
            return (out, new_state)
        key = jax.random.key(seed)
        ks = jax.random.split(key, 6)
        B, T, C = (8, 512, DIM)
        x = jax.random.normal(ks[0], (B, T, C), dtype=jnp.float32)
        s = 1.0 / np.sqrt(C)
        W_r = jax.random.uniform(ks[1], (C, C), jnp.float32, -s, s)
        W_k = jax.random.uniform(ks[2], (C, C), jnp.float32, -s, s)
        W_v = jax.random.uniform(ks[3], (C, C), jnp.float32, -s, s)
        mu_r = jax.random.uniform(ks[4], (C,), jnp.float32)
        mu_k = jax.random.uniform(ks[5], (C,), jnp.float32)
        return {'x': x, 'W_r': W_r, 'W_k': W_k, 'W_v': W_v, 'mu_r': mu_r, 'mu_k': mu_k}
    _L2_ffn_all = _L2_ffn_setup()
    _L2_ffn_in = {k: v for k, v in _L2_ffn_all.items() if k in ('W_r', 'W_k', 'W_v', 'mu_r', 'mu_k')}
    del _L2_ffn_all

    def _L3_xattn_setup():
        import jax, jax.numpy as jnp
        import numpy as np
        B, N, D = (4, 1024, 256)
        H = 16
        HD = D // H
        EPS = 1e-06
        BASE_SPARSITY = 0.3
        KEEP = max(int((1.0 - BASE_SPARSITY) * HD), 1)
        LEAKY_SLOPE = 0.01

        def _focus(x, focusing_factor):
            x = jnp.abs(jnp.where(x >= 0, x, LEAKY_SLOPE * x)) + EPS
            nrm = x.mean(axis=-1, keepdims=True)
            return jax.nn.softmax(jnp.log(x) * focusing_factor, axis=-1) * nrm

        def _to_heads(x):
            b, n, d = x.shape
            return x.reshape(b, n, H, HD).transpose(0, 2, 1, 3).reshape(b * H, n, HD)

        def _topk_sparsify(x):
            c = x.shape[-1]
            flat = x.reshape(-1, c)
            _, idx = jax.lax.top_k(jnp.abs(flat), KEEP)
            rows = jnp.arange(flat.shape[0])[:, None]
            mask = jnp.zeros(flat.shape, dtype=bool).at[rows, idx].set(True)
            return (flat * mask).reshape(x.shape)
        key = jax.random.key(seed)
        ks = jax.random.split(key, 8)
        mk = lambda k_, shp, s: jax.random.normal(k_, shp, dtype=jnp.float32) * s
        return {'q': mk(ks[0], (B, N, D), 1.0), 'k': mk(ks[1], (B, N, D), 1.0), 'v': mk(ks[2], (B, N, D), 1.0), 'Wq': mk(ks[3], (D, D), 0.02), 'Wk': mk(ks[4], (D, D), 0.02), 'Wv': mk(ks[5], (D, D), 0.02), 'Wp': mk(ks[6], (D, D), 0.02), 'focusing_factor': jnp.asarray(3.0, dtype=jnp.float32)}
    _L3_xattn_all = _L3_xattn_setup()
    _L3_xattn_in = {k: v for k, v in _L3_xattn_all.items() if k in ('Wq', 'Wk', 'Wv', 'Wp', 'focusing_factor')}
    del _L3_xattn_all

    def _L3_attn_setup():
        import jax, jax.numpy as jnp
        import numpy as np
        D_MODEL = 256
        NHEAD = 16
        WIN = 128
        key = jax.random.key(seed)
        k0, k1, k2 = jax.random.split(key, 3)
        B, S = (4, 1024)
        x = jax.random.normal(k0, (B, S, D_MODEL), dtype=jnp.float32)
        Wqkv = jax.random.normal(k1, (D_MODEL, 3 * D_MODEL), dtype=jnp.float32) * 0.02
        bqkv = jnp.zeros((3 * D_MODEL,), dtype=jnp.float32)
        Wout = jax.random.normal(k2, (D_MODEL, D_MODEL), dtype=jnp.float32) * 0.02
        bout = jnp.zeros((D_MODEL,), dtype=jnp.float32)
        return {'x': x, 'Wqkv': Wqkv, 'bqkv': bqkv, 'Wout': Wout, 'bout': bout}
    _L3_attn_all = _L3_attn_setup()
    _L3_attn_in = {k: v for k, v in _L3_attn_all.items() if k in ('Wqkv', 'bqkv', 'Wout', 'bout')}
    del _L3_attn_all

    def _L3_ffn_setup():
        import jax, jax.numpy as jnp
        import numpy as np
        DIM = 256
        DEPTH = 2
        HEADS = 8
        DIM_HEAD = 64
        WINDOW = 128
        INNER = HEADS * DIM_HEAD
        HID = int(DIM * 4 * 2 / 3)
        B, N = (2, 2048)
        QK_SCALE = 8.0

        def shift_token(t):
            t1, t2 = jnp.split(t, 2, axis=-1)
            t2 = jnp.pad(t2, ((0, 0), (1, 0), (0, 0)))[:, :-1]
            return jnp.concatenate([t1, t2], axis=-1)

        def l2norm(t):
            return t / jnp.clip(jnp.linalg.norm(t, axis=-1, keepdims=True), 1e-12)

        def rotate_half(x):
            x1, x2 = jnp.split(x, 2, axis=-1)
            return jnp.concatenate([-x2, x1], axis=-1)

        def rotary_xpos(q, k):
            n = q.shape[-2]
            half_idx = jnp.arange(0, DIM_HEAD, 2, dtype=jnp.float32)
            inv_freq = 1.0 / 10000.0 ** (half_idx / DIM_HEAD)
            t = jnp.arange(n, dtype=jnp.float32)
            freqs = t[:, None] * inv_freq[None, :]
            freqs = jnp.concatenate([freqs, freqs], axis=-1)
            base = (half_idx + 0.4 * DIM_HEAD) / (1.4 * DIM_HEAD)
            power = (t - n // 2) / float(WINDOW // 2)
            scale = base[None, :] ** power[:, None]
            scale = jnp.concatenate([scale, scale], axis=-1)
            cos, sin = (jnp.cos(freqs), jnp.sin(freqs))
            q = q * cos * scale + rotate_half(q) * sin * scale
            k = k * cos / scale + rotate_half(k) * sin / scale
            return (q, k)

        def local_attention(q, k, v):
            b, h, n, d = q.shape
            w = n // WINDOW
            bq = q.reshape(b, h, w, WINDOW, d) * QK_SCALE
            bk = k.reshape(b, h, w, WINDOW, d)
            bv = v.reshape(b, h, w, WINDOW, d)

            def look_around(t):
                p = jnp.pad(t, ((0, 0), (0, 0), (1, 0), (0, 0), (0, 0)))
                return jnp.concatenate([p[:, :, :w], p[:, :, 1:]], axis=3)
            bk, bv = (look_around(bk), look_around(bv))
            bt = jnp.arange(n).reshape(w, WINDOW)
            btp = jnp.pad(bt, ((1, 0), (0, 0)), constant_values=-1)
            btk = jnp.concatenate([btp[:w], btp[1:]], axis=1)
            sim = jnp.einsum('bhwid,bhwjd->bhwij', bq, bk)
            i = bt[:, :, None]
            j = btk[:, None, :]
            mask = (i < j) | (i > j + WINDOW) | (j == -1)
            sim = jnp.where(mask, -jnp.finfo(sim.dtype).max, sim)
            attn = jax.nn.softmax(sim, axis=-1)
            out = jnp.einsum('bhwij,bhwjd->bhwid', attn, bv)
            return out.reshape(b, h, n, d)

        def _layer(x, wqkv, qs, ksc, wo, lg, lb, w1, b1, w2, b2):
            b, n, _ = x.shape
            h = shift_token(x)
            qkv = h @ wqkv
            q, k, v = jnp.split(qkv, 3, axis=-1)
            to_heads = lambda t: t.reshape(b, n, HEADS, DIM_HEAD).transpose(0, 2, 1, 3)
            q, k, v = (to_heads(q), to_heads(k), to_heads(v))
            q = l2norm(q) * qs
            k = l2norm(k) * ksc
            q, k = rotary_xpos(q, k)
            o = local_attention(q, k, v)
            o = o.transpose(0, 2, 1, 3).reshape(b, n, INNER)
            x = x + o @ wo
            h = shift_token(x)
            mu = h.mean(-1, keepdims=True)
            var = h.var(-1, keepdims=True)
            h = (h - mu) / jnp.sqrt(var + 1e-05) * lg + lb
            h = h @ w1 + b1
            a, g = jnp.split(h, 2, axis=-1)
            h = a * jax.nn.gelu(g, approximate=False)
            x = x + h @ w2 + b2
            return x
        key = jax.random.key(seed)
        ks = jax.random.split(key, 6)
        return {'x': jax.random.normal(ks[0], (B, N, DIM), jnp.float32), 'wqkv': jax.random.normal(ks[1], (DEPTH, DIM, 3 * INNER), jnp.float32) * 0.02, 'q_scale': jnp.ones((DEPTH, DIM_HEAD), jnp.float32), 'k_scale': jnp.ones((DEPTH, DIM_HEAD), jnp.float32), 'wo': jax.random.normal(ks[2], (DEPTH, INNER, DIM), jnp.float32) * 0.02, 'ln_g': jnp.ones((DEPTH, DIM), jnp.float32), 'ln_b': jnp.zeros((DEPTH, DIM), jnp.float32), 'w1': jax.random.normal(ks[3], (DEPTH, DIM, 2 * HID), jnp.float32) * 0.02, 'b1': jnp.zeros((DEPTH, 2 * HID), jnp.float32), 'w2': jax.random.normal(ks[4], (DEPTH, HID, DIM), jnp.float32) * 0.02, 'b2': jnp.zeros((DEPTH, DIM), jnp.float32)}
    _L3_ffn_all = _L3_ffn_setup()
    _L3_ffn_in = {k: v for k, v in _L3_ffn_all.items() if k in ('wqkv', 'q_scale', 'k_scale', 'wo', 'ln_g', 'ln_b', 'w1', 'b1', 'w2', 'b2')}
    del _L3_ffn_all
    return {'x': x, 'ctx_1024': ctx_1024, 'mask_BxS2_ik0': mask_BxS2_ik0, 'L0_xattn_q_w': _L0_xattn_in['q_w'], 'L0_xattn_q_b': _L0_xattn_in['q_b'], 'L0_xattn_k_w': _L0_xattn_in['k_w'], 'L0_xattn_k_b': _L0_xattn_in['k_b'], 'L0_xattn_v_w': _L0_xattn_in['v_w'], 'L0_xattn_v_b': _L0_xattn_in['v_b'], 'L0_attn_w_down_q': _L0_attn_in['w_down_q'], 'L0_attn_w_down_kv': _L0_attn_in['w_down_kv'], 'L0_attn_w_up_q': _L0_attn_in['w_up_q'], 'L0_attn_w_up_k': _L0_attn_in['w_up_k'], 'L0_attn_w_up_v': _L0_attn_in['w_up_v'], 'L0_attn_w_out': _L0_attn_in['w_out'], 'L0_attn_ln_scale': _L0_attn_in['ln_scale'], 'L0_attn_ln_bias': _L0_attn_in['ln_bias'], 'L0_ffn_w1': _L0_ffn_in['w1'], 'L0_ffn_conv_w': _L0_ffn_in['conv_w'], 'L0_ffn_conv_b': _L0_ffn_in['conv_b'], 'L0_ffn_w2': _L0_ffn_in['w2'], 'L1_xattn_Wq': _L1_xattn_in['Wq'], 'L1_xattn_Wk': _L1_xattn_in['Wk'], 'L1_xattn_Wv': _L1_xattn_in['Wv'], 'L1_xattn_Wo': _L1_xattn_in['Wo'], 'L1_attn_Wq': _L1_attn_in['Wq'], 'L1_attn_Wk': _L1_attn_in['Wk'], 'L1_attn_Wv': _L1_attn_in['Wv'], 'L1_attn_Wu': _L1_attn_in['Wu'], 'L1_attn_bu': _L1_attn_in['bu'], 'L1_ffn_gate_w': _L1_ffn_in['gate_w'], 'L1_ffn_gate_b': _L1_ffn_in['gate_b'], 'L1_ffn_shared_wg': _L1_ffn_in['shared_wg'], 'L1_ffn_shared_wu': _L1_ffn_in['shared_wu'], 'L1_ffn_shared_wd': _L1_ffn_in['shared_wd'], 'L1_ffn_experts_wg': _L1_ffn_in['experts_wg'], 'L1_ffn_experts_wu': _L1_ffn_in['experts_wu'], 'L1_ffn_experts_wd': _L1_ffn_in['experts_wd'], 'L2_attn_norm_w': _L2_attn_in['norm_w'], 'L2_attn_Wq': _L2_attn_in['Wq'], 'L2_attn_Wkv': _L2_attn_in['Wkv'], 'L2_attn_Wout': _L2_attn_in['Wout'], 'L2_attn_Wg': _L2_attn_in['Wg'], 'L2_ffn_W_r': _L2_ffn_in['W_r'], 'L2_ffn_W_k': _L2_ffn_in['W_k'], 'L2_ffn_W_v': _L2_ffn_in['W_v'], 'L2_ffn_mu_r': _L2_ffn_in['mu_r'], 'L2_ffn_mu_k': _L2_ffn_in['mu_k'], 'L3_xattn_Wq': _L3_xattn_in['Wq'], 'L3_xattn_Wk': _L3_xattn_in['Wk'], 'L3_xattn_Wv': _L3_xattn_in['Wv'], 'L3_xattn_Wp': _L3_xattn_in['Wp'], 'L3_xattn_focusing_factor': _L3_xattn_in['focusing_factor'], 'L3_attn_Wqkv': _L3_attn_in['Wqkv'], 'L3_attn_bqkv': _L3_attn_in['bqkv'], 'L3_attn_Wout': _L3_attn_in['Wout'], 'L3_attn_bout': _L3_attn_in['bout'], 'L3_ffn_wqkv': _L3_ffn_in['wqkv'], 'L3_ffn_q_scale': _L3_ffn_in['q_scale'], 'L3_ffn_k_scale': _L3_ffn_in['k_scale'], 'L3_ffn_wo': _L3_ffn_in['wo'], 'L3_ffn_ln_g': _L3_ffn_in['ln_g'], 'L3_ffn_ln_b': _L3_ffn_in['ln_b'], 'L3_ffn_w1': _L3_ffn_in['w1'], 'L3_ffn_b1': _L3_ffn_in['b1'], 'L3_ffn_w2': _L3_ffn_in['w2'], 'L3_ffn_b2': _L3_ffn_in['b2']}

def reference(x, ctx_1024, mask_BxS2_ik0, L0_xattn_q_w, L0_xattn_q_b, L0_xattn_k_w, L0_xattn_k_b, L0_xattn_v_w, L0_xattn_v_b, L0_attn_w_down_q, L0_attn_w_down_kv, L0_attn_w_up_q, L0_attn_w_up_k, L0_attn_w_up_v, L0_attn_w_out, L0_attn_ln_scale, L0_attn_ln_bias, L0_ffn_w1, L0_ffn_conv_w, L0_ffn_conv_b, L0_ffn_w2, L1_xattn_Wq, L1_xattn_Wk, L1_xattn_Wv, L1_xattn_Wo, L1_attn_Wq, L1_attn_Wk, L1_attn_Wv, L1_attn_Wu, L1_attn_bu, L1_ffn_gate_w, L1_ffn_gate_b, L1_ffn_shared_wg, L1_ffn_shared_wu, L1_ffn_shared_wd, L1_ffn_experts_wg, L1_ffn_experts_wu, L1_ffn_experts_wd, L2_attn_norm_w, L2_attn_Wq, L2_attn_Wkv, L2_attn_Wout, L2_attn_Wg, L2_ffn_W_r, L2_ffn_W_k, L2_ffn_W_v, L2_ffn_mu_r, L2_ffn_mu_k, L3_xattn_Wq, L3_xattn_Wk, L3_xattn_Wv, L3_xattn_Wp, L3_xattn_focusing_factor, L3_attn_Wqkv, L3_attn_bqkv, L3_attn_Wout, L3_attn_bout, L3_ffn_wqkv, L3_ffn_q_scale, L3_ffn_k_scale, L3_ffn_wo, L3_ffn_ln_g, L3_ffn_ln_b, L3_ffn_w1, L3_ffn_b1, L3_ffn_w2, L3_ffn_b2):
    import jax
    import jax.numpy as jnp

    def _L0_xattn_ref(hidden_states, context, attention_mask, q_w, q_b, k_w, k_b, v_w, v_b):
        import jax, jax.numpy as jnp
        import numpy as np
        B, LQ, LK, D = (4, 512, 512, 256)
        H = 16
        HD = D // H

        def _split_heads(x):
            b, l, _ = x.shape
            return x.reshape(b, l, H, HD).transpose(0, 2, 1, 3)
        q = _split_heads(hidden_states @ q_w.T + q_b)
        k = _split_heads(context @ k_w.T + k_b)
        v = _split_heads(context @ v_w.T + v_b)
        scores = jnp.einsum('bhqd,bhkd->bhqk', q, k) / jnp.sqrt(jnp.float32(HD))
        mask = (attention_mask > 0)[:, None, None, :]
        scores = jnp.where(mask, -jnp.inf, scores)
        probs = jax.nn.softmax(scores, axis=-1)
        ctx = jnp.einsum('bhqk,bhkd->bhqd', probs, v)
        ctx = ctx.transpose(0, 2, 1, 3).reshape(ctx.shape[0], ctx.shape[2], H * HD)
        return ctx

    def _L0_attn_ref(x, w_down_q, w_down_kv, w_up_q, w_up_k, w_up_v, w_out, ln_scale, ln_bias):
        import jax, jax.numpy as jnp
        import numpy as np
        B, S, D = (2, 512, 256)
        H, DH = (16, 64)
        DQL, DKVL = (128, 128)
        DR = 64
        TOPK = 64
        LN_EPS = 1e-05
        ROPE_BASE = 10000.0

        def _rope_tables(seq_len, dim):
            inv_freq = 1.0 / ROPE_BASE ** (np.arange(0, dim, 2, dtype=np.float32) / dim)
            t = np.arange(seq_len, dtype=np.float32)
            freqs = np.outer(t, inv_freq)
            cos = np.concatenate([np.cos(freqs), np.cos(freqs)], -1)[:, ::2]
            sin = np.concatenate([np.sin(freqs), np.sin(freqs)], -1)[:, ::2]
            return (jnp.asarray(cos), jnp.asarray(sin))

        def _apply_rope_subspace(x, d_rope):
            s = x.shape[-2]
            cos, sin = _rope_tables(s, d_rope)
            xr, xp = (x[..., :d_rope], x[..., d_rope:])
            e, o = (xr[..., 0::2], xr[..., 1::2])
            rot = jnp.stack([e * cos - o * sin, e * sin + o * cos], axis=-1).reshape(xr.shape)
            return jnp.concatenate([rot, xp], axis=-1)

        def _reference_tuple_inner(x, w_down_q, w_down_kv, w_up_q, w_up_k, w_up_v, w_out, ln_scale, ln_bias):
            b, s, d = x.shape
            residual = x
            mu = jnp.mean(x, axis=-1, keepdims=True)
            var = jnp.mean((x - mu) ** 2, axis=-1, keepdims=True)
            h = (x - mu) * jax.lax.rsqrt(var + LN_EPS) * ln_scale + ln_bias
            c_q = h @ w_down_q.T
            c_kv = h @ w_down_kv.T
            q = (c_q @ w_up_q.T).reshape(b, s, H, DH).transpose(0, 2, 1, 3)
            k = (c_kv @ w_up_k.T).reshape(b, s, H, DH).transpose(0, 2, 1, 3)
            v = (c_kv @ w_up_v.T).reshape(b, s, H, DH).transpose(0, 2, 1, 3)
            q = _apply_rope_subspace(q, DR)
            k = _apply_rope_subspace(k, DR)
            scale = 1.0 / np.sqrt(DH).astype(np.float32)
            scores = jnp.einsum('bhqd,bhkd->bhqk', q, k) * scale
            _, indices = jax.lax.top_k(scores, min(TOPK, s))
            attn = jax.nn.softmax(scores, axis=-1)
            out = jnp.einsum('bhqk,bhkd->bhqd', attn, v)
            out = out.transpose(0, 2, 1, 3).reshape(b, s, H * DH)
            out = out @ w_out.T + residual
            return (out, indices.astype(jnp.int64))
        return _reference_tuple_inner(x, w_down_q, w_down_kv, w_up_q, w_up_k, w_up_v, w_out, ln_scale, ln_bias)[0]

    def _L0_ffn_ref(x, w1, conv_w, conv_b, w2):
        import jax, jax.numpy as jnp
        import numpy as np
        B, S, D_MODEL, D_HIDDEN = (4, 512, 256, 1024)

        def act_quant(x):
            scale = 127.0 / jnp.clip(jnp.max(jnp.abs(x), axis=-1, keepdims=True), 1e-05)
            return jnp.clip(jnp.round(x * scale), -128, 127) / scale

        def weight_quant(w):
            scale = 1.0 / jnp.clip(jnp.mean(jnp.abs(w)), 1e-05)
            return jnp.clip(jnp.round(w * scale), -1, 1) / scale

        def bit_linear(x, w):
            xq = x + jax.lax.stop_gradient(act_quant(x) - x)
            wq = w + jax.lax.stop_gradient(weight_quant(w) - w)
            return jnp.einsum('bsd,hd->bsh', xq, wq)

        def depthwise_conv1d(x_bcl, w, b):
            y = jax.lax.conv_general_dilated(x_bcl, w, window_strides=(1,), padding=[(1, 1)], dimension_numbers=('NCH', 'OIH', 'NCH'), feature_group_count=x_bcl.shape[1])
            return y + b[None, :, None]
        h = bit_linear(x, w1)
        h = depthwise_conv1d(h.transpose(0, 2, 1), conv_w, conv_b)
        h = h.transpose(0, 2, 1)
        h = jax.nn.silu(h)
        return bit_linear(h, w2)

    def _L1_xattn_ref(H, T, mask, Wq, Wk, Wv, Wo):
        import jax, jax.numpy as jnp
        import numpy as np
        HEADS = 16
        DIM_Q = 256
        DIM_KV = 256
        INNER = 256
        B, Lq, _ = H.shape
        Lkv = T.shape[1]
        dph = INNER // HEADS

        def shape(x, L):
            return x.reshape(B, L, HEADS, dph).transpose(0, 2, 1, 3)
        q = shape(H @ Wq, Lq) * dph ** (-0.5)
        k = shape(T @ Wk, Lkv)
        v = shape(T @ Wv, Lkv)
        scores = jnp.einsum('bhqd,bhkd->bhqk', q, k)
        ext = (1.0 - mask.astype(scores.dtype))[:, None, None, :] * jnp.finfo(scores.dtype).min
        scores = scores + ext
        attn = jax.nn.softmax(scores.astype(jnp.float32), axis=-1).astype(scores.dtype)
        out = jnp.einsum('bhqk,bhkd->bhqd', attn, v)
        out = out.transpose(0, 2, 1, 3).reshape(B, Lq, INNER)
        return out @ Wo

    def _L1_attn_ref(x, Wq, Wk, Wv, Wu, bu):
        import jax, jax.numpy as jnp
        import numpy as np
        K = 256
        H = 16
        b, t, k = x.shape
        hd = k // H
        scale = jnp.asarray(k, x.dtype) ** 0.25
        q = (jnp.einsum('btk,ok->bto', x, Wq) / scale).reshape(b, t, H, hd)
        kk = (jnp.einsum('btk,ok->bto', x, Wk) / scale).reshape(b, t, H, hd)
        v = jnp.einsum('btk,ok->bto', x, Wv).reshape(b, t, H, hd)
        dot = jnp.einsum('bthd,bshd->bhts', q, kk)
        att = jax.nn.softmax(dot, axis=-1)
        out = jnp.einsum('bhts,bshd->bthd', att, v).reshape(b, t, k)
        return jnp.einsum('btk,ok->bto', out, Wu) + bu

    def _L1_ffn_ref(x, gate_w, gate_b, shared_wg, shared_wu, shared_wd, experts_wg, experts_wu, experts_wd):
        import jax, jax.numpy as jnp
        import numpy as np
        B, S, D = (2, 512, 256)
        I = 128
        E = 16
        TOP_K = 2

        def _mlp(x, wg, wu, wd):
            return jnp.einsum('bsi,id->bsd', jax.nn.silu(x @ wg) * (x @ wu), wd)
        router_logits = jax.nn.sigmoid(x @ gate_w + gate_b)
        expert_values, expert_indices = jax.lax.top_k(router_logits, k=TOP_K)
        expert_values = expert_values / jnp.sum(expert_values, axis=-1, keepdims=True)
        hg = jnp.einsum('bsd,edi->bsei', x, experts_wg)
        hu = jnp.einsum('bsd,edi->bsei', x, experts_wu)
        all_outputs = jnp.einsum('bsei,eid->bsed', jax.nn.silu(hg) * hu, experts_wd)
        selected = jnp.take_along_axis(all_outputs, expert_indices[..., None], axis=2)
        expert_weighted = jnp.sum(expert_values[..., None] * selected, axis=2)
        return x + _mlp(x, shared_wg, shared_wu, shared_wd) + expert_weighted

    def _L2_xattn_ref(h_enc, h_dec):
        import jax, jax.numpy as jnp
        import numpy as np
        e = jnp.einsum('bnd,bmd->bnm', h_enc, h_dec)
        a = jax.nn.softmax(e, axis=1)
        c = jnp.einsum('bnm,bnd->bmd', a, h_enc)
        return c

    def _L2_attn_ref(tokens, norm_w, Wq, Wkv, Wout, Wg):
        import jax, jax.numpy as jnp
        import numpy as np
        DIM = 256
        HEADS = 16
        DIM_HEAD = 64
        DIM_INNER = HEADS * DIM_HEAD
        SCALE = DIM_HEAD ** (-0.5)

        def rmsnorm(x, w):
            eps = jnp.asarray(jnp.finfo(x.dtype).eps, x.dtype)
            var = jnp.mean(jnp.square(x), axis=-1, keepdims=True)
            return x * jax.lax.rsqrt(var + eps) * w
        b, n, _ = tokens.shape
        x = rmsnorm(tokens, norm_w)
        q = x @ Wq
        kv = x @ Wkv
        k, v = jnp.split(kv, 2, axis=-1)

        def split_heads(t):
            return t.reshape(b, n, HEADS, DIM_HEAD).transpose(0, 2, 1, 3)
        q, k, v = map(split_heads, (q, k, v))
        sim = jnp.einsum('bhid,bhjd->bhij', q, k) * SCALE
        causal_mask = jnp.triu(jnp.ones((n, n), dtype=bool), k=1)
        sim = jnp.where(causal_mask, jnp.asarray(-jnp.finfo(sim.dtype).max, sim.dtype), sim)
        attn = jax.nn.softmax(sim, axis=-1)
        out = jnp.einsum('bhij,bhjd->bhid', attn, v)
        gates = jax.nn.sigmoid(x @ Wg)
        gates = gates.transpose(0, 2, 1)[..., None]
        out = gates * out
        out = out.transpose(0, 2, 1, 3).reshape(b, n, DIM_INNER)
        return out @ Wout

    def _L2_ffn_ref(x, W_r, W_k, W_v, mu_r, mu_k):
        import jax, jax.numpy as jnp
        import numpy as np
        DIM = 256

        def _reference_tuple_inner(x, W_r, W_k, W_v, mu_r, mu_k):
            B, T, C = x.shape
            x_prev = jnp.concatenate([jnp.zeros((B, 1, C), x.dtype), x[:, :-1, :]], axis=1)
            xr = mu_r * x + (1.0 - mu_r) * x_prev
            xk = mu_k * x + (1.0 - mu_k) * x_prev
            r = jax.nn.sigmoid(jnp.einsum('btc,dc->btd', xr, W_r))
            k = jnp.einsum('btc,dc->btd', xk, W_k)
            k_act = jnp.square(jax.nn.relu(k))
            out = r * jnp.einsum('btc,dc->btd', k_act, W_v)
            new_state = x[:, -1, :]
            return (out, new_state)
        return _reference_tuple_inner(x, W_r, W_k, W_v, mu_r, mu_k)[0]

    def _L3_xattn_ref(q, k, v, Wq, Wk, Wv, Wp, focusing_factor):
        import jax, jax.numpy as jnp
        import numpy as np
        B, N, D = (4, 1024, 256)
        H = 16
        HD = D // H
        EPS = 1e-06
        BASE_SPARSITY = 0.3
        KEEP = max(int((1.0 - BASE_SPARSITY) * HD), 1)
        LEAKY_SLOPE = 0.01

        def _focus(x, focusing_factor):
            x = jnp.abs(jnp.where(x >= 0, x, LEAKY_SLOPE * x)) + EPS
            nrm = x.mean(axis=-1, keepdims=True)
            return jax.nn.softmax(jnp.log(x) * focusing_factor, axis=-1) * nrm

        def _to_heads(x):
            b, n, d = x.shape
            return x.reshape(b, n, H, HD).transpose(0, 2, 1, 3).reshape(b * H, n, HD)

        def _topk_sparsify(x):
            c = x.shape[-1]
            flat = x.reshape(-1, c)
            _, idx = jax.lax.top_k(jnp.abs(flat), KEEP)
            rows = jnp.arange(flat.shape[0])[:, None]
            mask = jnp.zeros(flat.shape, dtype=bool).at[rows, idx].set(True)
            return (flat * mask).reshape(x.shape)
        b, n, d = q.shape
        q = q @ Wq.T
        k = k @ Wk.T
        v = v @ Wv.T
        q = _focus(q, focusing_factor)
        k = _focus(k, focusing_factor)
        qh, kh, vh = (_to_heads(q), _to_heads(k), _to_heads(v))
        qh = _topk_sparsify(qh)
        kh = _topk_sparsify(kh)
        length_k = float(n)
        sqrt_l = jnp.sqrt(jnp.asarray(length_k, dtype=q.dtype))
        k_mean = kh.mean(axis=1)
        z_inv = jnp.einsum('bnd,bd->bn', qh, k_mean) + EPS
        kv = jnp.einsum('bnc,bnd->bcd', kh / sqrt_l, vh / sqrt_l)
        y = jnp.einsum('bnc,bcd->bnd', qh, kv) / z_inv[..., None]
        y = y.reshape(b, H, n, HD).transpose(0, 2, 1, 3).reshape(b, n, d)
        return y @ Wp.T

    def _L3_attn_ref(x, Wqkv, bqkv, Wout, bout):
        import jax, jax.numpy as jnp
        import numpy as np
        D_MODEL = 256
        NHEAD = 16
        WIN = 128
        B, S, dm = x.shape
        H, W = (NHEAD, WIN)
        Dh = dm // H
        nb = S // W
        qkv = (x @ Wqkv + bqkv).reshape(B, S, 3, H, Dh)
        q = qkv[:, :, 0].transpose(0, 2, 1, 3)
        k = qkv[:, :, 1].transpose(0, 2, 1, 3)
        v = qkv[:, :, 2].transpose(0, 2, 1, 3)
        qb = q.reshape(B, H, nb, W, Dh)
        kb = k.reshape(B, H, nb, W, Dh)
        vb = v.reshape(B, H, nb, W, Dh)
        kp = jnp.pad(kb, ((0, 0), (0, 0), (1, 1), (0, 0), (0, 0)))
        vp = jnp.pad(vb, ((0, 0), (0, 0), (1, 1), (0, 0), (0, 0)))
        kwin = jnp.concatenate([kp[:, :, :-2], kp[:, :, 1:-1], kp[:, :, 2:]], axis=3)
        vwin = jnp.concatenate([vp[:, :, :-2], vp[:, :, 1:-1], vp[:, :, 2:]], axis=3)
        scale = jnp.float32(1.0 / np.sqrt(dm))
        scores = jnp.einsum('bhnqd,bhnkd->bhnqk', qb, kwin) * scale
        n = jnp.arange(nb)[:, None, None]
        i = jnp.arange(W)[None, :, None]
        j = jnp.arange(3 * W)[None, None, :]
        qpos = n * W + i
        kpos = n * W - W + j
        mask = (jnp.abs(kpos - qpos) <= W) & (kpos >= 0) & (kpos < S)
        scores = jnp.where(mask[None, None], scores, jnp.float32(-1e+30))
        attn = jax.nn.softmax(scores, axis=-1)
        out = jnp.einsum('bhnqk,bhnkd->bhnqd', attn, vwin)
        out = out.reshape(B, H, S, Dh).transpose(0, 2, 1, 3).reshape(B, S, dm)
        return out @ Wout + bout

    def _L3_ffn_ref(x, wqkv, q_scale, k_scale, wo, ln_g, ln_b, w1, b1, w2, b2):
        import jax, jax.numpy as jnp
        import numpy as np
        DIM = 256
        DEPTH = 2
        HEADS = 8
        DIM_HEAD = 64
        WINDOW = 128
        INNER = HEADS * DIM_HEAD
        HID = int(DIM * 4 * 2 / 3)
        B, N = (2, 2048)
        QK_SCALE = 8.0

        def shift_token(t):
            t1, t2 = jnp.split(t, 2, axis=-1)
            t2 = jnp.pad(t2, ((0, 0), (1, 0), (0, 0)))[:, :-1]
            return jnp.concatenate([t1, t2], axis=-1)

        def l2norm(t):
            return t / jnp.clip(jnp.linalg.norm(t, axis=-1, keepdims=True), 1e-12)

        def rotate_half(x):
            x1, x2 = jnp.split(x, 2, axis=-1)
            return jnp.concatenate([-x2, x1], axis=-1)

        def rotary_xpos(q, k):
            n = q.shape[-2]
            half_idx = jnp.arange(0, DIM_HEAD, 2, dtype=jnp.float32)
            inv_freq = 1.0 / 10000.0 ** (half_idx / DIM_HEAD)
            t = jnp.arange(n, dtype=jnp.float32)
            freqs = t[:, None] * inv_freq[None, :]
            freqs = jnp.concatenate([freqs, freqs], axis=-1)
            base = (half_idx + 0.4 * DIM_HEAD) / (1.4 * DIM_HEAD)
            power = (t - n // 2) / float(WINDOW // 2)
            scale = base[None, :] ** power[:, None]
            scale = jnp.concatenate([scale, scale], axis=-1)
            cos, sin = (jnp.cos(freqs), jnp.sin(freqs))
            q = q * cos * scale + rotate_half(q) * sin * scale
            k = k * cos / scale + rotate_half(k) * sin / scale
            return (q, k)

        def local_attention(q, k, v):
            b, h, n, d = q.shape
            w = n // WINDOW
            bq = q.reshape(b, h, w, WINDOW, d) * QK_SCALE
            bk = k.reshape(b, h, w, WINDOW, d)
            bv = v.reshape(b, h, w, WINDOW, d)

            def look_around(t):
                p = jnp.pad(t, ((0, 0), (0, 0), (1, 0), (0, 0), (0, 0)))
                return jnp.concatenate([p[:, :, :w], p[:, :, 1:]], axis=3)
            bk, bv = (look_around(bk), look_around(bv))
            bt = jnp.arange(n).reshape(w, WINDOW)
            btp = jnp.pad(bt, ((1, 0), (0, 0)), constant_values=-1)
            btk = jnp.concatenate([btp[:w], btp[1:]], axis=1)
            sim = jnp.einsum('bhwid,bhwjd->bhwij', bq, bk)
            i = bt[:, :, None]
            j = btk[:, None, :]
            mask = (i < j) | (i > j + WINDOW) | (j == -1)
            sim = jnp.where(mask, -jnp.finfo(sim.dtype).max, sim)
            attn = jax.nn.softmax(sim, axis=-1)
            out = jnp.einsum('bhwij,bhwjd->bhwid', attn, bv)
            return out.reshape(b, h, n, d)

        def _layer(x, wqkv, qs, ksc, wo, lg, lb, w1, b1, w2, b2):
            b, n, _ = x.shape
            h = shift_token(x)
            qkv = h @ wqkv
            q, k, v = jnp.split(qkv, 3, axis=-1)
            to_heads = lambda t: t.reshape(b, n, HEADS, DIM_HEAD).transpose(0, 2, 1, 3)
            q, k, v = (to_heads(q), to_heads(k), to_heads(v))
            q = l2norm(q) * qs
            k = l2norm(k) * ksc
            q, k = rotary_xpos(q, k)
            o = local_attention(q, k, v)
            o = o.transpose(0, 2, 1, 3).reshape(b, n, INNER)
            x = x + o @ wo
            h = shift_token(x)
            mu = h.mean(-1, keepdims=True)
            var = h.var(-1, keepdims=True)
            h = (h - mu) / jnp.sqrt(var + 1e-05) * lg + lb
            h = h @ w1 + b1
            a, g = jnp.split(h, 2, axis=-1)
            h = a * jax.nn.gelu(g, approximate=False)
            x = x + h @ w2 + b2
            return x
        for l in range(DEPTH):
            x = _layer(x, wqkv[l], q_scale[l], k_scale[l], wo[l], ln_g[l], ln_b[l], w1[l], b1[l], w2[l], b2[l])
        return x
    x = x + _L0_xattn_ref(_layernorm(x, axis=-1), ctx_1024, mask_BxS2_ik0, L0_xattn_q_w, L0_xattn_q_b, L0_xattn_k_w, L0_xattn_k_b, L0_xattn_v_w, L0_xattn_v_b)
    x = x + _L0_attn_ref(_layernorm(x, axis=-1), L0_attn_w_down_q, L0_attn_w_down_kv, L0_attn_w_up_q, L0_attn_w_up_k, L0_attn_w_up_v, L0_attn_w_out, L0_attn_ln_scale, L0_attn_ln_bias)
    x = x + _L0_ffn_ref(_layernorm(x, axis=-1), L0_ffn_w1, L0_ffn_conv_w, L0_ffn_conv_b, L0_ffn_w2)
    x = x + _L1_xattn_ref(_layernorm(x, axis=-1), ctx_1024, mask_BxS2_ik0, L1_xattn_Wq, L1_xattn_Wk, L1_xattn_Wv, L1_xattn_Wo)
    x = x + _L1_attn_ref(_layernorm(x, axis=-1), L1_attn_Wq, L1_attn_Wk, L1_attn_Wv, L1_attn_Wu, L1_attn_bu)
    x = x + _L1_ffn_ref(_layernorm(x, axis=-1), L1_ffn_gate_w, L1_ffn_gate_b, L1_ffn_shared_wg, L1_ffn_shared_wu, L1_ffn_shared_wd, L1_ffn_experts_wg, L1_ffn_experts_wu, L1_ffn_experts_wd)
    x = x + _L2_xattn_ref(ctx_1024, _layernorm(x, axis=-1))
    x = x + _L2_attn_ref(_layernorm(x, axis=-1), L2_attn_norm_w, L2_attn_Wq, L2_attn_Wkv, L2_attn_Wout, L2_attn_Wg)
    x = x + _L2_ffn_ref(_layernorm(x, axis=-1), L2_ffn_W_r, L2_ffn_W_k, L2_ffn_W_v, L2_ffn_mu_r, L2_ffn_mu_k)
    x = x + _L3_xattn_ref(_layernorm(x, axis=-1), ctx_1024, ctx_1024, L3_xattn_Wq, L3_xattn_Wk, L3_xattn_Wv, L3_xattn_Wp, L3_xattn_focusing_factor)
    x = x + _L3_attn_ref(_layernorm(x, axis=-1), L3_attn_Wqkv, L3_attn_bqkv, L3_attn_Wout, L3_attn_bout)
    x = x + _L3_ffn_ref(_layernorm(x, axis=-1), L3_ffn_wqkv, L3_ffn_q_scale, L3_ffn_k_scale, L3_ffn_wo, L3_ffn_ln_g, L3_ffn_ln_b, L3_ffn_w1, L3_ffn_b1, L3_ffn_w2, L3_ffn_b2)
    return x

_drawn_inputs = setup_inputs


def setup_inputs(seed=0):
    import zlib

    import numpy as np

    out = dict(_drawn_inputs(seed))
    spreads = {'L0_xattn_q_b': (0.0, 0.8),
     'L0_xattn_k_b': (0.0, 2.0),
     'L0_xattn_v_b': (0.0, 0.1),
     'L0_attn_ln_scale': (1.0, 0.6),
     'L0_attn_ln_bias': (0.0, 0.8),
     'L1_ffn_gate_b': (0.0, 0.1),
     'L2_attn_norm_w': (1.0, 0.6),
     'L3_attn_bqkv': (0.0, 0.8),
     'L3_attn_bout': (0.0, 0.285),
     'L3_ffn_q_scale': (1.0, 0.6),
     'L3_ffn_k_scale': (1.0, 0.6),
     'L3_ffn_ln_g': (1.0, 0.6),
     'L3_ffn_ln_b': (0.0, 0.8),
     'L3_ffn_b1': (0.0, 0.8),
     'L3_ffn_b2': (0.0, 0.8)}
    factors = {'L0_xattn_q_w': 3.846,
     'L0_xattn_k_w': 3.664,
     'L0_attn_w_down_q': 8.0,
     'L0_attn_w_down_kv': 3.694,
     'L0_attn_w_up_q': 8.0,
     'L0_attn_w_up_k': 8.0,
     'L0_attn_w_up_v': 3.859,
     'L0_attn_w_out': 4.293,
     'L1_xattn_Wq': 8.0,
     'L1_xattn_Wk': 7.862,
     'L1_attn_Wq': 8.0,
     'L1_attn_Wk': 8.0,
     'L2_attn_Wq': 8.0,
     'L2_attn_Wkv': 7.243,
     'L2_attn_Wout': 7.531,
     'L2_attn_Wg': 8.0,
     'L2_ffn_W_r': 8.0,
     'L2_ffn_mu_r': 8.0,
     'L2_ffn_mu_k': 4.527,
     'L3_attn_Wqkv': 7.427,
     'L3_attn_Wout': 4.59,
     'L3_ffn_wqkv': 3.912,
     'L3_ffn_wo': 3.863,
     'L3_ffn_w1': 5.421,
     'L3_ffn_w2': 5.395}
    for name, (base, spread) in spreads.items():
        noise = np.random.default_rng([zlib.crc32(name.encode()), seed]).standard_normal(out[name].shape)
        drawn = base * np.exp(spread * noise) if base else spread * noise
        out[name] = jnp.asarray(drawn.astype(out[name].dtype))
    for name, factor in factors.items():
        out[name] = (out[name] * factor).astype(out[name].dtype)
    return out
```

```python
from contextlib import ExitStack

import numpy as np
import concourse.bass as bass
from concourse import mybir

F = mybir.dt.float32
R32 = mybir.dt.float32r
BF = mybir.dt.bfloat16
I32 = mybir.dt.int32
ALU = mybir.AluOpType
ACT = mybir.ActivationFunctionType
AX = mybir.AxisListType.X
BIG = float(2.0 ** 100)
MAGIC = 12582912.0
NT = 4
HID = 682


class Engine:

    def __init__(self, eng, sem):
        self.eng, self.sem, self.n, self.seen = eng, sem, 0, {}
        self.serial = False

    def wait(self, *tokens):
        if self.serial and self.n > self.seen.get(id(self), 0):
            self.eng.wait_ge(self.sem, self.n)
            self.seen[id(self)] = self.n
        for t in tokens:
            if t is None:
                continue
            if isinstance(t, list):
                self.wait(*t)
                continue
            sem, key, value = t
            if self.seen.get(key, 0) < value:
                self.eng.wait_ge(sem, value)
                self.seen[key] = value

    def done(self, ins):
        self.n += 1
        ins.then_inc(self.sem, 1)
        return (self.sem, id(self), self.n)

    def last(self):
        return (self.sem, id(self), self.n) if self.n else None


class Queue:

    def __init__(self, engine, sems):
        self.engine, self.sems, self.count, self.i = engine, sems, [0] * len(sems), 0

    def go(self, out, src, *waits):
        i = self.i
        self.i = (i + 1) % len(self.sems)
        if self.count[i]:
            self.engine.wait((self.sems[i], (id(self), i), self.count[i]))
        self.engine.wait(*waits)
        self.count[i] += 16
        self.engine.eng.dma_start(out, src).then_inc(self.sems[i], 16)
        return (self.sems[i], (id(self), i), self.count[i])


class Slot:

    def __init__(self, ap):
        self.ap, self.free = ap, []


class Ring:
    def __init__(self, aps):
        self.slots, self.i = [Slot(a) for a in aps], 0

    def take(self):
        s = self.slots[self.i]
        self.i = (self.i + 1) % len(self.slots)
        return s


def build(nc, D, out, stage=12):
    ctx = ExitStack()
    with ctx:
        def sb(name, shape, dt=F):
            return ctx.enter_context(nc.sbuf_tensor(name, shape, dt))

        def sem(name):
            return ctx.enter_context(nc.semaphore(name))

        PE = Engine(nc.tensor, sem("s_pe"))
        DV = Engine(nc.vector, sem("s_dve"))
        AC = Engine(nc.scalar, sem("s_act"))
        PO = Engine(nc.gpsimd, sem("s_pool"))
        SP = Engine(nc.sync, sem("s_sp"))
        PO.serial = True
        Q = Queue(SP, [sem(f"s_d{i}") for i in range(100)])

        def now():
            return [PE.last(), DV.last(), AC.last(), PO.last()]

        def mm(o, l, r, *w, start=True, stop=True, inc=None, cols=False):
            PE.wait(*w)
            i = nc.tensor.matmul(o, l, r, start=start, stop=stop, skip_group_check=cols)
            return PE.done(i) if (stop if inc is None else inc) else None

        def tr(o, x, ident, *w):
            PE.wait(*w)
            return PE.done(nc.tensor.transpose(o, x, ident))

        def act(o, x, f, *w, **k):
            AC.wait(*w)
            return AC.done(nc.scalar.activation(o, x, f, **k))

        def ts(o, x, a, b, op0, op1, *w, E=DV, **k):
            E.wait(*w)
            if b is None:
                return E.done(E.eng.tensor_scalar(o, x, a, None, op0, **k))
            return E.done(E.eng.tensor_scalar(o, x, a, b, op0, op1, **k))

        def tt(o, x, y, op, *w, E=DV):
            E.wait(*w)
            return E.done(E.eng.tensor_tensor(o, x, y, op))

        def stt(o, x, s, y, op0, op1, *w, **k):
            DV.wait(*w)
            return DV.done(nc.vector.scalar_tensor_tensor(out=o, in0=x, scalar=s, in1=y, op0=op0, op1=op1, **k))

        def red(o, x, op, *w, **k):
            DV.wait(*w)
            return DV.done(nc.vector.tensor_reduce(o, x, AX, op, **k))

        def cp(o, x, *w, E=DV):
            E.wait(*w)
            if E is AC:
                return E.done(nc.scalar.activation(o, x, ACT.Copy))
            if E is PO:
                return E.done(nc.gpsimd.tensor_scalar(o, x, 1.0, None, ALU.mult))
            return E.done(E.eng.tensor_copy(o, x))

        def rec(o, x, *w):
            DV.wait(*w)
            return DV.done(nc.vector.reciprocal(o, x))

        def fill(o, v, *w, E=PO):
            E.wait(*w)
            return E.done(E.eng.memset(o, v))

        def rsqrt(o, x, c, op, *w):
            a = ts(o, x, c, None, op, None, *w)
            a = act(o, o, ACT.Sqrt, a)
            return rec(o, o, a)

        X = sb("X", [128, NT, 256])
        XN = sb("XN", [128, NT, 256])
        HT = sb("HT", [128, 2, 512])
        WA = sb("WA", [128, 4096])
        WB = sb("WB", [128, 8704])
        WK = sb("WK", [128, 33792])
        idf = sb("idf", [128, 128])
        idb = sb("idb", [128, 128], BF)
        msk = sb("msk", [128, 3, 512], BF)
        sel = sb("sel", [128, 17])
        hm8 = sb("hm8", [128, 8])
        bmask = sb("bmask", [128, 2, 256])
        onesf = sb("onesf", [128, 128])
        XR0 = sb("XR0", [128, 1])
        st = sb("st", [128, NT, 6])
        mv = sb("mv", [128, NT, 2])
        rs = sb("rs", [128, NT])
        sm = sb("sm", [128, 256])
        PS = ctx.enter_context(nc.psum_tensor("PS", [128, 8, 512], F))
        banks = Ring([PS[:, i, :] for i in range(8)])

        def wview(t, a, n, shape=None):
            v = t[:, a:a + n]
            if shape and len(shape) == 2:
                return v.rearrange("p (a b) -> p a b", a=shape[0])
            if shape and len(shape) == 3:
                return v.rearrange("p (a b c) -> p a b c", a=shape[0], b=shape[1])
            return v

        def wload(t, at, name, kt, n, *w, rows=None):
            v = wview(t, at, kt * n, (kt, n))
            src = D[name] if rows is None else rows
            tok = Q.go(v, src.rearrange("(t p) n -> p t n", p=128), *w)
            return v, tok

        def col(name, at, n, *w):
            v = sm[:, at:at + n]
            return v, Q.go(v, D[name], *w)

        cl = [Q.go(idf[:, :], D["c_id"]), Q.go(sel[:, :], D["c_sel"]), Q.go(hm8[:, :], D["c_hm8"]),
              Q.go(bmask[:, :, :], D["c_bmask"].rearrange("(t p) n -> p t n", p=128)),
              Q.go(WK[:, 0:1536], D["c_msk"])]
        xl = Q.go(X[:, :, :], D["x"].rearrange("(t p) n -> p t n", p=128))
        t_ones = fill(onesf[:, :], 1.0)
        cst = [cp(idb[:, :], idf[:, :], cl), cp(msk[:, :, :].rearrange("p a b -> p (a b)"), WK[:, 0:1536], cl), t_ones]
        PE.wait(*cst)

        def layernorm(src, eps, *w, dst=None, E2=PO):
            dst = XN if dst is None else dst
            a = [None] * NT
            for t in range(NT):
                DV.wait(*w)
                a[t] = DV.done(nc.vector.bn_stats(st[:, t, :], src[:, t, :]))
            for t in range(NT):
                DV.wait(a[t])
                a[t] = DV.done(nc.vector.bn_aggr(mv[:, t, :], st[:, t, :]))
            r = rsqrt(rs[:, :], mv[:, :, 1], eps, ALU.add, a[3])
            return [ts(dst[:, t, :], src[:, t, :], mv[:, t, 0:1], rs[:, t:t + 1], ALU.subtract, ALU.mult, r)
                    for t in range(NT)]

        def turn(src, toks, dst, evac=None, n=2, *w):
            o = []
            for f in range(n):
                b = banks.take()
                for t in range(NT):
                    k = tr(b.ap[:, t * 128:(t + 1) * 128], src[:, t, f * 128:(f + 1) * 128], idf[:, :], toks[t], b.free)
                if evac is None:
                    e = cp(dst[:, f, :], b.ap, k, *w, E=(DV, AC)[f % 2])
                else:
                    e = evac(f, b.ap, dst[:, f, :], k)
                b.free = [e]
                o.append(e)
            return o

        def feat(Wt, c0, m, rhs, kt, toks):
            b = banks.take()
            for k in range(kt):
                t = mm(b.ap[0:m, :], Wt[:, k, c0:c0 + m], rhs[:, k, :], toks, b.free, start=k == 0, stop=k == kt - 1)
            return b, t

        def tokp(lhs, kt, t, Wt, c0, n, toks, bank=None, at=0):
            b = bank or banks.take()
            for k in range(kt):
                x = mm(b.ap[:, at:at + n], lhs[:, k, t * 128:(t + 1) * 128], Wt[:, k, c0:c0 + n], toks, b.free,
                       start=k == 0, stop=k == kt - 1)
            return b, x

        def selfattn(units, P, Pn, PT, rsum):
            n = len(units)
            S1, S2 = {}, {}
            ringP, ringN, ringT = Ring(P), Ring(Pn), Ring(PT)
            out = []

            def first(i):
                u = units[i]
                b = banks.take()
                for q in range(2):
                    o = b.ap[:, q * 256:(q + 1) * 256]
                    s = True
                    if u["mask"] is not None:
                        mm(o, idb[:, :], msk[:, u["mask"], q * 256:(q + 1) * 256], b.free, start=True, stop=False)
                        s = False
                    k = mm(o, u["q"][:, q * 128:(q + 1) * 128], u["k"], u["w"], b.free, start=s, stop=True)
                j = i % 4
                nm = rsum[:, j * 8:j * 8 + 2]
                m = red(nm, b.ap.rearrange("p (a b) -> p a b", a=2), ALU.max, k, u_free.get(j), negate=True)
                p = ringP.take()
                ss = rsum[:, j * 8 + 2:j * 8 + 4]
                for q in range(2):
                    e = act(p.ap[:, q * 256:(q + 1) * 256], b.ap[:, q * 256:(q + 1) * 256], ACT.Exp, m, p.free,
                            bias=nm[:, q:q + 1], scale=1.0, accum_out=ss[:, q:q + 1])
                b.free = [e, m]
                r = rec(rsum[:, j * 8 + 4:j * 8 + 6], ss, e)
                rr = rsum[:, j * 8 + 4:j * 8 + 6]
                if u["gate"] is not None:
                    r = tt(rr, rr, u["gate"], ALU.mult, r)
                pn = ringN.take()
                for q in range(2):
                    z = ts(pn.ap[:, q * 256:(q + 1) * 256], p.ap[:, q * 256:(q + 1) * 256], rr[:, q:q + 1], None,
                           ALU.mult, None, r, pn.free, E=PO)
                p.free = [z]
                u_free[j] = z
                S1[i] = (pn, z)

            def second(i):
                pn, z = S1.pop(i)
                b = banks.take()
                for k in range(2):
                    for q in range(2):
                        t = tr(b.ap[:, k * 256 + q * 128:k * 256 + (q + 1) * 128],
                               pn.ap[:, q * 256 + k * 128:q * 256 + (k + 1) * 128], idf[:, :], z, b.free)
                pn.free = [t]
                pt = ringT.take()
                c = cp(pt.ap, b.ap, t, pt.free, E=(DV, AC)[i % 2])
                b.free = [c]
                S2[i] = (pt, c)

            def third(i):
                pt, c = S2.pop(i)
                pt.free = [units[i]["pv"](pt.ap, c)]

            u_free = {}
            for i in range(n + 3):
                if i < n:
                    first(i)
                if 0 <= i - 2 < n:
                    second(i - 2)
                if 0 <= i - 3 < n:
                    third(i - 3)

        def add_out(src, kt, Wt, toks, extra=None, dst=None):
            dst = X if dst is None else dst
            o = []
            for t in range(NT):
                b, k = tokp(src, kt, t, Wt, 0, 256, toks)
                e = tt(dst[:, t, :], b.ap[:, 0:256], dst[:, t, :], ALU.add, k)
                b.free = [e]
                if extra is not None:
                    e = tt(dst[:, t, :], dst[:, t, :], extra[t][0], ALU.add, e, extra[t][1])
                o.append(e)
            return o

        scr = D["scr"]
        mi = WK[:, 2048:2176].bitcast(I32)
        mf = WK[:, 2176:2304]
        ml = Q.go(mi[0:64, :], D["mask_BxS2_ik0"].rearrange("b (t p) -> (b t) p", p=128))
        a = cp(mf[0:64, :], mi[0:64, :], ml)
        mrow = WK[:, 2304:2432].bitcast(BF)
        m0 = ts(mrow[0:64, 0:128], mf[0:64, :], 0.0, -BIG, ALU.is_gt, ALU.mult, a)
        m1a = ts(mf[0:64, :], mf[0:64, :], -1.0, 1.0, ALU.mult, ALU.add, a, m0)
        m1 = ts(mrow[0:64, 128:256], mf[0:64, :], -BIG, None, ALU.mult, None, m1a)
        md = [Q.go(scr[l:l + 1, :].rearrange("a (t p) -> (a t) p", p=128), mrow[0:64, l * 128:(l + 1) * 128], [m0, m1][l])
              for l in range(2)]
        mn = WK[:, 2440:2456]
        a = red(mn[0:64, 0:1], mf[0:64, :], ALU.min, m1)
        b = banks.take()
        a = tr(b.ap[0:1, 0:64], mn[0:64, 0:1], idf[0:64, 0:64], a)
        e = red(mn[0:1, 4:6], b.ap[0:1, 0:64].rearrange("p (a b) -> p a b", a=2), ALU.min, a)
        b.free = [e]
        e = ts(mn[0:1, 6:8], mn[0:1, 4:6], 1.0, None, ALU.is_lt, None, e)
        b = banks.take()
        a = mm(b.ap[:, 0:2], onesf[0:1, :], mn[0:1, 6:8], e)
        anyk = sb("anyk", [128, 2])
        t_any = cp(anyk[:, :], b.ap[:, 0:2], a)
        b.free = [t_any]

        def load_l0x(*w):
            q = wload(WA, 0, "L0x_q", 2, 256, *w)
            k = wload(WA, 512, "L0x_k", 2, 256, *w)
            v = wload(WA, 1024, "L0x_v", 2, 256, *w)
            c = [col("L0x_qb", 0, 2, *w)[1], col("L0x_kb", 2, 2, *w)[1]]
            return dict(q=q[0], k=k[0], v=v[0], tok=[q[1], k[1], v[1]] + c, qb=sm[:, 0:2], kb=sm[:, 2:4])

        def load_l1x(*w):
            r = {}
            tok = []
            for i, n in enumerate("qkvo"):
                r[n], t = wload(WB, 512 * i, "L1x_" + n, 2, 256, *w)
                tok.append(t)
            r["tok"] = tok
            return r

        def crossattn(W, lay, xn_tok):
            start = now() + [xn_tok]
            o = 0

            def part(n, dt=F):
                nonlocal o
                v = WK[:, o:o + n]
                o += n
                return v if dt is F else v.bitcast(dt)

            KS = [part(2048, BF) for _ in range(3)]
            KH, KM, KL = part(2048, BF), part(2048, BF), part(2048, BF)
            CT = Ring([part(1024).rearrange("p (a b) -> p a b", a=2) for _ in range(2)])
            K32 = Ring([part(512) for _ in range(2)])
            V = [part(4832).rearrange("p (a b) -> p a b", a=32) for _ in range(2)]
            PR = Ring([part(1024) for _ in range(3)])
            QS = part(4096, BF).rearrange("p (h t) -> p h t", h=16)
            PV = Ring([part(256) for _ in range(2)])
            mx = part(64)
            mxb = part(32, BF)
            mxr = part(16)
            rd = part(16)
            assert o <= 33792, o
            ones16 = bmask
            q32 = V[1][:, :, :].rearrange("p a b -> p (a b)")[:, 0:1024].rearrange("p (a b) -> p a b", a=2)
            qx = V[1][:, :, :].rearrange("p a b -> p (a b)")
            qp = [qx[:, 1024 + 512 * i:1536 + 512 * i].bitcast(BF).rearrange("p (a b) -> p a b", a=2) for i in range(3)]
            qr = qx[:, 2560:3584].rearrange("p (a b) -> p a b", a=2)
            qt = []
            DV.wait(*start)
            PO.wait(*start)
            AC.wait(*start)
            for m in range(2):
                b, k = feat(W["q"], m * 128, 128, HT, 2, [xn_tok, W["tok"]])
                if lay == 0:
                    e = ts(q32[:, m, :], b.ap, W["qb"][:, m:m + 1], 0.25, ALU.add, ALU.mult, k, W["tok"])
                else:
                    for bb in range(2):
                        e = ts(q32[:, m, bb * 256:(bb + 1) * 256], b.ap[:, bb * 256:(bb + 1) * 256],
                               anyk[:, bb:bb + 1], 0.25, ALU.mult, ALU.mult, k, t_any)
                b.free = [e]
                h = cp(qp[0][:, m, :], q32[:, m, :], e)
                r = tt(qr[:, m, :], q32[:, m, :], qp[0][:, m, :], ALU.subtract, h)
                l = cp(qp[1][:, m, :], qr[:, m, :], r)
                l2 = tt(qp[2][:, m, :], qr[:, m, :], qp[1][:, m, :], ALU.subtract, l)
                qt += [h, l, l2]
            z1 = fill(QS[96:100, :, :], 1.0, start, E=DV)
            z2 = fill(QS[96:99, :, :], 0.0, z1, E=DV)
            qsd = {}
            for hh in range(16):
                m, r0 = hh // 8, (hh % 8) * 16
                for j, s in enumerate((0, 1, 2, 0, 1, 0)):
                    qsd.setdefault(hh, []).append(
                        Q.go(QS[16 * j:16 * j + 16, hh, :], qp[s][r0:r0 + 16, m, :], qt, start))
            qdone = [x for v in qsd.values() for x in v]
            ko = (0, 0, 0, 1, 1, 2)
            kparts = (KH, KM, KL)
            kst = []
            for s in range(3):
                kst.append(fill(KS[s][96:99, :], 1.0, start, E=PO))
            vc = []
            for s in range(2):
                vv = V[s]
                w = qdone if s == 1 else None
                vc.append([fill(vv[:, :, 136:151], 0.0, start, w, E=PO),
                           fill(vv[:, :, 0:136].rearrange("p a (h c) -> p a h c", c=17)[:, :, :, 16], 1.0, start, w, E=PO)])
            kpar_free = [[], ]
            state = dict(kfree=[], vfree=[[], []], ktok={}, vtok={}, kstfree=[[], [], []], stk={})
            pj = [Slot(PS[:, 7, :])]
            pj[0].free = start
            P1 = Ring([PS[:, 4, :], PS[:, 5, :]])
            ST = Ring([PS[:, 0:2, :], PS[:, 2:4, :]])
            PVB = Slot(PS[:, 6, :])
            for s in P1.slots + ST.slots + [PVB]:
                s.free = start
            cT = D["ctxT"]

            def project(g, c):
                bb, m = g // 2, g % 2
                ct = CT.take()
                src = cT[:, bb * 4096 + c * 512:bb * 4096 + (c + 1) * 512].rearrange("(t p) n -> p t n", p=128)
                ld = Q.go(ct.ap, src, start, ct.free)
                b = pj[0]
                for k in range(2):
                    x = mm(b.ap, W["k"][:, k, m * 128:(m + 1) * 128], ct.ap[:, k, :], ld, b.free, W["tok"],
                           start=k == 0, stop=k == 1)
                k32 = K32.take()
                if lay == 0:
                    e = act(k32.ap, b.ap, ACT.Identity, x, k32.free, bias=W["kb"][:, m:m + 1], scale=1.0)
                else:
                    e = act(k32.ap, b.ap, ACT.Copy, x, k32.free)
                b.free = [e]
                sl = slice(c * 512, (c + 1) * 512)
                wf = state["kfree"]
                h = cp(KH[:, sl], k32.ap, e, wf, E=PO)
                r = tt(k32.ap, k32.ap, KH[:, sl], ALU.subtract, h, E=PO)
                m1 = cp(KM[:, sl], k32.ap, r, E=PO)
                l = tt(KL[:, sl], k32.ap, KM[:, sl], ALU.subtract, m1, E=PO)
                k32.free = [l]
                state["ktok"].setdefault(g, []).append(l)
                yield
                vv = V[g % 2]
                for hf in range(2):
                    b = pj[0]
                    for q in range(2):
                        t = hf * 2 + q
                        for k in range(2):
                            x = mm(b.ap[:, q * 128:(q + 1) * 128], ct.ap[:, k, t * 128:(t + 1) * 128],
                                   W["v"][:, k, m * 128:(m + 1) * 128], b.free, start=k == 0, stop=k == 1)
                    dst = vv[:, c * 4 + hf * 2:c * 4 + hf * 2 + 2, 0:136].rearrange("p a (h c) -> p a h c", c=17)
                    for q in range(2):
                        e = cp(dst[:, q, :, 0:16], b.ap[:, q * 128:(q + 1) * 128].rearrange("p (h c) -> p h c", c=16),
                               x, state["vfree"][g % 2], vc[g % 2], E=AC)
                    b.free = [e]
                    state["vtok"].setdefault(g, []).append(e)
                    ct.free = [x]
                    yield

            def stack(s):
                g, hh = s // 8, s % 8
                ks = KS[s % 3]
                tk = state["ktok"][g]
                d = []
                for j, pn in enumerate(ko):
                    d.append(Q.go(ks[16 * j:16 * j + 16, :], kparts[pn][16 * hh:16 * hh + 16, :], tk,
                                  state["kstfree"][s % 3], kst[s % 3]))
                d.append(Q.go(ks[99:100, :], scr[lay:lay + 1, (g // 2) * 4096:(g // 2) * 4096 + 4096], md[lay],
                              state["kstfree"][s % 3]))
                state["stk"][s] = d
                if hh == 7:
                    state["kfree"] = d
            state["mtok"] = {}
            mxfree = [[], []]

            def pass1_steps(s):
                g, hh = s // 8, s % 8
                bb, h = g // 2, (g % 2) * 8 + hh
                ks = KS[s % 3]
                mt = mx[:, (s % 2) * 32:(s % 2) * 32 + 32]
                tk = []
                for q in range(2):
                    for c in range(8):
                        b = P1.take()
                        x = mm(b.ap, QS[0:100, h, bb * 256 + q * 128:bb * 256 + (q + 1) * 128],
                               ks[0:100, c * 512:(c + 1) * 512], state["stk"][s], qsd[h], z2, b.free)
                        e = red(mt[:, q * 8 + c:q * 8 + c + 1], b.ap, ALU.max, x, mxfree[s % 2])
                        b.free = [e]
                        tk.append(e)
                        yield
                state["p1"] = x
                nm = mxr[:, (s % 2) * 8:(s % 2) * 8 + 2]
                r1 = mxr[:, (s % 2) * 8 + 2:(s % 2) * 8 + 4]
                nb = mxb[:, (s % 2) * 8:(s % 2) * 8 + 8].rearrange("p (q c) -> p q c", c=4)
                a = red(nm, mt[:, 0:16].rearrange("p (a b) -> p a b", a=2), ALU.max, tk[-1], mxfree[s % 2], negate=True)
                h1 = cp(nb[:, :, 0], nm, a)
                r = tt(r1, nm, nb[:, :, 0], ALU.subtract, h1)
                h2 = cp(nb[:, :, 1], r1, r)
                h3 = tt(nb[:, :, 2], r1, nb[:, :, 1], ALU.subtract, h2)
                state["mtok"][s] = (nb, [h1, h2, h3])

            def maxrow(s):
                g, hh = s // 8, s % 8
                bb, h = g // 2, (g % 2) * 8 + hh
                nb, w = state["mtok"][s]
                b = pj[0]
                bv = b.ap.bitcast(BF)
                for q in range(2):
                    PE.wait(w, b.free)
                    x = PE.done(nc.tensor.transpose(bv[96:99, q * 128:(q + 1) * 128], nb[:, q, 0:3], idb[:, :]))
                e = cp(QS[96:99, h, bb * 256:bb * 256 + 256], bv[96:99, 0:256], x, state["p1x"])
                b.free = [e]
                mxfree[s % 2] = [x]
                state["mrow"] = e

            def finish(s):
                g, hh = s // 8, s % 8
                bb, h = g // 2, (g % 2) * 8 + hh
                pv = PV.take()
                e = cp(pv.ap, PVB.ap[:, 0:256], state["pvt"], pv.free)
                PVB.free = [e]
                b = pj[0]
                for q in range(2):
                    x = mm(b.ap[:, q * 17:q * 17 + 17], pv.ap[:, q * 128:(q + 1) * 128], sel[:, :], e, b.free)
                pv.free = [x]
                r = rec(rd[:, 0:2], b.ap[:, 0:34].rearrange("p (a b) -> p a b", a=2)[:, :, 16], x, state.get("rdfree"))
                for q in range(2):
                    t = 2 * bb + q
                    if lay == 0:
                        e = stt(X[:, t, 16 * h:16 * h + 16], b.ap[:, q * 17:q * 17 + 16], rd[:, q:q + 1],
                                X[:, t, 16 * h:16 * h + 16], ALU.mult, ALU.add, r)
                    else:
                        e = ts(XN[:, t, 16 * h:16 * h + 16], b.ap[:, q * 17:q * 17 + 16], rd[:, q:q + 1], None,
                               ALU.mult, None, r)
                b.free = [e]
                state["rdfree"] = [e]
                return e

            def projgen(g):
                for c in range(8):
                    yield from project(g, c)

            def drain(it):
                for _ in it:
                    pass

            drain(projgen(0))
            stack(0)
            stack(1)
            drain(pass1_steps(0))
            state["p1x"] = state["p1"]
            maxrow(0)
            NS = 32
            todo = None
            fin = None
            prev = None
            for s in range(NS):
                g, hh = s // 8, s % 8
                bb, h = g // 2, (g % 2) * 8 + hh
                if hh == 0 and g < 3:
                    todo = None
                if hh == 5 and g < 3:
                    pass
                ks = KS[s % 3]
                V_ = V[g % 2]
                p1 = pass1_steps(s + 1) if s + 1 < NS else iter(())
                mrow = state["mrow"]
                pend = []

                def flush(item):
                    c, pr, e = item
                    for j in range(4):
                        x = mm(PVB.ap[32 * j:32 * j + 32, 0:256], V_[:, c * 4 + j, 17 * hh:17 * hh + 32],
                               pr.ap[:, j * 256:(j + 1) * 256], e, PVB.free, state["vtok"][g], start=c == 0,
                               stop=c == 7, inc=(j == 3), cols=True)
                    pr.free = [x]
                    state["pvt"] = x

                for c in range(8):
                    sT = ST.take()
                    for j in range(4):
                        kt = c * 4 + j
                        x = mm(sT.ap[:, j // 2, (j % 2) * 256:(j % 2) * 256 + 256], ks[0:100, kt * 128:(kt + 1) * 128],
                               QS[0:100, h, bb * 256:bb * 256 + 256], mrow, sT.free)
                    pr = PR.take()
                    e = act(pr.ap, sT.ap.rearrange("p a b -> p (a b)"), ACT.Exp, x, pr.free)
                    sT.free = [e]
                    state["lastS"] = x
                    for _ in range(3 if c < 4 else 2):
                        next(p1, None)
                    if c == 1 and prev is not None:
                        fin = finish(prev)
                    pend.append((c, pr, e))
                    if len(pend) > 1:
                        flush(pend.pop(0))
                    if todo is not None and c % 1 == 0:
                        next(todo, None)
                        if hh >= 5:
                            next(todo, None)
                if s == NS - 1:
                    pass
                drain(p1)
                flush(pend.pop(0))
                if hh == 7:
                    state["vfree"][g % 2] = [state["pvt"]]
                state["kstfree"][s % 3] = [state["lastS"]]
                if s + 2 < NS:
                    if (s + 2) % 8 == 0 and todo is not None:
                        drain(todo)
                        todo = None
                    stack(s + 2)
                if s + 1 < NS:
                    state["p1x"] = state["p1"]
                    maxrow(s + 1)
                prev = s
                if hh == 5 and g < 3:
                    todo = projgen(g + 1)
                    state["kneed"] = True
            return finish(prev)

        W = load_l0x()
        ln = layernorm(X, 1e-5, xl)
        ht = turn(XN, ln, HT)
        def load_l0a(*w):
            r, tok = {}, []
            at = 0
            for n, kt, m in (("dq", 2, 128), ("dkv", 2, 128), ("uq", 1, 1024), ("uqs", 1, 1024), ("uk", 1, 1024),
                             ("uks", 1, 1024), ("uv", 1, 1024), ("o", 8, 256), ("C", 1, 512), ("S", 1, 512)):
                r[n], t = wload(WB, at, "L0a_" + n, kt, m, *w)
                at += kt * m
                tok.append(t)
            tok.append(col("L0a_g", 4, 2, *w)[1])
            tok.append(col("L0a_b", 6, 2, *w)[1])
            r["tok"] = tok
            return r

        WL0a = load_l0a()
        vbt = WA[:, 1536:1792]
        tvb = Q.go(vbt, D["L0x_vb"].rearrange("(a n) -> a n", a=1).to_broadcast([128, 256]))
        if "fake0" in D:
            e = Q.go(X[:, :, :], D["fake0"].rearrange("(t p) n -> p t n", p=128), now(), ht)
            cp(XR0[:, :], X[:, 0, 0:1], e)
        else:
            e = crossattn(W, 0, ht)
            for t in range(NT):
                tt(X[:, t, :], X[:, t, :], vbt, ALU.add, e, tvb)
        s0 = now()

        def dump(src):
            o = []
            for t in range(NT):
                o.append(Q.go(out.rearrange("(t p) n -> p t n", p=128)[:, t, :], src[:, t, :], *now()))
            SP.wait(*o)

        if stage == 1:
            dump(X)
            return

        for bk in banks.slots:
            bk.free = list(s0)

        WL0f = [wload(WA, 0, "L0f_w1", 2, 1024, s0), wload(WA, 2048, "L0f_w2", 8, 256, s0)]
        cv = sm[:, 16:48].rearrange("p (a b) -> p a b", a=8)
        WL0f.append((None, Q.go(cv, D["L0f_cv"].rearrange("(t p) n -> p t n", p=128), s0)))

        def heads64(k2, base):
            QZ = wview(WK, 0, 8192, (16, 512))
            return QZ

        QZ = wview(WK, 0, 8192, (16, 512))
        KT = wview(WK, 8192, 4096, (8, 512))
        VT = wview(WK, 12288, 4096, (4, 1024))
        OT = wview(WK, 16384, 4096, (8, 512))
        PP = [wview(WK, 20480 + 512 * i, 512) for i in range(4)]
        PN = [wview(WK, 22528 + 512 * i, 512) for i in range(4)]
        PTT = [wview(WK, 24576 + 512 * i, 512) for i in range(3)]
        TMP = Ring([wview(WK, 26112 + 512 * i, 512) for i in range(6)])
        CQ = wview(WK, 29184, 1024, (2, 512))
        XR = wview(WK, 30208, 1024, (4, 256))
        RS = wview(WK, 31232, 32)

        def zero_halves(w):
            a = fill(QZ[64:128, 0:16:2, :], 0.0, w, E=PO)
            b = fill(QZ[0:64, 1:16:2, :], 0.0, w, E=PO)
            return [a, b]

        zh = zero_halves(s0)
        ln = layernorm(X, 1e-5, s0)
        ln2 = layernorm(XN, 1e-5, ln, dst=XR)
        g_, b_ = sm[:, 4:6], sm[:, 6:8]
        W = WL0a

        def affine(g, bb, tok):
            def ev(f, src, dst, k):
                return ts(dst, src, g[:, f:f + 1], bb[:, f:f + 1], ALU.mult, ALU.add, k, tok)
            return ev

        ht = turn(XR, ln2, HT, affine(g_, b_, W["tok"]))
        cc = []
        for i, n in enumerate(("dq", "dkv")):
            b, k = feat(W[n], 0, 128, HT, 2, [ht, W["tok"]])
            e = cp(CQ[:, i, :], b.ap, k, E=(DV, AC)[i])
            b.free = [e]
            cc.append(e)

        def rope(n, ns, src, m, dsts, sc):
            b, k = feat(W[n], m * 128, 128, src, 1, cc)
            b2, k2 = feat(W[ns], m * 128, 128, src, 1, cc)
            u, v = TMP.take(), TMP.take()
            e1 = stt(u.ap, b.ap, sc, W["C"][:, 0, :], ALU.mult, ALU.mult, k, u.free, W["tok"])
            e2 = stt(v.ap, b2.ap, sc, W["S"][:, 0, :], ALU.mult, ALU.mult, k2, v.free)
            b.free, b2.free = [e1], [e2]
            o = [tt(d, u.ap[p0:p1, :], v.ap[p0:p1, :], ALU.add, e1, e2, E=PO) for d, p0, p1 in dsts]
            u.free = v.free = o
            return o

        qk = []
        for m in range(8):
            qk += rope("uq", "uqs", CQ[:, 0:1, :], m, [(QZ[0:64, 2 * m, :], 0, 64), (QZ[64:128, 2 * m + 1, :], 64, 128)], 0.125)
            qk += rope("uk", "uks", CQ[:, 1:2, :], m, [(KT[:, m, :], 0, 128)], 1.0)
        vt = []

        def vproj(lhs, kt, Wv, c0, toks, dst=None, n=1024):
            o = []
            for t in range(NT):
                for c in range(0, n, 512):
                    b, k = tokp(lhs, kt, t, Wv, c0 + c, 512, toks)
                    e = cp((VT if dst is None else dst)[:, t, c:c + 512], b.ap, k, E=AC)
                    b.free = [e]
                    o.append(e)
            return o

        vt = vproj(CQ[:, 1:2, :], 1, W["uv"], 0, cc)

        def attn64(nh, wts, mask, gate=None, gtok=None, OTv=None):
            OTv = OT if OTv is None else OTv
            units, held = [], {}
            for bb in range(2):
                for h in range(nh):
                    def pv(PTap, c, bb=bb, h=h):
                        j = h % 2
                        if j == 0:
                            held["b"] = banks.take()
                        b = held["b"]
                        for k in range(2):
                            x = mm(b.ap[64 * j:64 * j + 64, 0:256], VT[:, bb * 2 + k, h * 64:(h + 1) * 64],
                                   PTap[:, k * 256:(k + 1) * 256], c, wts, b.free, start=k == 0, stop=k == 1, cols=True)
                        if j == 1:
                            e = cp(OTv[:, h // 2, bb * 256:(bb + 1) * 256], b.ap[:, 0:256], x, E=AC)
                            b.free = [e]
                            held["o"] = e
                        return x
                    units.append(dict(q=QZ[:, h, bb * 256:(bb + 1) * 256], k=KT[:, h // 2, bb * 256:(bb + 1) * 256],
                                      w=wts, mask=mask, pv=pv,
                                      gate=None if gate is None else gate[:, 2 * bb:2 * bb + 2, h]))
            selfattn(units, PP, PN, PTT, RS)
            return held["o"]

        o = attn64(16, [qk[-1], vt[-1], now()], None)
        e = add_out(OT, 8, W["o"], [o], extra=[(XN[:, t, :], None) for t in range(NT)])
        s1 = now()
        if stage == 2:
            dump(X)
            return

        WL1x = load_l1x(s1)
        ln = layernorm(X, 1e-5, s1)
        w1, w2 = WL0f[0][0], WL0f[1][0]
        wt = [x[1] for x in WL0f]
        WQ1 = wview(WK, 0, 2048, (2, 1024))
        WQ2 = wview(WK, 2048, 1024).bitcast(BF).rearrange("p (a b) -> p a b", a=8)
        wtmp = wview(WK, 3072, 2048)
        XQ = wview(WK, 5120, 1024, (4, 256))
        HB = wview(WK, 6144, 4128).rearrange("p (m b t) -> p m b t", m=8, b=2)
        Y = Ring([wview(WK, 10272 + 512 * i, 512) for i in range(3)])
        YT = wview(WK, 11808, 4096, (8, 512))
        HK = wview(WK, 15904, 4096, (4, 1024))
        HQ = wview(WK, 20000, 2048).bitcast(BF).rearrange("p (t n) -> p t n", t=4)
        HQT = wview(WK, 22048, 2048).bitcast(BF).rearrange("p (m t) -> p m t", m=8)
        hq1 = wview(WK, 24096, 2048, (2, 1024))
        wst = wview(WK, 26144, 64)

        def wquant(wap, n, at, dst):
            flat = wap.rearrange("p a b -> p (a b)")
            DV.wait(*wt, *s1)
            a = DV.done(nc.vector.tensor_reduce(wst[:, at:at + 1], flat, AX, ALU.add, apply_absolute_value=True))
            b = banks.take()
            x = mm(b.ap[:, 0:1], onesf[:, :], wst[:, at:at + 1], a, b.free)
            e = ts(wst[:, at + 1:at + 2], b.ap[:, 0:1], 1.0 / n, 1e-5, ALU.mult, ALU.max, x)
            b.free = [e]
            r = rec(wst[:, at + 2:at + 3], wst[:, at + 1:at + 2], e)
            q = ts(wtmp[:, :], flat, wst[:, at + 2:at + 3], MAGIC, ALU.mult, ALU.add, r)
            q = ts(wtmp[:, :], wtmp[:, :], MAGIC, -1.0, ALU.subtract, ALU.max, q)
            q = ts(dst.rearrange("p a b -> p (a b)"), wtmp[:, :], 1.0, None, ALU.min, None, q)
            return q, wst[:, at + 1:at + 2]

        q1, sw1 = wquant(w1, 262144, 0, WQ1)
        q2, sw2 = wquant(w2, 262144, 4, WQ2)

        def aquant(src, t, n, dst, tmp, at, w, back):
            DV.wait(w)
            c = wst[:, at + 3 * t:at + 3 * t + 1]
            c1 = wst[:, at + 3 * t + 1:at + 3 * t + 2]
            c2 = wst[:, at + 3 * t + 2:at + 3 * t + 3]
            a = DV.done(nc.vector.tensor_reduce(c, src, AX, ALU.max, apply_absolute_value=True))
            a = ts(c, c, 1e-5, None, ALU.max, None, a)
            r = rec(c1, c, a)
            i1 = ts(c1, c1, 127.0, None, ALU.mult, None, r)
            i2 = ts(c2, c, 1.0 / 127.0, None, ALU.mult, None, a)
            q = ts(tmp, src, c1, MAGIC, ALU.mult, ALU.add, i1)
            q = ts(tmp, tmp, MAGIC, 127.0, ALU.subtract, ALU.min, q)
            if back:
                return ts(dst, tmp, -128.0, c2, ALU.max, ALU.mult, q, i2), c2
            return ts(dst, tmp, -128.0, None, ALU.max, None, q), c2

        xq = [aquant(XN[:, t, :], t, 256, XQ[:, t, :], hq1[:, 0, t * 256:(t + 1) * 256], 16, ln[t], True)[0] for t in range(NT)]
        ht = turn(XQ, xq, HT)
        z = [fill(HB[:, :, :, 0:1], 0.0, s1), fill(HB[:, :, :, 257:258], 0.0, s1)]
        yt = []
        for m in range(8):
            b, k = feat(WQ1, m * 128, 128, HT, 2, [ht, q1])
            e = act(HB[:, m, :, 1:257], b.ap.rearrange("p (b t) -> p b t", b=2), ACT.Copy, k, z, s1, scale=sw1)
            b.free = [e]
            y = Y.take()
            yv = y.ap.rearrange("p (b t) -> p b t", b=2)
            a = ts(yv, HB[:, m, :, 1:257], cv[:, m, 1:2], cv[:, m, 3:4], ALU.mult, ALU.add, e, y.free)
            a = stt(yv, HB[:, m, :, 0:256], cv[:, m, 0:1], yv, ALU.mult, ALU.add, a)
            a = stt(yv, HB[:, m, :, 2:258], cv[:, m, 2:3], yv, ALU.mult, ALU.add, a)
            e = act(YT[:, m, :], y.ap, ACT.Silu, a)
            y.free = [e]
            yt.append(e)
        hk = []
        for t in range(NT):
            hs = []
            for g in range(2):
                b = banks.take()
                for j in range(4):
                    m = g * 4 + j
                    k = tr(b.ap[:, j * 128:(j + 1) * 128], YT[:, m, t * 128:(t + 1) * 128], idf[:, :], yt[m], b.free)
                e = cp(HK[:, t, g * 512:(g + 1) * 512], b.ap, k, E=AC)
                b.free = [e]
                hs.append(e)
            hk.append(aquant(HK[:, t, :], t, 1024, HQ[:, t, :], hq1[:, t % 2, :], 32, hs, False))
        tq = []
        for m in range(8):
            b = banks.take()
            bv = b.ap.bitcast(BF)
            for t in range(NT):
                k = tr(bv[:, t * 128:(t + 1) * 128], HQ[:, t, m * 128:(m + 1) * 128], idb[:, :], hk[t][0], b.free)
            e = cp(HQT[:, m, :], bv[:, 0:512], k, E=AC)
            b.free = [e]
            tq.append(e)
        for t in range(NT):
            b, k = tokp(HQT, 8, t, WQ2, 0, 256, [tq, q2])
            a = ts(wst[:, 48 + t:49 + t], hk[t][1], sw2, None, ALU.mult, None, hk[t][0], q2)
            e = stt(X[:, t, :], b.ap[:, 0:256], wst[:, 48 + t:49 + t], X[:, t, :], ALU.mult, ALU.add, k, a)
            b.free = [e]
        s2 = now()
        if stage == 3:
            dump(X)
            return

        def load_l1a(*w):
            r, tok, at = {}, [], 0
            for n, kt, m in (("q", 2, 256), ("k", 2, 256), ("v", 2, 512), ("u", 4, 256)):
                r[n], t = wload(WA, at, "L1a_" + n, kt, m, *w)
                at += kt * m
                tok.append(t)
            r["bu"] = WA[:, at:at + 256]
            tok.append(Q.go(WA[:, at:at + 256], D["L1a_bu"].rearrange("(a n) -> a n", a=1).to_broadcast([128, 256]), *w))
            r["tok"] = tok
            return r

        WL1a = load_l1a(s2)
        ln = layernorm(X, 1e-5, s2)
        ht = turn(XN, ln, HT)
        W = WL1x
        if "fake1" in D:
            e = Q.go(X[:, :, :], D["fake1"].rearrange("(t p) n -> p t n", p=128), now(), ht)
            cp(XR0[:, :], X[:, 0, 0:1], e)
        else:
            e = crossattn(W, 1, ht + [PE.last()])
            s3 = now()
            for bk in banks.slots:
                bk.free = list(s3)
            ht = turn(XN, [e] * NT, HT)
            add_out(HT, 2, W["o"], [ht])
        s3 = now()
        if stage == 4:
            dump(X)
            return

        NE = 11
        exp_slots = Ring([WB[:, 768 * i:768 * (i + 1)] for i in range(NE)])
        exq = {}

        def load_expert(i, *w):
            s = exp_slots.take()
            g = s.ap[:, 0:256].rearrange("p (a b) -> p a b", a=2)
            u = s.ap[:, 256:512].rearrange("p (a b) -> p a b", a=2)
            d = s.ap[:, 512:768]
            tk = [Q.go(g, D["L1f_g"][i].rearrange("(t p) n -> p t n", p=128), s.free, *w),
                  Q.go(u, D["L1f_u"][i].rearrange("(t p) n -> p t n", p=128), s.free, *w),
                  Q.go(d, D["L1f_d"][i], s.free, *w)]
            exq[i] = (s, g, u, d, tk)

        for i in range(NE):
            load_expert(i, s3)
        ln = layernorm(X, 1e-5, s3)
        ht = turn(XN, ln, HT)
        KT2 = wview(WK, 8192, 1024, (2, 512))
        VT2 = wview(WK, 12288, 2048, (4, 512))
        OT2 = wview(WK, 16384, 2048, (4, 512))
        hmask = hm8

        def attn16(Wq, Wk, Wv, toks, sc, mask, qb=None, kb=None, vb=None):
            qk, vt = [], []
            for m in range(2):
                b, k = feat(Wq, m * 128, 128, HT, 2, toks)
                u = TMP.take()
                if qb is None:
                    e0 = ts(u.ap, b.ap, sc, None, ALU.mult, None, k, u.free)
                else:
                    e0 = ts(u.ap, b.ap, qb[:, m:m + 1], sc, ALU.add, ALU.mult, k, u.free)
                b.free = [e0]
                for j in range(8):
                    if j % 2:
                        e = ts(QZ[:, m * 8 + j, :], u.ap, hm8[:, j:j + 1], None, ALU.mult, None, e0, E=PO)
                    else:
                        e = act(QZ[:, m * 8 + j, :], u.ap, ACT.Copy, e0, scale=hm8[:, j:j + 1])
                    qk.append(e)
                u.free = qk[-2:]
                b, k = feat(Wk, m * 128, 128, HT, 2, toks)
                if kb is None:
                    e = cp(KT2[:, m, :], b.ap, k, E=DV)
                else:
                    e = ts(KT2[:, m, :], b.ap, kb[:, m:m + 1], None, ALU.add, None, k)
                b.free = [e]
                qk.append(e)
            for t in range(NT):
                b, k = tokp(HT, 2, t, Wv, 0, 512, toks)
                if vb is None:
                    e = cp(VT2[:, t, :], b.ap, k, E=AC)
                else:
                    e = tt(VT2[:, t, :], b.ap, vb, ALU.add, k)
                b.free = [e]
                vt.append(e)
            units, held = [], {}
            wts = qk + vt
            for bb in range(2):
                for h in range(16):
                    def pv(PTap, c, bb=bb, h=h):
                        j = h % 4
                        if j == 0:
                            held["b"] = banks.take()
                        b = held["b"]
                        for k in range(2):
                            x = mm(b.ap[32 * j:32 * j + 32, 0:256], VT2[:, bb * 2 + k, h * 32:(h + 1) * 32],
                                   PTap[:, k * 256:(k + 1) * 256], c, wts, b.free, start=k == 0, stop=k == 1, cols=True)
                        if j == 3:
                            e = cp(OT2[:, h // 4, bb * 256:(bb + 1) * 256], b.ap[:, 0:256], x, E=AC)
                            b.free = [e]
                            held["o"] = e
                        return x
                    units.append(dict(q=QZ[:, h, bb * 256:(bb + 1) * 256], k=KT2[:, h // 8, bb * 256:(bb + 1) * 256],
                                      w=wts, mask=mask, pv=pv, gate=None))
            selfattn(units, PP, PN, PTT, RS)
            return held["o"]

        W = WL1a
        PO.wait(*s3)
        AC.wait(*s3)
        DV.wait(*s3)
        o = attn16(W["q"], W["k"], W["v"], [ht, W["tok"]], 1.0 / 16, None)
        add_out(OT2, 4, W["u"], [o], extra=[(W["bu"], W["tok"])] * NT)
        s4 = now()
        if stage == 5:
            dump(X)
            return

        gw, gt = wload(WA, 0, "L1f_gate", 2, 16, s4)
        gb = WA[:, 32:48]
        gt2 = Q.go(gb, D["L1f_gb"].rearrange("(a n) -> a n", a=1).to_broadcast([128, 16]), s4)
        ll = WA[:, 64:320].rearrange("p (a b) -> p a b", a=16)
        gt3 = Q.go(WA[:, 64:320], D["c_lower"], s4)
        DV.wait(*s4)
        AC.wait(*s4)
        PO.wait(*s4)
        ln = layernorm(X, 1e-5, s4)
        ht = turn(XN, ln, HT)
        G = wview(WK, 0, 64, (4, 16))
        Gr = wview(WK, 64, 64, (4, 16))
        gs = wview(WK, 128, 8)
        cmpA = wview(WK, 256, 256, (16, 16))
        cmpB = wview(WK, 512, 256, (16, 16))
        AT = Ring([wview(WK, 1024 + 512 * i, 512) for i in range(3)])
        SG = Ring([wview(WK, 3072 + 512 * i, 512) for i in range(3)])
        gtok = []
        for t in range(NT):
            b, k = tokp(HT, 2, t, gw, 0, 16, [ht, gt])
            g = G[:, t, :]
            e = tt(g, b.ap[:, 0:16], gb, ALU.add, k, gt2)
            b.free = [e]
            e = act(g, g, ACT.Sigmoid, e)
            gj = g.rearrange("p (a b) -> p a b", a=1).to_broadcast([128, 16, 16])
            gi = g.rearrange("p (a b) -> p a b", b=1).to_broadcast([128, 16, 16])
            c1 = tt(cmpA, gj, gi, ALU.is_equal, e)
            c2 = tt(cmpB, gj, gi, ALU.is_gt, e)
            c1 = tt(cmpA, cmpA, ll, ALU.mult, c1, gt3)
            c1 = tt(cmpA, cmpA, cmpB, ALU.add, c1, c2)
            r = red(Gr[:, t, :], cmpA, ALU.add, c1)
            r = stt(Gr[:, t, :], Gr[:, t, :], 2.0, g, ALU.is_lt, ALU.mult, r)
            e = red(gs[:, t:t + 1], Gr[:, t, :], ALU.add, r)
            e = rec(gs[:, t:t + 1], gs[:, t:t + 1], e)
            gtok.append(ts(g, Gr[:, t, :], gs[:, t:t + 1], None, ALU.mult, None, e))
        xa = [tt(X[:, t, :], X[:, t, :], XN[:, t, :], ALU.add, ln, E=PO) for t in range(NT)]
        for i in range(17):
            s, wg, wu, wd, tk = exq.pop(i)
            b, k = feat(wg, 0, 128, HT, 2, [ht, tk])
            b2, k2 = feat(wu, 0, 128, HT, 2, [ht, tk])
            sg, at = SG.take(), AT.take()
            e = act(sg.ap, b.ap, ACT.Silu, k, sg.free)
            b.free = [e]
            e = tt(at.ap, sg.ap, b2.ap, ALU.mult, e, k2, at.free)
            b2.free = [e]
            sg.free = [e]
            for t in range(0, NT, 2):
                b = banks.take()
                for q in range(2):
                    x = mm(b.ap[:, q * 256:(q + 1) * 256], at.ap[:, (t + q) * 128:(t + q + 1) * 128], wd, e, tk, b.free)
                for q in range(2):
                    sc = 1.0 if i == 16 else G[:, t + q, i:i + 1]
                    xa[t + q] = stt(X[:, t + q, :], b.ap[:, q * 256:(q + 1) * 256], sc, X[:, t + q, :],
                                    ALU.mult, ALU.add, x, xa[t + q], gtok[t + q])
                b.free = [xa[t + 1]]
            at.free = [x]
            s.free = [x]
            if i + NE < 17:
                load_expert(i + NE)
        s5 = now()
        if stage == 6:
            dump(X)
            return

        def load_l2a(*w):
            r, tok, at = {}, [], 0
            for n, kt, m in (("q", 2, 1024), ("kv", 2, 2048), ("o", 8, 256), ("g", 2, 16)):
                r[n], t = wload(WB, at, "L2a_" + n, kt, m, *w)
                at += kt * m
                tok.append(t)
            tok.append(col("L2a_w", 8, 2, *w)[1])
            r["tok"] = tok
            return r

        WL2a = load_l2a(s5)
        for e_ in (DV, AC, PO):
            e_.wait(*s5)
        ln = layernorm(X, 1e-5, s5)
        ht = turn(XN, ln, HT)
        S = [wview(WK, 4096 * i, 4096) for i in range(4)]
        CT = Ring([wview(WK, 16384 + 1024 * i, 1024, (2, 512)) for i in range(3)])
        CN = Ring([wview(WK, 19456 + 2048 * i, 2048, (8, 256)) for i in range(3)])
        PT4 = Ring([wview(WK, 25600 + 512 * i, 512) for i in range(4)])
        mxs = wview(WK, 27648, 64)
        for bb in range(2):
            ev = {0: [], 1: []}
            for c in range(8):
                ct = CT.take()
                src = D["ctxT"][:, bb * 4096 + c * 512:bb * 4096 + (c + 1) * 512].rearrange("(t p) n -> p t n", p=128)
                ld = Q.go(ct.ap, src, s5, ct.free)
                for q in range(2):
                    t = bb * 2 + q
                    b = banks.take()
                    for k in range(2):
                        x = mm(b.ap, HT[:, k, t * 128:(t + 1) * 128], ct.ap[:, k, :], ht, ld, b.free, start=k == 0, stop=k == 1)
                    m = red(mxs[:, t * 16 + c:t * 16 + c + 1], b.ap, ALU.max, x)
                    e = cp(S[t][:, c * 512:(c + 1) * 512], b.ap, m, E=AC)
                    b.free = [e, m]
                    ev[q] = [e, m]
                ct.free = [x]
            ex = []
            for q in range(2):
                t = bb * 2 + q
                m = red(mxs[:, t * 16 + 8:t * 16 + 9], mxs[:, t * 16:t * 16 + 8], ALU.max, ev[q], negate=True)
                e = act(S[t], S[t], ACT.Exp, m, ev[q], bias=mxs[:, t * 16 + 8:t * 16 + 9], scale=1.0,
                        accum_out=mxs[:, t * 16 + 9:t * 16 + 10])
                ex.append(e)
            acc = [banks.take(), banks.take()]
            pend = []

            def pvx(item):
                cn, ld, j0, pts = item
                for q in range(2):
                    pt, c = pts[q]
                    for j in range(4):
                        n = j0 + j
                        x = mm(acc[q].ap[:, 0:256], pt.ap[:, j * 128:(j + 1) * 128], cn.ap[:, n % 8, :], c, ld,
                               acc[q].free, start=n == 0, stop=n == 31, inc=j == 3)
                    pt.free = [x]
                cn.free = [x]
                return x
            TB = [bk for bk in banks.slots if bk not in acc]
            for g in range(8):
                if g % 2 == 0:
                    cn = CN.take()
                    r0 = bb * 4096 + g * 512
                    ld = Q.go(cn.ap, D["ctx"][r0:r0 + 1024, :].rearrange("(t p) n -> p t n", p=128), s5, cn.free)
                pts = []
                for q in range(2):
                    t = bb * 2 + q
                    b = TB[(g * 2 + q) % 6]
                    for j in range(4):
                        n = g * 4 + j
                        x = tr(b.ap[:, j * 128:(j + 1) * 128], S[t][:, n * 128:(n + 1) * 128], idf[:, :], ex[q], b.free)
                    pt = PT4.take()
                    c = cp(pt.ap, b.ap, x, pt.free, E=(DV, AC)[q])
                    b.free = [c]
                    pts.append((pt, c))
                pend.append((cn, ld, g * 4, pts))
                if len(pend) > 1:
                    x = pvx(pend.pop(0))
            x = pvx(pend.pop(0))
            for q in range(2):
                t = bb * 2 + q
                r = rec(mxs[:, t * 16 + 10:t * 16 + 11], mxs[:, t * 16 + 9:t * 16 + 10], ex[q])
                e = stt(X[:, t, :], acc[q].ap[:, 0:256], mxs[:, t * 16 + 10:t * 16 + 11], X[:, t, :], ALU.mult, ALU.add, x, r, ln)
                acc[q].free = [e]
        s6 = now()
        if stage == 7:
            dump(X)
            return

        def load_l2f(*w):
            r, tok = {}, []
            for i, n in enumerate("rkv"):
                r[n], t = wload(WA, 512 * i, "L2f_" + n, 2, 256, *w)
                tok.append(t)
            tok.append(col("L2f_mr", 48, 2, *w)[1])
            tok.append(col("L2f_mk", 50, 2, *w)[1])
            r["tok"] = tok
            return r

        WL2f = load_l2f(s6)
        for e_ in (DV, AC, PO):
            e_.wait(*s6)
        zh = zero_halves(s6)
        ln = layernorm(X, 1e-5, s6)
        W = WL2a
        a = []
        for t in range(NT):
            DV.wait(ln[t])
            a.append(DV.done(nc.vector.bn_stats(st[:, t, :], XN[:, t, :])))
        for t in range(NT):
            DV.wait(a[t])
            a[t] = DV.done(nc.vector.bn_aggr(mv[:, t, :], st[:, t, :]))
        e = tt(rs[:, :], mv[:, :, 0], mv[:, :, 0], ALU.mult, a[3])
        e = tt(rs[:, :], rs[:, :], mv[:, :, 1], ALU.add, e)
        e = rsqrt(rs[:, :], rs[:, :], float(np.finfo(np.float32).eps), ALU.add, e)
        xr = [ts(XR[:, t, :], XN[:, t, :], rs[:, t:t + 1], None, ALU.mult, None, e) for t in range(NT)]

        def scaled(f, src, dst, k):
            return ts(dst, src, sm[:, 8 + f:9 + f], None, ALU.mult, None, k, W["tok"])

        ht = turn(XR, xr, HT, scaled)
        qk = []
        for m in range(8):
            b, k = feat(W["q"], m * 128, 128, HT, 2, [ht, W["tok"]])
            qk.append(ts(QZ[0:64, 2 * m, :], b.ap[0:64, :], 0.125, None, ALU.mult, None, k))
            qk.append(ts(QZ[64:128, 2 * m + 1, :], b.ap[64:128, :], 0.125, None, ALU.mult, None, k))
            b.free = [qk[-1]]
            b, k = feat(W["kv"], m * 128, 128, HT, 2, [ht])
            qk.append(cp(KT[:, m, :], b.ap, k, E=AC))
            b.free = [qk[-1]]
        vt = vproj(HT, 2, W["kv"], 1024, [ht])
        gate = wview(WK, 31264, 64, (4, 16))
        ge = None
        for t in range(NT):
            b, k = tokp(HT, 2, t, W["g"], 0, 16, [ht])
            ge = act(gate[:, t, :], b.ap[:, 0:16], ACT.Sigmoid, k)
            b.free = [ge]
        o = attn64(16, [qk, vt, ge, zh], 0, gate=gate)
        add_out(OT, 8, W["o"], [o])
        s7 = now()
        if stage == 8:
            dump(X)
            return

        def load_l3x(*w):
            r, tok = {}, []
            for i, n in enumerate("qkvp"):
                r[n], t = wload(WB, 512 * i, "L3x_" + n, 2, 256, *w)
                tok.append(t)
            r["ff"] = sm[:, 52:53]
            tok.append(Q.go(sm[:, 52:53], D["L3x_ff"].rearrange("(a n) -> a n", a=1).to_broadcast([128, 1]), *w))
            r["tok"] = tok
            return r

        WL3x = load_l3x(s7)
        for e_ in (DV, AC, PO):
            e_.wait(*s7)
        W = WL2f
        ln = layernorm(X, 1e-5, s7)
        ht = turn(XN, ln, HT)
        XRK = [wview(WK, 1024 * i, 1024, (2, 512)) for i in range(2)]
        XD = wview(WK, 2048, 1024, (2, 512))
        KA = wview(WK, 3072, 1024, (2, 512))
        RR = wview(WK, 4096, 1024, (4, 256))
        d = []
        for f in range(2):
            hv = HT[:, f, :].rearrange("p (b t) -> p b t", b=2)
            dv = XD[:, f, :].rearrange("p (b t) -> p b t", b=2)
            e = tt(dv[:, :, 1:256], hv[:, :, 1:256], hv[:, :, 0:255], ALU.subtract, ht)
            e2 = cp(dv[:, :, 0:1], hv[:, :, 0:1], ht)
            for i in range(2):
                pv_ = XRK[i][:, f, :].rearrange("p (b t) -> p b t", b=2)
                mu = sm[:, 48 + 2 * i + f:49 + 2 * i + f]
                e3 = ts(rs[:, 0:1], mu, -1.0, 1.0, ALU.mult, ALU.add, W["tok"], now())
                e4 = ts(pv_, hv, mu, None, ALU.mult, None, e3)
                e5 = stt(pv_[:, :, 1:256], hv[:, :, 0:255], rs[:, 0:1], pv_[:, :, 1:256], ALU.mult, ALU.add, e3, e4)
                d.append(e5)
        ka = []
        for m in range(2):
            b, k = feat(W["k"], m * 128, 128, XRK[1], 2, [d, W["tok"]])
            e = ts(KA[:, m, :], b.ap, 0.0, None, ALU.max, None, k)
            b.free = [e]
            ka.append(tt(KA[:, m, :], KA[:, m, :], KA[:, m, :], ALU.mult, e))
        for t in range(NT):
            b, k = tokp(XRK[0], 2, t, W["r"], 0, 256, [d])
            e = act(RR[:, t, :], b.ap[:, 0:256], ACT.Sigmoid, k)
            b.free = [e]
            b, k = tokp(KA, 2, t, W["v"], 0, 256, [ka])
            e = tt(RR[:, t, :], b.ap[:, 0:256], RR[:, t, :], ALU.mult, e, k)
            b.free = [e]
            e = tt(X[:, t, :], X[:, t, :], RR[:, t, :], ALU.add, e)
        s8 = now()
        if stage == 9:
            dump(X)
            return

        def load_l3a(*w):
            r, tok, at = {}, [], 0
            for n, kt, m in (("q", 2, 256), ("k", 2, 256), ("v", 2, 512), ("o", 4, 256)):
                r[n], t = wload(WA, at, "L3a_" + n, kt, m, *w)
                at += kt * m
                tok.append(t)
            r["vb"] = WA[:, at:at + 512]
            tok.append(Q.go(r["vb"], D["L3a_vb"].rearrange("(a n) -> a n", a=1).to_broadcast([128, 512]), *w))
            r["ob"] = WA[:, at + 512:at + 768]
            tok.append(Q.go(r["ob"], D["L3a_ob"].rearrange("(a n) -> a n", a=1).to_broadcast([128, 256]), *w))
            tok.append(col("L3a_qb", 54, 2, *w)[1])
            tok.append(col("L3a_kb", 56, 2, *w)[1])
            r["tok"] = tok
            return r

        WL3a = load_l3a(s8)
        for e_ in (DV, AC, PO):
            e_.wait(*s8)
        W = WL3x
        ln = layernorm(X, 1e-5, s8)
        ht = turn(XN, ln, HT)
        NB = 4
        o_ = 0

        def part(n):
            nonlocal o_
            v = WK[:, o_:o_ + n]
            o_ += n
            return v

        CT = Ring([part(1024).rearrange("p (a b) -> p a b", a=2) for _ in range(3)])
        AXR = Ring([part(NB * 256).rearrange("p (a b) -> p a b", a=NB) for _ in range(2)])
        NPR = Ring([part(NB * 304).rearrange("p (a h c) -> p a h c", a=NB, h=16) for _ in range(2)])
        RPR = Ring([part(NB * 304).rearrange("p (a h c) -> p a h c", a=NB, h=16) for _ in range(2)])
        M8R = Ring([part(NB * 128).rearrange("p (a h c) -> p a h c", a=NB, h=16) for _ in range(2)])
        KHR = Ring([part(NB * 256).rearrange("p (a b) -> p a b", a=NB) for _ in range(2)])
        CNR = Ring([part(NB * 260).rearrange("p (a b) -> p a b", a=NB) for _ in range(3)])
        stR = Ring([part(32) for _ in range(3)])
        QH = part(1024).rearrange("p (a b) -> p a b", a=4)
        QHT = part(1024).rearrange("p (a b) -> p a b", a=2)
        GS = part(2 * 2 * 260).rearrange("p (b c n) -> p b c n", b=2, c=2)
        GTs = part(1024).rearrange("p (b f c) -> p b f c", b=2, f=2)
        KV = part(2 * 2 * 272).rearrange("p (b c n) -> p b c n", b=2, c=2)
        YY = part(1024).rearrange("p (a b) -> p a b", a=4)
        YYT = part(1024).rearrange("p (a b) -> p a b", a=2)
        epsc = part(1)
        t_eps = fill(epsc, 1e-6, s8)
        hm16 = part(32).rearrange("p (a b) -> p a b", a=2)
        t_hm = Q.go(hm16, D["c_hm16"].rearrange("(t p) n -> p t n", p=128), s8)
        assert o_ <= 33792
        pad = []
        for s in NPR.slots:
            pad.append(fill(s.ap[:, :, :, 16:19], 5.0, s8))
        for s in CNR.slots:
            pad.append(fill(s.ap[:, :, 256:257], 1.0, s8))
        focR = Ring([PS[:, i, :] for i in range(4)])
        GB = [Slot(PS[:, 4 + i, :]) for i in range(2)]
        for s in focR.slots + GB:
            s.free = list(s8) + [PE.last(), DV.last(), AC.last()]

        def focus(lhs_of, Wm, wtok, dst):
            ax, npr, rpr, m8, sts = AXR.take(), NPR.take(), RPR.take(), M8R.take(), stR.take()
            sv = sts.ap
            e1 = []
            for i in range(NB):
                if i % 2 == 0:
                    b = focR.take()
                lhs, lt = lhs_of(i)
                for k in range(2):
                    x = mm(b.ap[:, (i % 2) * 256:(i % 2) * 256 + 256], lhs[k], Wm[:, k, 0:256], lt, wtok, b.free,
                           start=k == 0, stop=k == 1)
                po = b.ap[:, (i % 2) * 256:(i % 2) * 256 + 256]
                y0 = act(ax.ap[:, i, :], po, ACT.Copy, x, ax.free, scale=-0.01)
                e = stt(ax.ap[:, i, :], ax.ap[:, i, :], 1.0, po, ALU.mult, ALU.max, y0, sts.free,
                        accum_out=sv[:, i:i + 1])
                b.free = [e]
                e1.append(e)
            axf = ax.ap.rearrange("p a b -> p (a b)")
            l = act(axf, axf, ACT.Ln, e1, t_eps, bias=epsc[:, 0:1], scale=1.0)
            z = ts(axf, axf, W["ff"], None, ALU.mult, None, l, W["tok"], E=PO)
            m = red(sv[:, 4:8], ax.ap, ALU.max, z, negate=True)
            e2 = []
            for i in range(NB):
                e2.append(act(ax.ap[:, i, :], ax.ap[:, i, :], ACT.Exp, m, bias=sv[:, 4 + i:5 + i], scale=1.0,
                              accum_out=sv[:, 8 + i:9 + i]))
            n1 = ts(sv[:, 12:16], sv[:, 0:4], 1.0 / 256, 1e-6, ALU.mult, ALU.add, e1[-1])
            r1 = rec(sv[:, 16:20], sv[:, 8:12], e2[-1])
            f = stt(sv[:, 20:24], sv[:, 12:16], -1.0, sv[:, 16:20], ALU.mult, ALU.mult, n1, r1)
            toks = []
            for i in range(NB):
                src = ax.ap[:, i, :].rearrange("p (h c) -> p h c", c=16)[:, :, ::-1]
                e = act(npr.ap[:, i, :, 0:16], src, ACT.Copy, e2[i], npr.free, pad, scale=-1.0)
                if i == NB - 1:
                    ax.free = [e]
                mm8 = []
                for h in range(16):
                    DV.wait(e, m8.free)
                    mm8.append(DV.done(nc.vector.max(m8.ap[:, i, h, :], npr.ap[:, i, h, :])))
                for h in range(16):
                    DV.wait(mm8[h], rpr.free)
                    q = DV.done(nc.vector.match_replace(rpr.ap[:, i, h, :], m8.ap[:, i, h, :], npr.ap[:, i, h, :], 0.0))
                d_, dfree = dst(i)
                o = ts(d_.rearrange("p (h c) -> p h c", c=16), rpr.ap[:, i, :, 0:16][:, :, ::-1], sv[:, 20 + i:21 + i],
                       None, ALU.mult, None, q, f, dfree, E=PO)
                toks.append(o)
            m8.free = [q]
            npr.free = [q]
            rpr.free = [o]
            sts.free = [o]
            return toks

        qh = focus(lambda i: ([HT[:, k, i * 128:(i + 1) * 128] for k in range(2)], ht), W["q"], W["tok"],
                   lambda i: (QH[:, i, :], None))
        SB = [Slot(PS[:, 6 + i, :]) for i in range(2)]
        for s in SB:
            s.free = list(s8) + [PE.last(), DV.last(), AC.last()]
        qht = []
        for f in range(2):
            b = SB[f]
            for t in range(NT):
                k = tr(b.ap[:, t * 128:(t + 1) * 128], QH[:, t, f * 128:(f + 1) * 128], idf[:, :], qh[t], b.free)
            e = cp(QHT[:, f, :], b.ap, k)
            b.free = [e]
            qht.append(e)
        gts = []
        pend = []

        def gram(item):
            kh, cn, ld, toks, bb, g = item
            for i in range(NB):
                n = g * NB + i
                for c in range(2):
                    x = mm(GB[c].ap[:, 0:257], kh.ap[:, i, c * 128:(c + 1) * 128], cn.ap[:, i, 0:257], toks[i], ld,
                           GB[c].free, start=n == 0, stop=n == 31, inc=True)
            kh.free = [x]
            cn.free = [x]
            if g == 7:
                for c in range(2):
                    e = cp(GS[:, bb, c, 0:257], GB[c].ap[:, 0:257], x, E=AC)
                    GB[c].free = [e]
                    gts.append(e)

        for bb in range(2):
            for g in range(8):
                ct = CT.take()
                src = D["ctxT"][:, bb * 4096 + g * 512:bb * 4096 + (g + 1) * 512].rearrange("(t p) n -> p t n", p=128)
                ld = Q.go(ct.ap, src, s8, ct.free)
                cn = CNR.take()
                r0 = bb * 4096 + g * 512
                ld2 = Q.go(cn.ap[:, :, 0:256], D["ctx"][r0:r0 + 512, :].rearrange("(t p) n -> p t n", p=128), s8, cn.free)
                kh = KHR.take()
                toks = focus(lambda i: ([ct.ap[:, k, i * 128:(i + 1) * 128] for k in range(2)], ld), W["k"], W["tok"],
                             lambda i: (kh.ap[:, i, :], kh.free))
                ct.free = [PE.last()]
                pend.append((kh, cn, [ld2, pad], toks, bb, g))
                if len(pend) > 1:
                    gram(pend.pop(0))
        gram(pend.pop(0))
        s8b = now()
        for bk in banks.slots:
            bk.free = list(s8b)
        yv_ = []
        for bb in range(2):
            gt = []
            for f in range(2):
                b = banks.take()
                for c in range(2):
                    k = tr(b.ap[:, c * 128:(c + 1) * 128], GS[:, bb, c, f * 128:(f + 1) * 128], idf[:, :], gts, b.free)
                e = cp(GTs[:, bb, f, :], b.ap[:, 0:256], k)
                b.free = [e]
                gt.append(e)
            kv = []
            for c in range(2):
                b = banks.take()
                for f in range(2):
                    x = mm(b.ap[:, 0:256], GTs[:, bb, f, c * 128:(c + 1) * 128], W["v"][:, f, :], gt, b.free,
                           start=f == 0, stop=f == 1)
                e = stt(KV[:, bb, c, 0:256], b.ap[:, 0:256], 1.0 / 256, bmask[:, c, :], ALU.mult, ALU.mult, x)
                b.free = [e]
                e2 = ts(KV[:, bb, c, 256:272], hm16[:, c, :], GS[:, bb, c, 256:257], 1.0 / 4096, ALU.mult, ALU.mult, t_hm, gts)
                kv += [e, e2]
            for q in range(2):
                t = bb * 2 + q
                b, x = tokp(QHT, 2, t, KV[:, bb, :, :], 0, 272, [kv, qht])
                z = YY[:, t, :]
                zi = mv_ = WK[:, o_ + 16 * t:o_ + 16 * t + 16]
                e = ts(zi, b.ap[:, 256:272], 1e-6, None, ALU.add, None, x)
                e = rec(zi, zi, e)
                e = tt(z.rearrange("p (h c) -> p h c", c=16), b.ap[:, 0:256].rearrange("p (h c) -> p h c", c=16),
                       zi.rearrange("p (h c) -> p h c", c=1).to_broadcast([128, 16, 16]), ALU.mult, e)
                b.free = [e]
                yv_.append(e)
        yt = turn(YY, yv_, YYT)
        add_out(YYT, 2, W["p"], [yt])
        s9 = now()
        if stage == 10:
            dump(X)
            return

        def load_l3f(l, t_, w):
            r, tok, at = {}, [], 0
            for n, kt, m in (("qkv", 2, 1536), ("o", 4, 256), ("w2", 6, 256)):
                r[n], t = wload(t_, at, f"L3f_{n}{l}", kt, m, w)
                at += kt * m
                tok.append(t)
            return r, tok, at

        WL3f, tk3, at3 = load_l3f(0, WB, s9)
        WL3f["w1"], t = wload(WB, at3, "L3f_w10", 2, 1536, s9)
        tk3.append(t)
        for e_ in (DV, AC, PO):
            e_.wait(*s9)
        W = WL3a
        ln = layernorm(X, 1e-5, s9)
        ht = turn(XN, ln, HT)
        o = attn16(W["q"], W["k"], W["v"], [ht, W["tok"]], 1.0 / 16, 1, qb=sm[:, 54:56], kb=sm[:, 56:58], vb=W["vb"])
        add_out(OT2, 4, W["o"], [o], extra=[(W["ob"], W["tok"])] * NT)
        s10 = now()
        if stage == 11:
            dump(X)
            return

        for e_ in (DV, AC, PO):
            e_.wait(*s10)
        ln = layernorm(X, 1e-5, s10)
        XL = XN
        xtok = ln
        tab = wview(WA, 0, 1024, (4, 256))
        ttab = Q.go(tab, D["L3f_tab"].rearrange("(t p) n -> p t n", p=128), s10)
        zrow = WA[:, 1024:1152]
        tz = fill(zrow, 0.0, s10)
        QT_ = wview(WK, 26112, 0) if False else None
        QN = wview(WK, 20480, 2048, (4, 512))
        QN2 = wview(WK, 22528, 2048, (4, 512))
        sq = Ring([wview(WK, 24576 + 512 * i, 512) for i in range(3)])
        XS = wview(WK, 30208, 1024, (4, 256))
        OT3 = wview(WK, 16384, 2048, (4, 512))
        for l in range(2):
            W = WL3f
            sl = now()
            for e_ in (DV, AC, PO):
                e_.wait(*sl)
            wx = [xtok, sl]
            small = [Q.go(WA[:, 1152 + 64 * i:1216 + 64 * i],
                          D[n][l:l + 1, :].to_broadcast([128, 64]), sl)
                     for i, n in enumerate(("L3f_qs", "L3f_ks"))]
            small.append(Q.go(WA[:, 1280:1536], D["L3f_b2"][l:l + 1, :].to_broadcast([128, 256]), sl))
            small.append(Q.go(sm[:, 64:76], D["L3f_b1"][l], sl))
            small.append(Q.go(sm[:, 76:78], D["L3f_lg"][l], sl))
            small.append(Q.go(sm[:, 78:80], D["L3f_lb"][l], sl))
            zh = zero_halves(sl)
            zz = fill(HT[:, 1, :].rearrange("p (b t) -> p b t", b=2)[:, :, 0:1], 0.0, sl)

            def shifted(f, src, dst, k):
                if f == 0:
                    return cp(dst, src, k)
                sv = src.rearrange("p (b t) -> p b t", b=2)
                dv = dst.rearrange("p (b t) -> p b t", b=2)
                return cp(dv[:, :, 1:256], sv[:, :, 0:255], k, zz)

            ht = turn(XL, [xtok] * NT, HT, shifted)
            fin = []
            for which in range(2):
                QQ = (QN, QN2)[which]
                s_ = WA[:, 1152 + 64 * which:1216 + 64 * which]
                qq = []
                for t in range(NT):
                    b, k = tokp(HT, 2, t, W["qkv"], 512 * which, 512, [ht, zz, tk3])
                    s = sq.take()
                    e = act(s.ap, b.ap, ACT.Square, k, s.free, sl)
                    rr = rs2 = wview(WK, 31300 + (which * 4 + t) * 16, 8)
                    e = red(rr, s.ap.rearrange("p (h d) -> p h d", d=64), ALU.add, e)
                    s.free = [e]
                    e = rsqrt(rr, rr, 1e-24, ALU.max, e)
                    q3 = QQ[:, t, :].rearrange("p (h d) -> p h d", d=64)
                    e = tt(q3, b.ap.rearrange("p (h d) -> p h d", d=64),
                           rr.rearrange("p (h d) -> p h d", d=1).to_broadcast([128, 8, 64]), ALU.mult, e)
                    b.free = [e]
                    e = tt(q3, q3, s_.rearrange("p (h d) -> p h d", h=1).to_broadcast([128, 8, 64]), ALU.mult, e, small)
                    C = tab[:, t, 0:64] if which == 0 else tab[:, t, 128:192]
                    Sn = tab[:, t, 64:128] if which == 0 else tab[:, t, 192:256]
                    s = sq.take()
                    s3 = s.ap.rearrange("p (h d) -> p h d", d=64)
                    Sb = Sn.rearrange("p (h d) -> p h d", h=1)
                    e2 = tt(s3[:, :, 0:32], q3[:, :, 32:64], Sb[:, :, 0:32].to_broadcast([128, 8, 32]), ALU.mult, e, s.free, ttab, E=PO)
                    e2 = tt(s3[:, :, 32:64], q3[:, :, 0:32], Sb[:, :, 32:64].to_broadcast([128, 8, 32]), ALU.mult, e, E=PO)
                    e = tt(q3, q3, C.rearrange("p (h d) -> p h d", h=1).to_broadcast([128, 8, 64]), ALU.mult, e, e2, ttab)
                    e = tt(QQ[:, t, :], QQ[:, t, :], s.ap, ALU.add, e, e2)
                    s.free = [e]
                    qq.append(e)
                for m in range(4):
                    b = banks.take()
                    for t in range(NT):
                        k = tr(b.ap[:, t * 128:(t + 1) * 128], QQ[:, t, m * 128:(m + 1) * 128], idf[:, :], qq[t], b.free)
                    if which == 0:
                        e = cp(QZ[0:64, 2 * m, :], b.ap[0:64, :], k, zh, E=DV)
                        e2 = cp(QZ[64:128, 2 * m + 1, :], b.ap[64:128, :], k, zh, E=AC)
                        b.free = [e, e2]
                        fin += [e, e2]
                    else:
                        e = cp(KT[:, m, :], b.ap, k, E=AC)
                        b.free = [e]
                        fin.append(e)
            vt = vproj(HT, 2, W["qkv"], 1024, [ht, zz, tk3], n=512)
            o = attn64(8, [fin, vt, zh, now()], 2, OTv=OT3)
            e = add_out(OT3, 4, W["o"], [o], dst=XL)
            sh = []
            for t in range(NT):
                sh.append(Q.go(XS[1:128, t, 128:256], XL[0:127, t, 128:256], e))
                if t % 2 == 0:
                    sh.append(Q.go(XS[0:1, t, 128:256], zrow[0:1, 0:128], tz, e))
                else:
                    sh.append(Q.go(XS[0:1, t, 128:256], XL[127:128, t - 1, 128:256], e))
                sh.append(cp(XS[:, t, 0:128], XL[:, t, 0:128], e, E=PO))
            ln = layernorm(XS, 1e-5, sh, dst=XS)
            ht = turn(XS, ln, HT, affine(sm[:, 76:78], sm[:, 78:80], small))
            if l == 0:
                sw = now()
                nxt, tkn = {}, []
                for n, kt, m, at in (("qkv", 2, 1536, 0), ("o", 4, 256, 3072)):
                    nxt[n], t = wload(WB, at, f"L3f_{n}1", kt, m, sw)
                    tkn.append(t)
            AG = wview(WK, 0, 3072, (6, 512))
            GG = Ring([wview(WK, 3072 + 512 * i, 512) for i in range(3)])
            sA = now()
            ag = []
            for m in range(6):
                b, k = feat(W["w1"], m * 128, 128, HT, 2, [ht, tk3])
                b2, k2 = feat(W["w1"], 768 + m * 128, 128, HT, 2, [ht])
                g = GG.take()
                e = act(g.ap, b2.ap, ACT.Gelu, k2, small, g.free, sA, bias=sm[:, 70 + m:71 + m], scale=1.0)
                b2.free = [e]
                e = stt(AG[:, m, :], b.ap, sm[:, 64 + m:65 + m], g.ap, ALU.add, ALU.mult, e, k, small)
                b.free = [e]
                g.free = [e]
                ag.append(e)
            e = add_out(AG, 6, W["w2"] if l == 0 else W["w2"], [ag], extra=[(WA[:, 1280:1536], small)] * NT, dst=XL)
            xtok = e
            if l == 0:
                sw = now()
                nxt["w1"], t = wload(WB, 5632, "L3f_w11", 2, 1536, sw)
                nxt["w2"], t2 = wload(WB, 4096, "L3f_w21", 6, 256, sw)
                WL3f = nxt
                tk3 = tkn + [t, t2]
        for t in range(NT):
            e = tt(X[:, t, :], X[:, t, :], XL[:, t, :], ALU.add, xtok)
        dump(X)


def host_arrays(v):
    f = np.float32

    def T(a):
        return np.ascontiguousarray(np.asarray(a).T)

    def C(a):
        return np.ascontiguousarray(np.asarray(a))

    def headpad(a, n=16, hd=16, to=32):
        a = np.asarray(a)
        o = np.zeros(a.shape[:-1] + (n, to), a.dtype)
        o[..., :hd] = a.reshape(a.shape[:-1] + (n, hd))
        return np.ascontiguousarray(o.reshape(a.shape[:-1] + (n * to,)))

    A = {}
    A["x"] = C(v["x"]).reshape(512, 256)
    ctx = C(v["ctx_1024"]).reshape(8192, 256)
    A["ctx"] = ctx
    A["ctxT"] = T(ctx)
    A["mask_BxS2_ik0"] = C(v["mask_BxS2_ik0"])
    for n in "qkv":
        A["L0x_" + n] = T(v[f"L0_xattn_{n}_w"])
    A["L0x_qb"] = C(v["L0_xattn_q_b"])
    A["L0x_kb"] = C(v["L0_xattn_k_b"])
    A["L0x_vb"] = C(v["L0_xattn_v_b"])
    A["L0a_dq"], A["L0a_dkv"] = T(v["L0_attn_w_down_q"]), T(v["L0_attn_w_down_kv"])
    swap = np.arange(1024) ^ 1
    for n, w in (("uq", "q"), ("uk", "k"), ("uv", "v")):
        A["L0a_" + n] = T(v["L0_attn_w_up_" + w])
    A["L0a_uqs"] = C(T(v["L0_attn_w_up_q"])[:, swap])
    A["L0a_uks"] = C(T(v["L0_attn_w_up_k"])[:, swap])
    A["L0a_o"] = T(v["L0_attn_w_out"])
    A["L0a_g"], A["L0a_b"] = C(v["L0_attn_ln_scale"]), C(v["L0_attn_ln_bias"])
    inv = 1.0 / 10000.0 ** (np.arange(0, 64, 2, dtype=f) / 64)
    fr = np.outer(np.arange(256, dtype=f), inv)
    cos = np.concatenate([np.cos(fr), np.cos(fr)], -1)[:, ::2]
    sin = np.concatenate([np.sin(fr), np.sin(fr)], -1)[:, ::2]
    ct = np.repeat(cos.T, 2, axis=0)
    sg = np.where(np.arange(64) % 2 == 0, -1.0, 1.0).astype(f)
    stb = np.repeat(sin.T, 2, axis=0) * sg[:, None]
    A["L0a_C"] = np.tile(ct, (2, 2)).astype(f)
    A["L0a_S"] = np.tile(stb, (2, 2)).astype(f)
    A["L0f_w1"] = T(v["L0_ffn_w1"])
    A["L0f_w2"] = T(v["L0_ffn_w2"])
    A["L0f_cv"] = C(np.concatenate([np.asarray(v["L0_ffn_conv_w"]).reshape(1024, 3), np.asarray(v["L0_ffn_conv_b"])[:, None]], 1))
    for n in "qkvo":
        A["L1x_" + n] = C(v["L1_xattn_W" + n])
    A["L1a_q"], A["L1a_k"] = T(v["L1_attn_Wq"]), T(v["L1_attn_Wk"])
    A["L1a_v"] = headpad(T(v["L1_attn_Wv"]))
    A["L1a_u"] = T(headpad(v["L1_attn_Wu"]))
    A["L1a_bu"] = C(v["L1_attn_bu"])
    A["L1f_gate"], A["L1f_gb"] = C(v["L1_ffn_gate_w"]), C(v["L1_ffn_gate_b"])
    for n, a, b in (("g", "wg", "shared_wg"), ("u", "wu", "shared_wu"), ("d", "wd", "shared_wd")):
        A["L1f_" + n] = np.concatenate([np.asarray(v["L1_ffn_experts_" + a]), np.asarray(v["L1_ffn_" + b])[None]], 0)
    A["L2a_q"], A["L2a_kv"], A["L2a_o"], A["L2a_g"] = (C(v["L2_attn_" + n]) for n in ("Wq", "Wkv", "Wout", "Wg"))
    A["L2a_w"] = C(v["L2_attn_norm_w"])
    for n in "rkv":
        A["L2f_" + n] = T(v["L2_ffn_W_" + n])
    A["L2f_mr"], A["L2f_mk"] = C(v["L2_ffn_mu_r"]), C(v["L2_ffn_mu_k"])
    for n in "qkvp":
        A["L3x_" + n] = T(v["L3_xattn_W" + n])
    A["L3x_ff"] = C(v["L3_xattn_focusing_factor"]).reshape(1)
    w = C(v["L3_attn_Wqkv"])
    bq = C(v["L3_attn_bqkv"])
    A["L3a_q"], A["L3a_k"], A["L3a_v"] = C(w[:, 0:256]), C(w[:, 256:512]), headpad(w[:, 512:768])
    A["L3a_qb"], A["L3a_kb"], A["L3a_vb"] = C(bq[0:256]), C(bq[256:512]), headpad(bq[512:768])
    A["L3a_o"] = T(headpad(T(v["L3_attn_Wout"])))
    A["L3a_ob"] = C(v["L3_attn_bout"])
    for l in range(2):
        A[f"L3f_qkv{l}"] = C(np.asarray(v["L3_ffn_wqkv"])[l])
        A[f"L3f_o{l}"] = C(np.asarray(v["L3_ffn_wo"])[l])
        w1 = np.asarray(v["L3_ffn_w1"])[l]
        p = np.zeros((256, 2, 768), w1.dtype)
        p[:, :, :HID] = w1.reshape(256, 2, HID)
        A[f"L3f_w1{l}"] = p.reshape(256, 1536)
        w2 = np.asarray(v["L3_ffn_w2"])[l]
        p = np.zeros((768, 256), w2.dtype)
        p[:HID] = w2
        A[f"L3f_w2{l}"] = p
    b1 = np.asarray(v["L3_ffn_b1"])
    p = np.zeros((2, 2, 768), b1.dtype)
    p[:, :, :HID] = b1.reshape(2, 2, HID)
    A["L3f_b1"] = p.reshape(2, 1536)
    A["L3f_b2"], A["L3f_lg"], A["L3f_lb"] = C(v["L3_ffn_b2"]), C(v["L3_ffn_ln_g"]), C(v["L3_ffn_ln_b"])
    A["L3f_qs"], A["L3f_ks"] = C(v["L3_ffn_q_scale"]), C(v["L3_ffn_k_scale"])
    half = np.arange(0, 64, 2, dtype=f)
    invf = 1.0 / 10000.0 ** (half / 64)
    t = np.arange(256, dtype=f)
    fr = t[:, None] * invf[None, :]
    fr = np.concatenate([fr, fr], -1)
    base = (half + 0.4 * 64) / (1.4 * 64)
    sc = base[None, :] ** ((t - 128) / 64.0)[:, None]
    sc = np.concatenate([sc, sc], -1)
    cs, sn = np.cos(fr), np.sin(fr)
    sgn = np.where(np.arange(64) < 32, -1.0, 1.0)
    tab = np.concatenate([cs * sc * 8.0, sn * sc * 8.0 * sgn, cs / sc, sn / sc * sgn], 1).astype(f)
    A["L3f_tab"] = np.ascontiguousarray(np.tile(tab, (2, 1)))
    for n in ("L0x_qb", "L0x_kb", "L0a_g", "L0a_b", "L2a_w", "L2f_mr", "L2f_mk", "L3a_qb", "L3a_kb"):
        A[n] = T(A[n].reshape(-1, 128))
    for n in ("L3f_b1", "L3f_lg", "L3f_lb"):
        A[n] = np.ascontiguousarray(A[n].reshape(2, -1, 128).transpose(0, 2, 1))
    A["c_id"] = np.eye(128, dtype=f)
    i, j = np.arange(256)[:, None], np.arange(256)[None, :]
    ms = [j > i, np.abs(i - j) > 128, (i < j) | (i > j + 128)]
    ms = [np.where(m, -BIG, 0.0).astype(f).reshape(2, 128, 256).transpose(1, 0, 2).reshape(128, 512) for m in ms]
    A["c_msk"] = np.ascontiguousarray(np.concatenate(ms, 1))
    s = np.zeros((128, 17), f)
    for q in range(4):
        s[32 * q:32 * q + 17] = np.eye(17, dtype=f)
    A["c_sel"] = s
    A["c_hm8"] = np.repeat(np.eye(8, dtype=f), 16, axis=0)
    hm = np.repeat(np.eye(16, dtype=f), 16, axis=0)
    A["c_hm16"] = hm
    A["c_bmask"] = np.ascontiguousarray(np.repeat(hm, 16, axis=1))
    lo = (np.arange(16)[None, :] < np.arange(16)[:, None]).astype(f)
    A["c_lower"] = np.ascontiguousarray(np.broadcast_to(lo.reshape(1, 256), (128, 256)))
    return A


def program(nc, arrays, stage=12):
    D = {n: nc.dram_tensor("in_" + n, a.shape, mybir.dt.from_np(a.dtype), kind="ExternalInput").ap()
         for n, a in arrays.items()}
    D["scr"] = nc.dram_tensor("scratch_mask", [2, 8192], BF, kind="Internal").ap()
    out = nc.dram_tensor("out_0", [512, 256], F, kind="ExternalOutput").ap()
    build(nc, D, out, stage)


def kernel(**inputs):
    import concourse.bacc as _bacc
    from concourse.bass_utils import run_bass_kernel_spmd as _run

    arrays = host_arrays(inputs)
    nc = _bacc.Bacc("TRN2", target_bir_lowering=False, num_devices=1)
    program(nc, arrays)
    r = _run(nc, [{"in_" + n: a for n, a in arrays.items()}], core_ids=[0])
    return np.asarray(r.results[0]["out_0"]).reshape(2, 256, 256)
```

```python
from contextlib import ExitStack

import numpy as np
import concourse.bass as bass
from concourse import mybir

F = mybir.dt.float32
R32 = mybir.dt.float32r
BF = mybir.dt.bfloat16
I32 = mybir.dt.int32
ALU = mybir.AluOpType
ACT = mybir.ActivationFunctionType
AX = mybir.AxisListType.X
BIG = float(2.0 ** 100)
MAGIC = 12582912.0
NT = 4
HID = 682
WKN = 34432


class Engine:

    def __init__(self, eng, sem):
        self.eng, self.sem, self.n, self.seen = eng, sem, 0, {}
        self.serial = False

    def wait(self, *tokens):
        if self.serial and self.n > self.seen.get(id(self), 0):
            self.eng.wait_ge(self.sem, self.n)
            self.seen[id(self)] = self.n
        for t in tokens:
            if t is None:
                continue
            if isinstance(t, list):
                self.wait(*t)
                continue
            sem, key, value = t
            if self.seen.get(key, 0) < value:
                self.eng.wait_ge(sem, value)
                self.seen[key] = value

    def done(self, ins):
        self.n += 1
        ins.then_inc(self.sem, 1)
        return (self.sem, id(self), self.n)

    def last(self):
        return (self.sem, id(self), self.n) if self.n else None


class Queue:

    def __init__(self, engine, sems):
        self.engine, self.sems, self.count, self.i = engine, sems, [0] * len(sems), 0

    def go(self, out, src, *waits):
        i = self.i
        self.i = (i + 1) % len(self.sems)
        if self.count[i]:
            self.engine.wait((self.sems[i], (id(self), i), self.count[i]))
        self.engine.wait(*waits)
        self.count[i] += 16
        self.engine.eng.dma_start(out, src).then_inc(self.sems[i], 16)
        return (self.sems[i], (id(self), i), self.count[i])


class Slot:

    def __init__(self, ap):
        self.ap, self.free = ap, []


class Ring:
    def __init__(self, aps):
        self.slots, self.i = [Slot(a) for a in aps], 0

    def take(self):
        s = self.slots[self.i]
        self.i = (self.i + 1) % len(self.slots)
        return s


def build(nc, D, out, stage=12):
    ctx = ExitStack()
    with ctx:
        def sb(name, shape, dt=F):
            return ctx.enter_context(nc.sbuf_tensor(name, shape, dt))

        def sem(name):
            return ctx.enter_context(nc.semaphore(name))

        PE = Engine(nc.tensor, sem("s_pe"))
        DV = Engine(nc.vector, sem("s_dve"))
        AC = Engine(nc.scalar, sem("s_act"))
        PO = Engine(nc.gpsimd, sem("s_pool"))
        SP = Engine(nc.sync, sem("s_sp"))
        PO.serial = True
        Q = Queue(SP, [sem(f"s_d{i}") for i in range(100)])

        def now():
            return [PE.last(), DV.last(), AC.last(), PO.last()]

        def mm(o, l, r, *w, start=True, stop=True, inc=None, cols=False):
            PE.wait(*w)
            i = nc.tensor.matmul(o, l, r, start=start, stop=stop, skip_group_check=cols)
            return PE.done(i) if (stop if inc is None else inc) else None

        def tr(o, x, ident, *w):
            PE.wait(*w)
            return PE.done(nc.tensor.transpose(o, x, ident))

        def act(o, x, f, *w, **k):
            AC.wait(*w)
            return AC.done(nc.scalar.activation(o, x, f, **k))

        def ts(o, x, a, b, op0, op1, *w, E=DV, **k):
            E.wait(*w)
            if b is None:
                return E.done(E.eng.tensor_scalar(o, x, a, None, op0, **k))
            return E.done(E.eng.tensor_scalar(o, x, a, b, op0, op1, **k))

        def tt(o, x, y, op, *w, E=DV):
            E.wait(*w)
            return E.done(E.eng.tensor_tensor(o, x, y, op))

        def stt(o, x, s, y, op0, op1, *w, **k):
            DV.wait(*w)
            return DV.done(nc.vector.scalar_tensor_tensor(out=o, in0=x, scalar=s, in1=y, op0=op0, op1=op1, **k))

        def red(o, x, op, *w, **k):
            DV.wait(*w)
            return DV.done(nc.vector.tensor_reduce(o, x, AX, op, **k))

        def cp(o, x, *w, E=DV):
            E.wait(*w)
            if E is AC:
                return E.done(nc.scalar.activation(o, x, ACT.Copy))
            if E is PO:
                return E.done(nc.gpsimd.tensor_scalar(o, x, 1.0, None, ALU.mult))
            return E.done(E.eng.tensor_copy(o, x))

        def rec(o, x, *w):
            DV.wait(*w)
            return DV.done(nc.vector.reciprocal(o, x))

        def fill(o, v, *w, E=PO):
            E.wait(*w)
            return E.done(E.eng.memset(o, v))

        def rsqrt(o, x, c, op, *w):
            a = ts(o, x, c, None, op, None, *w)
            a = act(o, o, ACT.Sqrt, a)
            return rec(o, o, a)

        X = sb("X", [128, NT, 256])
        XN = sb("XN", [128, NT, 256])
        HT = sb("HT", [128, 2, 512])
        WA = sb("WA", [128, 4096])
        WB = sb("WB", [128, 8704])
        WK = sb("WK", [128, WKN])
        idf = sb("idf", [128, 128])
        idb = sb("idb", [128, 128], BF)
        msk = sb("msk", [128, 3, 512], BF)
        sel = sb("sel", [128, 17])
        hm8 = sb("hm8", [128, 8])
        bmask = sb("bmask", [128, 2, 256])
        onesf = sb("onesf", [128, 128])
        XR0 = sb("XR0", [128, 1])
        st = sb("st", [128, NT, 6])
        mv = sb("mv", [128, NT, 2])
        rs = sb("rs", [128, NT])
        sm = sb("sm", [128, 256])
        PS = ctx.enter_context(nc.psum_tensor("PS", [128, 8, 512], F))
        banks = Ring([PS[:, i, :] for i in range(8)])

        def wview(t, a, n, shape=None):
            v = t[:, a:a + n]
            if shape and len(shape) == 2:
                return v.rearrange("p (a b) -> p a b", a=shape[0])
            if shape and len(shape) == 3:
                return v.rearrange("p (a b c) -> p a b c", a=shape[0], b=shape[1])
            return v

        def wload(t, at, name, kt, n, *w, rows=None):
            v = wview(t, at, kt * n, (kt, n))
            src = D[name] if rows is None else rows
            tok = Q.go(v, src.rearrange("(t p) n -> p t n", p=128), *w)
            return v, tok

        def col(name, at, n, *w):
            v = sm[:, at:at + n]
            return v, Q.go(v, D[name], *w)

        cl = [Q.go(idf[:, :], D["c_id"]), Q.go(sel[:, :], D["c_sel"]), Q.go(hm8[:, :], D["c_hm8"]),
              Q.go(bmask[:, :, :], D["c_bmask"].rearrange("(t p) n -> p t n", p=128)),
              Q.go(WK[:, 0:1536], D["c_msk"])]
        xl = Q.go(X[:, :, :], D["x"].rearrange("(t p) n -> p t n", p=128))
        t_ones = fill(onesf[:, :], 1.0)
        cst = [cp(idb[:, :], idf[:, :], cl), cp(msk[:, :, :].rearrange("p a b -> p (a b)"), WK[:, 0:1536], cl), t_ones]
        PE.wait(*cst)

        def layernorm(src, eps, *w, dst=None, E2=PO):
            dst = XN if dst is None else dst
            a = [None] * NT
            for t in range(NT):
                DV.wait(*w)
                a[t] = DV.done(nc.vector.bn_stats(st[:, t, :], src[:, t, :]))
            for t in range(NT):
                DV.wait(a[t])
                a[t] = DV.done(nc.vector.bn_aggr(mv[:, t, :], st[:, t, :]))
            r = rsqrt(rs[:, :], mv[:, :, 1], eps, ALU.add, a[3])
            return [ts(dst[:, t, :], src[:, t, :], mv[:, t, 0:1], rs[:, t:t + 1], ALU.subtract, ALU.mult, r)
                    for t in range(NT)]

        def turn(src, toks, dst, evac=None, n=2, *w):
            o = []
            for f in range(n):
                b = banks.take()
                for t in range(NT):
                    k = tr(b.ap[:, t * 128:(t + 1) * 128], src[:, t, f * 128:(f + 1) * 128], idf[:, :], toks[t], b.free)
                if evac is None:
                    e = cp(dst[:, f, :], b.ap, k, *w, E=(DV, AC)[f % 2])
                else:
                    e = evac(f, b.ap, dst[:, f, :], k)
                b.free = [e]
                o.append(e)
            return o

        def feat(Wt, c0, m, rhs, kt, toks):
            b = banks.take()
            for k in range(kt):
                t = mm(b.ap[0:m, :], Wt[:, k, c0:c0 + m], rhs[:, k, :], toks, b.free, start=k == 0, stop=k == kt - 1)
            return b, t

        def tokp(lhs, kt, t, Wt, c0, n, toks, bank=None, at=0):
            b = bank or banks.take()
            for k in range(kt):
                x = mm(b.ap[:, at:at + n], lhs[:, k, t * 128:(t + 1) * 128], Wt[:, k, c0:c0 + n], toks, b.free,
                       start=k == 0, stop=k == kt - 1)
            return b, x

        def selfattn(units, P, Pn, PT, rsum):
            n = len(units)
            S1, S2 = {}, {}
            ringP, ringN, ringT = Ring(P), Ring(Pn), Ring(PT)
            out = []

            def first(i):
                u = units[i]
                b = banks.take()
                for q in range(2):
                    o = b.ap[:, q * 256:(q + 1) * 256]
                    s = True
                    if u["mask"] is not None:
                        mm(o, idb[:, :], msk[:, u["mask"], q * 256:(q + 1) * 256], b.free, start=True, stop=False)
                        s = False
                    k = mm(o, u["q"][:, q * 128:(q + 1) * 128], u["k"], u["w"], b.free, start=s, stop=True)
                j = i % 4
                nm = rsum[:, j * 8:j * 8 + 2]
                m = red(nm, b.ap.rearrange("p (a b) -> p a b", a=2), ALU.max, k, u_free.get(j), negate=True)
                p = ringP.take()
                ss = rsum[:, j * 8 + 2:j * 8 + 4]
                for q in range(2):
                    e = act(p.ap[:, q * 256:(q + 1) * 256], b.ap[:, q * 256:(q + 1) * 256], ACT.Exp, m, p.free,
                            bias=nm[:, q:q + 1], scale=1.0, accum_out=ss[:, q:q + 1])
                b.free = [e, m]
                r = rec(rsum[:, j * 8 + 4:j * 8 + 6], ss, e)
                rr = rsum[:, j * 8 + 4:j * 8 + 6]
                if u["gate"] is not None:
                    r = tt(rr, rr, u["gate"], ALU.mult, r)
                pn = ringN.take()
                for q in range(2):
                    z = ts(pn.ap[:, q * 256:(q + 1) * 256], p.ap[:, q * 256:(q + 1) * 256], rr[:, q:q + 1], None,
                           ALU.mult, None, r, pn.free)
                p.free = [z]
                u_free[j] = z
                S1[i] = (pn, z)

            def second(i):
                pn, z = S1.pop(i)
                b = banks.take()
                for k in range(2):
                    for q in range(2):
                        t = tr(b.ap[:, k * 256 + q * 128:k * 256 + (q + 1) * 128],
                               pn.ap[:, q * 256 + k * 128:q * 256 + (k + 1) * 128], idf[:, :], z, b.free)
                pn.free = [t]
                pt = ringT.take()
                c = cp(pt.ap, b.ap, t, pt.free, E=(DV, AC)[i % 2])
                b.free = [c]
                S2[i] = (pt, c)

            def third(i):
                pt, c = S2.pop(i)
                pt.free = [units[i]["pv"](pt.ap, c)]

            u_free = {}
            for i in range(n + 3):
                if i < n:
                    first(i)
                if 0 <= i - 2 < n:
                    second(i - 2)
                if 0 <= i - 3 < n:
                    third(i - 3)

        def add_out(src, kt, Wt, toks, extra=None, dst=None):
            dst = X if dst is None else dst
            o = []
            for t in range(NT):
                b, k = tokp(src, kt, t, Wt, 0, 256, toks)
                e = tt(dst[:, t, :], b.ap[:, 0:256], dst[:, t, :], ALU.add, k)
                b.free = [e]
                if extra is not None:
                    e = tt(dst[:, t, :], dst[:, t, :], extra[t][0], ALU.add, e, extra[t][1])
                o.append(e)
            return o

        scr = D["scr"]
        mi = WK[:, 2048:2176].bitcast(I32)
        mf = WK[:, 2176:2304]
        ml = Q.go(mi[0:64, :], D["mask_BxS2_ik0"].rearrange("b (t p) -> (b t) p", p=128))
        a = cp(mf[0:64, :], mi[0:64, :], ml)
        mrow = WK[:, 2304:2432].bitcast(BF)
        m0 = ts(mrow[0:64, 0:128], mf[0:64, :], 0.0, -BIG, ALU.is_gt, ALU.mult, a)
        m1a = ts(mf[0:64, :], mf[0:64, :], -1.0, 1.0, ALU.mult, ALU.add, a, m0)
        m1 = ts(mrow[0:64, 128:256], mf[0:64, :], -BIG, None, ALU.mult, None, m1a)
        md = [Q.go(scr[l:l + 1, :].rearrange("a (t p) -> (a t) p", p=128), mrow[0:64, l * 128:(l + 1) * 128], [m0, m1][l])
              for l in range(2)]
        mn = WK[:, 2440:2456]
        a = red(mn[0:64, 0:1], mf[0:64, :], ALU.min, m1)
        b = banks.take()
        a = tr(b.ap[0:1, 0:64], mn[0:64, 0:1], idf[0:64, 0:64], a)
        e = red(mn[0:1, 4:6], b.ap[0:1, 0:64].rearrange("p (a b) -> p a b", a=2), ALU.min, a)
        b.free = [e]
        e = ts(mn[0:1, 6:8], mn[0:1, 4:6], 1.0, None, ALU.is_lt, None, e)
        b = banks.take()
        a = mm(b.ap[:, 0:2], onesf[0:1, :], mn[0:1, 6:8], e)
        anyk = sb("anyk", [128, 2])
        t_any = cp(anyk[:, :], b.ap[:, 0:2], a)
        b.free = [t_any]

        def load_l0x(*w):
            q = wload(WA, 0, "L0x_q", 2, 256, *w)
            k = wload(WA, 512, "L0x_k", 2, 256, *w)
            v = wload(WA, 1024, "L0x_v", 2, 256, *w)
            c = [col("L0x_qb", 0, 2, *w)[1], col("L0x_kb", 2, 2, *w)[1]]
            return dict(q=q[0], k=k[0], v=v[0], tok=[q[1], k[1], v[1]] + c, qb=sm[:, 0:2], kb=sm[:, 2:4])

        def load_l1x(*w):
            r = {}
            tok = []
            for i, n in enumerate("qkvo"):
                r[n], t = wload(WB, 512 * i, "L1x_" + n, 2, 256, *w)
                tok.append(t)
            r["tok"] = tok
            return r

        def crossattn(W, lay, xn_tok):
            start = now() + [xn_tok]
            o = 0

            def part(n, dt=F):
                nonlocal o
                v = WK[:, o:o + n]
                o += n
                return v if dt is F else v.bitcast(dt)

            KS = [part(2048, BF) for _ in range(4)]
            KH, KM, KL = part(2048, BF), part(2048, BF), part(2048, BF)
            CT = Ring([part(1024).rearrange("p (a b) -> p a b", a=2) for _ in range(2)])
            K32 = Ring([part(512) for _ in range(2)])
            V = [part(4832).rearrange("p (a b) -> p a b", a=32) for _ in range(2)]
            PR = Ring([part(512) for _ in range(5)])
            QS = part(4096, BF).rearrange("p (h t) -> p h t", h=16)
            PV = Ring([part(256) for _ in range(1)])
            mx = part(64)
            mxb = part(16, BF)
            mxr = part(16)
            rd = Ring([part(36) for _ in range(2)])
            assert o <= WKN, o
            qx = V[1][:, :, :].rearrange("p a b -> p (a b)")
            q32 = qx[:, 0:1024].rearrange("p (a b) -> p a b", a=2)
            qp = [qx[:, 1024 + 512 * i:1536 + 512 * i].bitcast(BF).rearrange("p (a b) -> p a b", a=2) for i in range(3)]
            qr = qx[:, 2560:3584].rearrange("p (a b) -> p a b", a=2)
            qt = []
            DV.wait(*start)
            PO.wait(*start)
            AC.wait(*start)
            PE.wait(*start)
            for m in range(2):
                b, k = feat(W["q"], m * 128, 128, HT, 2, [xn_tok, W["tok"]])
                if lay == 0:
                    e = ts(q32[:, m, :], b.ap, W["qb"][:, m:m + 1], 0.25, ALU.add, ALU.mult, k, W["tok"])
                else:
                    for bb in range(2):
                        e = ts(q32[:, m, bb * 256:(bb + 1) * 256], b.ap[:, bb * 256:(bb + 1) * 256],
                               anyk[:, bb:bb + 1], 0.25, ALU.mult, ALU.mult, k, t_any)
                b.free = [e]
                h = cp(qp[0][:, m, :], q32[:, m, :], e)
                r = tt(qr[:, m, :], q32[:, m, :], qp[0][:, m, :], ALU.subtract, h)
                l = cp(qp[1][:, m, :], qr[:, m, :], r)
                l2 = tt(qp[2][:, m, :], qr[:, m, :], qp[1][:, m, :], ALU.subtract, l)
                qt += [h, l, l2]
            z1 = fill(QS[96:100, :, :], 1.0, start, E=DV)
            z2 = fill(QS[96:99, :, :], 0.0, z1, E=DV)
            free0 = now()
            kst = [fill(KS[s][96:99, :], 1.0, E=PO) for s in range(4)]
            sq_ = D["scrq"]
            qw = [Q.go(sq_[s].rearrange("(m p) t -> p m t", p=128), qp[s], qt, start) for s in range(3)]
            qd = [Q.go(QS[16 * j:16 * j + 16, :, :], sq_[s].rearrange("(h p) t -> p h t", p=16), qw[s], start)
                  for j, s in enumerate((0, 1, 2, 0, 1, 0))]

            vc = []
            for s in range(2):
                vv = V[s]
                vc.append(None)

            def vconst(s, *w):
                vv = V[s]
                vc[s] = [fill(vv[:, :, 136:151], 0.0, *w, E=PO),
                         fill(vv[:, :, 0:136].rearrange("p a (h c) -> p a h c", c=17)[:, :, :, 16], 1.0, *w, E=PO)]

            vconst(0)
            ko = (0, 0, 0, 1, 1, 2)
            kparts = (KH, KM, KL)
            kfree, vfree = [], [[], []]
            ktok, vtok, stk, mtok = {}, {}, {}, {}
            kstfree, mxfree = [[] for _ in range(4)], [[], []]
            PJ = Ring([PS[:, 6, :], PS[:, 7, :]])
            P1 = Ring([PS[:, 3, :], PS[:, 4, :]])
            ST = Ring([PS[:, 0, :], PS[:, 1, :], PS[:, 2, :]])
            PVB = Slot(PS[:, 5, :])
            for s in PJ.slots + P1.slots + ST.slots + [PVB]:
                s.free = free0
            cT = D["ctxT"]

            def chunk(g, c):
                ct = CT.take()
                bb = g // 2
                src = cT[:, bb * 4096 + c * 512:bb * 4096 + (c + 1) * 512].rearrange("(t p) n -> p t n", p=128)
                return ct, Q.go(ct.ap, src, start, ct.free)

            def keys(g, c, ct, ld):
                m = g % 2
                b = PJ.take()
                for k in range(2):
                    x = mm(b.ap, W["k"][:, k, m * 128:(m + 1) * 128], ct.ap[:, k, :], ld, b.free, W["tok"],
                           start=k == 0, stop=k == 1)
                    if k == 0:
                        yield
                k32 = K32.take()
                sl = slice(c * 512, (c + 1) * 512)
                if lay == 0:
                    e = act(k32.ap, b.ap, ACT.Identity, x, k32.free, bias=W["kb"][:, m:m + 1], scale=1.0)
                    h = act(KH[:, sl], b.ap, ACT.Identity, kfree, bias=W["kb"][:, m:m + 1], scale=1.0)
                else:
                    e = act(k32.ap, b.ap, ACT.Copy, x, k32.free)
                    h = act(KH[:, sl], b.ap, ACT.Copy, kfree)
                b.free = [h]
                ct.free = ct.free + [x]
                r = tt(k32.ap, k32.ap, KH[:, sl], ALU.subtract, e, h, E=PO)
                m1 = cp(KM[:, sl], k32.ap, r, kfree, E=DV)
                l = tt(KL[:, sl], k32.ap, KM[:, sl], ALU.subtract, m1, kfree, E=PO)
                k32.free = [l]
                ktok.setdefault(g, []).append(l)
                yield

            def values(g, c, ct, ld):
                m = g % 2
                b = PJ.take()
                for t in range(4):
                    for k in range(2):
                        x = mm(b.ap[:, t * 128:(t + 1) * 128], ct.ap[:, k, t * 128:(t + 1) * 128],
                               W["v"][:, k, m * 128:(m + 1) * 128], ld, b.free, W["tok"], start=k == 0, stop=k == 1)
                    if t < 3:
                        yield
                dst = V[g % 2][:, c * 4:c * 4 + 4, 0:136].rearrange("p a (h c) -> p a h c", c=17)[:, :, :, 0:16]
                e = cp(dst, b.ap.rearrange("p (a h c) -> p a h c", a=4, h=8), x, vfree[g % 2], vc[g % 2], E=AC)
                b.free = [e]
                ct.free = ct.free + [x]
                vtok.setdefault(g, []).append(e)
                yield

            def allof(g, what):
                for c in range(8):
                    ct, ld = chunk(g, c)
                    ct.free = []
                    yield from what(g, c, ct, ld)

            def stack(s):
                g, hh = s // 8, s % 8
                ks = KS[s % 4]
                d = []
                for j, pn in enumerate(ko):
                    d.append(Q.go(ks[16 * j:16 * j + 16, :], kparts[pn][16 * hh:16 * hh + 16, :], ktok[g],
                                  kstfree[s % 4], kst[s % 4]))
                d.append(Q.go(ks[99:100, :], scr[lay:lay + 1, (g // 2) * 4096:(g // 2) * 4096 + 4096], md[lay],
                              kstfree[s % 4]))
                stk[s] = d
                if hh == 7:
                    kfree[:] = d

            def where(s):
                g, hh = s // 8, s % 8
                return g, hh, g // 2, (g % 2) * 8 + hh

            state = {}

            def rowmax(s):
                g, hh, bb, h = where(s)
                ks = KS[s % 4]
                mt = mx[:, (s % 2) * 32:(s % 2) * 32 + 32]
                for q in range(2):
                    for c in range(8):
                        b = P1.take()
                        x = mm(b.ap, QS[0:100, h, bb * 256 + q * 128:bb * 256 + (q + 1) * 128],
                               ks[0:100, c * 512:(c + 1) * 512], stk[s], qd, z2, b.free)
                        e = red(mt[:, q * 8 + c:q * 8 + c + 1], b.ap, ALU.max, x, mxfree[s % 2])
                        b.free = [e]
                        if q * 8 + c < 15:
                            yield
                state["p1"] = x
                nm = mxr[:, (s % 2) * 8:(s % 2) * 8 + 2]
                r1 = mxr[:, (s % 2) * 8 + 2:(s % 2) * 8 + 4]
                nb = mxb[:, (s % 2) * 8:(s % 2) * 8 + 8].rearrange("p (q c) -> p q c", c=4)
                a = red(nm, mt[:, 0:16].rearrange("p (a b) -> p a b", a=2), ALU.max, e, mxfree[s % 2], negate=True)
                h1 = cp(nb[:, :, 0], nm, a)
                r = tt(r1, nm, nb[:, :, 0], ALU.subtract, h1)
                h2 = cp(nb[:, :, 1], r1, r)
                h3 = tt(nb[:, :, 2], r1, nb[:, :, 1], ALU.subtract, h2)
                mtok[s] = (nb, [h1, h2, h3])
                yield

            def maxrow(s):
                g, hh, bb, h = where(s)
                nb, w = mtok[s]
                b = PJ.take()
                bv = b.ap.bitcast(BF)
                for q in range(2):
                    PE.wait(w, b.free)
                    x = PE.done(nc.tensor.transpose(bv[96:99, q * 128:(q + 1) * 128], nb[:, q, 0:3], idb[:, :]))
                e = cp(QS[96:99, h, bb * 256:bb * 256 + 256], bv[96:99, 0:256], x, state["p1"])
                b.free = [e]
                mxfree[s % 2] = [x]
                state["mrow"] = e

            def finish(s, part):
                g, hh, bb, h = where(s)
                if part == 0:
                    pv = PV.take()
                    e = cp(pv.ap, PVB.ap[:, 0:256], state["pvt"], pv.free)
                    PVB.free = [e]
                    state["pvs"] = (pv, e)
                    return
                pv, e = state["pvs"]
                b = PJ.take()
                for q in range(2):
                    x = tr(b.ap[:, q * 128:(q + 1) * 128], pv.ap[:, q * 128:(q + 1) * 128], idf[:, :], e, b.free)
                pv.free = [x]
                r_ = rd.take()
                sm_ = r_.ap[:, 0:34].rearrange("p (a b) -> p a b", a=2)
                e = red(sm_, b.ap[:, 0:256].rearrange("p (a j c) -> p a c j", a=2, j=4)[:, :, 0:17, :], ALU.add, x, r_.free)
                b.free = [e]
                r = rec(r_.ap[:, 34:36], sm_[:, :, 16], e)
                for q in range(2):
                    t = 2 * bb + q
                    if lay == 0:
                        e = stt(X[:, t, 16 * h:16 * h + 16], sm_[:, q, 0:16], r_.ap[:, 34 + q:35 + q],
                                X[:, t, 16 * h:16 * h + 16], ALU.mult, ALU.add, r)
                    else:
                        e = ts(XN[:, t, 16 * h:16 * h + 16], sm_[:, q, 0:16], r_.ap[:, 34 + q:35 + q], None,
                               ALU.mult, None, r)
                r_.free = [e]
                return e

            def drain(it):
                for _ in it:
                    pass

            NS = 32
            for c in range(8):
                ct, ld = chunk(0, c)
                ct.free = []
                drain(keys(0, c, ct, ld))
            vconst(1, qw)
            for hh in range(3):
                stack(hh)
            drain(allof(0, values))
            drain(rowmax(0))
            maxrow(0)
            prev = None
            kwork = vwork = iter(())
            for s in range(NS):
                g, hh, bb, h = where(s)
                if hh == 0:
                    vwork = allof(g + 1, values) if g < 3 else iter(())
                if hh == 5:
                    drain(vwork)
                    kwork = allof(g + 1, keys) if g < 3 else iter(())
                ks = KS[s % 4]
                V_ = V[g % 2]
                p1 = rowmax(s + 1) if s + 1 < NS else iter(())
                mrow = state["mrow"]
                pend = []

                def flush(c, items):
                    for j in range(4):
                        pr, e = items[j // 2]
                        x = mm(PVB.ap[32 * j:32 * j + 32, 0:256], V_[:, c * 4 + j, 17 * hh:17 * hh + 32],
                               pr.ap[:, (j % 2) * 256:(j % 2) * 256 + 256], e, PVB.free, vtok[g], start=c == 0,
                               stop=c == 7, inc=(j == 3), cols=True)
                    for pr, e in items:
                        pr.free = [x]
                    state["pvt"] = x

                for i in range(16):
                    sT = ST.take()
                    for j in range(2):
                        kt = i * 2 + j
                        x = mm(sT.ap[:, j * 256:j * 256 + 256], ks[0:100, kt * 128:(kt + 1) * 128],
                               QS[0:100, h, bb * 256:bb * 256 + 256], mrow, sT.free)
                    pr = PR.take()
                    e = act(pr.ap, sT.ap, ACT.Exp, x, pr.free)
                    sT.free = [e]
                    lastS = x
                    pend.append((pr, e))
                    if i < 12:
                        next(p1, None)
                        if i % 3 == 2:
                            next(p1, None)
                    if i == 0 and prev is not None:
                        finish(prev, 0)
                    if i == 2 and prev is not None:
                        finish(prev, 1)
                    if i % 2 == 1 and i >= 3:
                        flush((i - 3) // 2, [pend.pop(0), pend.pop(0)])
                    if i % 2 == 0:
                        next(vwork, None)
                    next(kwork, None)
                drain(p1)
                if s + 1 < NS:
                    maxrow(s + 1)
                flush(7, [pend.pop(0), pend.pop(0)])
                kstfree[s % 4] = [lastS]
                if hh == 7:
                    vfree[g % 2] = [state["pvt"]]
                if hh < 5:
                    stack(s + 3)
                elif g < 3 and hh == 6:
                    drain(kwork)
                    stack(s + 2)
                    stack(s + 3)
                elif g < 3 and hh == 7:
                    stack(s + 3)
                prev = s
            finish(prev, 0)
            return finish(prev, 1)

        W = load_l0x()
        ln = layernorm(X, 1e-5, xl)
        ht = turn(XN, ln, HT)
        def load_l0a(*w):
            r, tok = {}, []
            at = 0
            for n, kt, m in (("dq", 2, 128), ("dkv", 2, 128), ("uq", 1, 1024), ("uqs", 1, 1024), ("uk", 1, 1024),
                             ("uks", 1, 1024), ("uv", 1, 1024), ("o", 8, 256), ("C", 1, 512), ("S", 1, 512)):
                r[n], t = wload(WB, at, "L0a_" + n, kt, m, *w)
                at += kt * m
                tok.append(t)
            tok.append(col("L0a_g", 4, 2, *w)[1])
            tok.append(col("L0a_b", 6, 2, *w)[1])
            r["tok"] = tok
            return r

        WL0a = load_l0a()
        vbt = WA[:, 1536:1792]
        tvb = Q.go(vbt, D["L0x_vb"].rearrange("(a n) -> a n", a=1).to_broadcast([128, 256]))
        if "fake0" in D:
            e = Q.go(X[:, :, :], D["fake0"].rearrange("(t p) n -> p t n", p=128), now(), ht)
            cp(XR0[:, :], X[:, 0, 0:1], e)
        else:
            e = crossattn(W, 0, ht)
            for t in range(NT):
                tt(X[:, t, :], X[:, t, :], vbt, ALU.add, e, tvb)
        s0 = now()

        def dump(src):
            o = []
            for t in range(NT):
                o.append(Q.go(out.rearrange("(t p) n -> p t n", p=128)[:, t, :], src[:, t, :], *now()))
            SP.wait(*o)

        if stage == 1:
            dump(X)
            return

        for bk in banks.slots:
            bk.free = list(s0)

        WL0f = [wload(WA, 0, "L0f_w1", 2, 1024, s0), wload(WA, 2048, "L0f_w2", 8, 256, s0)]
        cv = sm[:, 16:48].rearrange("p (a b) -> p a b", a=8)
        WL0f.append((None, Q.go(cv, D["L0f_cv"].rearrange("(t p) n -> p t n", p=128), s0)))

        def heads64(k2, base):
            QZ = wview(WK, 0, 8192, (16, 512))
            return QZ

        QZ = wview(WK, 0, 8192, (16, 512))
        KT = wview(WK, 8192, 4096, (8, 512))
        VT = wview(WK, 12288, 4096, (4, 1024))
        OT = wview(WK, 16384, 4096, (8, 512))
        PP = [wview(WK, 20480 + 512 * i, 512) for i in range(4)]
        PN = [wview(WK, 22528 + 512 * i, 512) for i in range(4)]
        PTT = [wview(WK, 24576 + 512 * i, 512) for i in range(3)]
        TMP = Ring([wview(WK, 26112 + 512 * i, 512) for i in range(6)])
        CQ = wview(WK, 29184, 1024, (2, 512))
        XR = wview(WK, 30208, 1024, (4, 256))
        RS = wview(WK, 31232, 32)

        def zero_halves(w):
            a = fill(QZ[64:128, 0:16:2, :], 0.0, w, E=PO)
            b = fill(QZ[0:64, 1:16:2, :], 0.0, w, E=PO)
            return [a, b]

        zh = zero_halves(s0)
        ln = layernorm(X, 1e-5, s0)
        ln2 = layernorm(XN, 1e-5, ln, dst=XR)
        g_, b_ = sm[:, 4:6], sm[:, 6:8]
        W = WL0a

        def affine(g, bb, tok):
            def ev(f, src, dst, k):
                return ts(dst, src, g[:, f:f + 1], bb[:, f:f + 1], ALU.mult, ALU.add, k, tok)
            return ev

        ht = turn(XR, ln2, HT, affine(g_, b_, W["tok"]))
        cc = []
        for i, n in enumerate(("dq", "dkv")):
            b, k = feat(W[n], 0, 128, HT, 2, [ht, W["tok"]])
            e = cp(CQ[:, i, :], b.ap, k, E=(DV, AC)[i])
            b.free = [e]
            cc.append(e)

        def rope(n, ns, src, m, dsts, sc):
            b, k = feat(W[n], m * 128, 128, src, 1, cc)
            b2, k2 = feat(W[ns], m * 128, 128, src, 1, cc)
            u, v = TMP.take(), TMP.take()
            e1 = stt(u.ap, b.ap, sc, W["C"][:, 0, :], ALU.mult, ALU.mult, k, u.free, W["tok"])
            e2 = stt(v.ap, b2.ap, sc, W["S"][:, 0, :], ALU.mult, ALU.mult, k2, v.free)
            b.free, b2.free = [e1], [e2]
            o = [tt(d, u.ap[p0:p1, :], v.ap[p0:p1, :], ALU.add, e1, e2, E=PO) for d, p0, p1 in dsts]
            u.free = v.free = o
            return o

        qk = []
        for m in range(8):
            qk += rope("uq", "uqs", CQ[:, 0:1, :], m, [(QZ[0:64, 2 * m, :], 0, 64), (QZ[64:128, 2 * m + 1, :], 64, 128)], 0.125)
            qk += rope("uk", "uks", CQ[:, 1:2, :], m, [(KT[:, m, :], 0, 128)], 1.0)
        vt = []

        def vproj(lhs, kt, Wv, c0, toks, dst=None, n=1024):
            o = []
            for t in range(NT):
                for c in range(0, n, 512):
                    b, k = tokp(lhs, kt, t, Wv, c0 + c, 512, toks)
                    e = cp((VT if dst is None else dst)[:, t, c:c + 512], b.ap, k, E=AC)
                    b.free = [e]
                    o.append(e)
            return o

        vt = vproj(CQ[:, 1:2, :], 1, W["uv"], 0, cc)

        def attn64(nh, wts, mask, gate=None, gtok=None, OTv=None):
            OTv = OT if OTv is None else OTv
            units, held = [], {}
            for bb in range(2):
                for h in range(nh):
                    def pv(PTap, c, bb=bb, h=h):
                        j = h % 2
                        if j == 0:
                            held["b"] = banks.take()
                        b = held["b"]
                        for k in range(2):
                            x = mm(b.ap[64 * j:64 * j + 64, 0:256], VT[:, bb * 2 + k, h * 64:(h + 1) * 64],
                                   PTap[:, k * 256:(k + 1) * 256], c, wts, b.free, start=k == 0, stop=k == 1, cols=True)
                        if j == 1:
                            e = cp(OTv[:, h // 2, bb * 256:(bb + 1) * 256], b.ap[:, 0:256], x, E=AC)
                            b.free = [e]
                            held["o"] = e
                        return x
                    units.append(dict(q=QZ[:, h, bb * 256:(bb + 1) * 256], k=KT[:, h // 2, bb * 256:(bb + 1) * 256],
                                      w=wts, mask=mask, pv=pv,
                                      gate=None if gate is None else gate[:, 2 * bb:2 * bb + 2, h]))
            selfattn(units, PP, PN, PTT, RS)
            return held["o"]

        o = attn64(16, [qk[-1], vt[-1], now()], None)
        e = add_out(OT, 8, W["o"], [o], extra=[(XN[:, t, :], None) for t in range(NT)])
        s1 = now()
        if stage == 2:
            dump(X)
            return

        WL1x = load_l1x(s1)
        ln = layernorm(X, 1e-5, s1)
        w1, w2 = WL0f[0][0], WL0f[1][0]
        wt = [x[1] for x in WL0f]
        WQ1 = wview(WK, 0, 2048, (2, 1024))
        WQ2 = wview(WK, 2048, 1024).bitcast(BF).rearrange("p (a b) -> p a b", a=8)
        wtmp = wview(WK, 3072, 2048)
        XQ = wview(WK, 5120, 1024, (4, 256))
        HB = wview(WK, 6144, 4128).rearrange("p (m b t) -> p m b t", m=8, b=2)
        Y = Ring([wview(WK, 10272 + 512 * i, 512) for i in range(3)])
        YT = wview(WK, 11808, 4096, (8, 512))
        HK = wview(WK, 15904, 4096, (4, 1024))
        HQ = wview(WK, 20000, 2048).bitcast(BF).rearrange("p (t n) -> p t n", t=4)
        HQT = wview(WK, 22048, 2048).bitcast(BF).rearrange("p (m t) -> p m t", m=8)
        hq1 = wview(WK, 24096, 2048, (2, 1024))
        wst = wview(WK, 26144, 64)

        def wquant(wap, n, at, dst):
            flat = wap.rearrange("p a b -> p (a b)")
            DV.wait(*wt, *s1)
            a = DV.done(nc.vector.tensor_reduce(wst[:, at:at + 1], flat, AX, ALU.add, apply_absolute_value=True))
            b = banks.take()
            x = mm(b.ap[:, 0:1], onesf[:, :], wst[:, at:at + 1], a, b.free)
            e = ts(wst[:, at + 1:at + 2], b.ap[:, 0:1], 1.0 / n, 1e-5, ALU.mult, ALU.max, x)
            b.free = [e]
            r = rec(wst[:, at + 2:at + 3], wst[:, at + 1:at + 2], e)
            q = ts(wtmp[:, :], flat, wst[:, at + 2:at + 3], MAGIC, ALU.mult, ALU.add, r)
            q = ts(wtmp[:, :], wtmp[:, :], MAGIC, -1.0, ALU.subtract, ALU.max, q)
            q = ts(dst.rearrange("p a b -> p (a b)"), wtmp[:, :], 1.0, None, ALU.min, None, q)
            return q, wst[:, at + 1:at + 2]

        q1, sw1 = wquant(w1, 262144, 0, WQ1)
        q2, sw2 = wquant(w2, 262144, 4, WQ2)

        def aquant(src, t, n, dst, tmp, at, w, back):
            DV.wait(w)
            c = wst[:, at + 3 * t:at + 3 * t + 1]
            c1 = wst[:, at + 3 * t + 1:at + 3 * t + 2]
            c2 = wst[:, at + 3 * t + 2:at + 3 * t + 3]
            a = DV.done(nc.vector.tensor_reduce(c, src, AX, ALU.max, apply_absolute_value=True))
            a = ts(c, c, 1e-5, None, ALU.max, None, a)
            r = rec(c1, c, a)
            i1 = ts(c1, c1, 127.0, None, ALU.mult, None, r)
            i2 = ts(c2, c, 1.0 / 127.0, None, ALU.mult, None, a)
            q = ts(tmp, src, c1, MAGIC, ALU.mult, ALU.add, i1)
            q = ts(tmp, tmp, MAGIC, 127.0, ALU.subtract, ALU.min, q)
            if back:
                return ts(dst, tmp, -128.0, c2, ALU.max, ALU.mult, q, i2), c2
            return ts(dst, tmp, -128.0, None, ALU.max, None, q), c2

        xq = [aquant(XN[:, t, :], t, 256, XQ[:, t, :], hq1[:, 0, t * 256:(t + 1) * 256], 16, ln[t], True)[0] for t in range(NT)]
        ht = turn(XQ, xq, HT)
        z = [fill(HB[:, :, :, 0:1], 0.0, s1), fill(HB[:, :, :, 257:258], 0.0, s1)]
        yt = []
        for m in range(8):
            b, k = feat(WQ1, m * 128, 128, HT, 2, [ht, q1])
            e = act(HB[:, m, :, 1:257], b.ap.rearrange("p (b t) -> p b t", b=2), ACT.Copy, k, z, s1, scale=sw1)
            b.free = [e]
            y = Y.take()
            yv = y.ap.rearrange("p (b t) -> p b t", b=2)
            a = ts(yv, HB[:, m, :, 1:257], cv[:, m, 1:2], cv[:, m, 3:4], ALU.mult, ALU.add, e, y.free)
            a = stt(yv, HB[:, m, :, 0:256], cv[:, m, 0:1], yv, ALU.mult, ALU.add, a)
            a = stt(yv, HB[:, m, :, 2:258], cv[:, m, 2:3], yv, ALU.mult, ALU.add, a)
            e = act(YT[:, m, :], y.ap, ACT.Silu, a)
            y.free = [e]
            yt.append(e)
        hk = []
        for t in range(NT):
            hs = []
            for g in range(2):
                b = banks.take()
                for j in range(4):
                    m = g * 4 + j
                    k = tr(b.ap[:, j * 128:(j + 1) * 128], YT[:, m, t * 128:(t + 1) * 128], idf[:, :], yt[m], b.free)
                e = cp(HK[:, t, g * 512:(g + 1) * 512], b.ap, k, E=AC)
                b.free = [e]
                hs.append(e)
            hk.append(aquant(HK[:, t, :], t, 1024, HQ[:, t, :], hq1[:, t % 2, :], 32, hs, False))
        tq = []
        for m in range(8):
            b = banks.take()
            bv = b.ap.bitcast(BF)
            for t in range(NT):
                k = tr(bv[:, t * 128:(t + 1) * 128], HQ[:, t, m * 128:(m + 1) * 128], idb[:, :], hk[t][0], b.free)
            e = cp(HQT[:, m, :], bv[:, 0:512], k, E=AC)
            b.free = [e]
            tq.append(e)
        for t in range(NT):
            b, k = tokp(HQT, 8, t, WQ2, 0, 256, [tq, q2])
            a = ts(wst[:, 48 + t:49 + t], hk[t][1], sw2, None, ALU.mult, None, hk[t][0], q2)
            e = stt(X[:, t, :], b.ap[:, 0:256], wst[:, 48 + t:49 + t], X[:, t, :], ALU.mult, ALU.add, k, a)
            b.free = [e]
        s2 = now()
        if stage == 3:
            dump(X)
            return

        def load_l1a(*w):
            r, tok, at = {}, [], 0
            for n, kt, m in (("q", 2, 256), ("k", 2, 256), ("v", 2, 512), ("u", 4, 256)):
                r[n], t = wload(WA, at, "L1a_" + n, kt, m, *w)
                at += kt * m
                tok.append(t)
            r["bu"] = WA[:, at:at + 256]
            tok.append(Q.go(WA[:, at:at + 256], D["L1a_bu"].rearrange("(a n) -> a n", a=1).to_broadcast([128, 256]), *w))
            r["tok"] = tok
            return r

        WL1a = load_l1a(s2)
        ln = layernorm(X, 1e-5, s2)
        ht = turn(XN, ln, HT)
        W = WL1x
        if "fake1" in D:
            e = Q.go(X[:, :, :], D["fake1"].rearrange("(t p) n -> p t n", p=128), now(), ht)
            cp(XR0[:, :], X[:, 0, 0:1], e)
        else:
            e = crossattn(W, 1, ht + [PE.last()])
            s3 = now()
            for bk in banks.slots:
                bk.free = list(s3)
            ht = turn(XN, [e] * NT, HT)
            add_out(HT, 2, W["o"], [ht])
        s3 = now()
        if stage == 4:
            dump(X)
            return

        NE = 11
        exp_slots = Ring([WB[:, 768 * i:768 * (i + 1)] for i in range(NE)])
        exq = {}

        def load_expert(i, *w):
            s = exp_slots.take()
            g = s.ap[:, 0:256].rearrange("p (a b) -> p a b", a=2)
            u = s.ap[:, 256:512].rearrange("p (a b) -> p a b", a=2)
            d = s.ap[:, 512:768]
            tk = [Q.go(g, D["L1f_g"][i].rearrange("(t p) n -> p t n", p=128), s.free, *w),
                  Q.go(u, D["L1f_u"][i].rearrange("(t p) n -> p t n", p=128), s.free, *w),
                  Q.go(d, D["L1f_d"][i], s.free, *w)]
            exq[i] = (s, g, u, d, tk)

        for i in range(NE):
            load_expert(i, s3)
        ln = layernorm(X, 1e-5, s3)
        ht = turn(XN, ln, HT)
        KT2 = wview(WK, 8192, 1024, (2, 512))
        VT2 = wview(WK, 12288, 2048, (4, 512))
        OT2 = wview(WK, 16384, 2048, (4, 512))
        hmask = hm8

        def attn16(Wq, Wk, Wv, toks, sc, mask, qb=None, kb=None, vb=None):
            qk, vt = [], []
            for m in range(2):
                b, k = feat(Wq, m * 128, 128, HT, 2, toks)
                u = TMP.take()
                if qb is None:
                    e0 = ts(u.ap, b.ap, sc, None, ALU.mult, None, k, u.free)
                else:
                    e0 = ts(u.ap, b.ap, qb[:, m:m + 1], sc, ALU.add, ALU.mult, k, u.free)
                b.free = [e0]
                for j in range(8):
                    if j % 2:
                        e = ts(QZ[:, m * 8 + j, :], u.ap, hm8[:, j:j + 1], None, ALU.mult, None, e0, E=PO)
                    else:
                        e = act(QZ[:, m * 8 + j, :], u.ap, ACT.Copy, e0, scale=hm8[:, j:j + 1])
                    qk.append(e)
                u.free = qk[-2:]
                b, k = feat(Wk, m * 128, 128, HT, 2, toks)
                if kb is None:
                    e = cp(KT2[:, m, :], b.ap, k, E=DV)
                else:
                    e = ts(KT2[:, m, :], b.ap, kb[:, m:m + 1], None, ALU.add, None, k)
                b.free = [e]
                qk.append(e)
            for t in range(NT):
                b, k = tokp(HT, 2, t, Wv, 0, 512, toks)
                if vb is None:
                    e = cp(VT2[:, t, :], b.ap, k, E=AC)
                else:
                    e = tt(VT2[:, t, :], b.ap, vb, ALU.add, k)
                b.free = [e]
                vt.append(e)
            units, held = [], {}
            wts = qk + vt
            for bb in range(2):
                for h in range(16):
                    def pv(PTap, c, bb=bb, h=h):
                        j = h % 4
                        if j == 0:
                            held["b"] = banks.take()
                        b = held["b"]
                        for k in range(2):
                            x = mm(b.ap[32 * j:32 * j + 32, 0:256], VT2[:, bb * 2 + k, h * 32:(h + 1) * 32],
                                   PTap[:, k * 256:(k + 1) * 256], c, wts, b.free, start=k == 0, stop=k == 1, cols=True)
                        if j == 3:
                            e = cp(OT2[:, h // 4, bb * 256:(bb + 1) * 256], b.ap[:, 0:256], x, E=AC)
                            b.free = [e]
                            held["o"] = e
                        return x
                    units.append(dict(q=QZ[:, h, bb * 256:(bb + 1) * 256], k=KT2[:, h // 8, bb * 256:(bb + 1) * 256],
                                      w=wts, mask=mask, pv=pv, gate=None))
            selfattn(units, PP, PN, PTT, RS)
            return held["o"]

        W = WL1a
        PO.wait(*s3)
        AC.wait(*s3)
        DV.wait(*s3)
        o = attn16(W["q"], W["k"], W["v"], [ht, W["tok"]], 1.0 / 16, None)
        add_out(OT2, 4, W["u"], [o], extra=[(W["bu"], W["tok"])] * NT)
        s4 = now()
        if stage == 5:
            dump(X)
            return

        gw, gt = wload(WA, 0, "L1f_gate", 2, 16, s4)
        gb = WA[:, 32:48]
        gt2 = Q.go(gb, D["L1f_gb"].rearrange("(a n) -> a n", a=1).to_broadcast([128, 16]), s4)
        ll = WA[:, 64:320].rearrange("p (a b) -> p a b", a=16)
        gt3 = Q.go(WA[:, 64:320], D["c_lower"], s4)
        DV.wait(*s4)
        AC.wait(*s4)
        PO.wait(*s4)
        ln = layernorm(X, 1e-5, s4)
        ht = turn(XN, ln, HT)
        G = wview(WK, 0, 64, (4, 16))
        Gr = wview(WK, 64, 64, (4, 16))
        gs = wview(WK, 128, 8)
        cmpA = wview(WK, 256, 256, (16, 16))
        cmpB = wview(WK, 512, 256, (16, 16))
        AT = Ring([wview(WK, 1024 + 512 * i, 512) for i in range(3)])
        SG = Ring([wview(WK, 3072 + 512 * i, 512) for i in range(3)])
        gtok = []
        for t in range(NT):
            b, k = tokp(HT, 2, t, gw, 0, 16, [ht, gt])
            g = G[:, t, :]
            e = tt(g, b.ap[:, 0:16], gb, ALU.add, k, gt2)
            b.free = [e]
            e = act(g, g, ACT.Sigmoid, e)
            gj = g.rearrange("p (a b) -> p a b", a=1).to_broadcast([128, 16, 16])
            gi = g.rearrange("p (a b) -> p a b", b=1).to_broadcast([128, 16, 16])
            c1 = tt(cmpA, gj, gi, ALU.is_equal, e)
            c2 = tt(cmpB, gj, gi, ALU.is_gt, e)
            c1 = tt(cmpA, cmpA, ll, ALU.mult, c1, gt3)
            c1 = tt(cmpA, cmpA, cmpB, ALU.add, c1, c2)
            r = red(Gr[:, t, :], cmpA, ALU.add, c1)
            r = stt(Gr[:, t, :], Gr[:, t, :], 2.0, g, ALU.is_lt, ALU.mult, r)
            e = red(gs[:, t:t + 1], Gr[:, t, :], ALU.add, r)
            e = rec(gs[:, t:t + 1], gs[:, t:t + 1], e)
            gtok.append(ts(g, Gr[:, t, :], gs[:, t:t + 1], None, ALU.mult, None, e))
        xa = [tt(X[:, t, :], X[:, t, :], XN[:, t, :], ALU.add, ln, E=PO) for t in range(NT)]
        for i in range(17):
            s, wg, wu, wd, tk = exq.pop(i)
            b, k = feat(wg, 0, 128, HT, 2, [ht, tk])
            b2, k2 = feat(wu, 0, 128, HT, 2, [ht, tk])
            sg, at = SG.take(), AT.take()
            e = act(sg.ap, b.ap, ACT.Silu, k, sg.free)
            b.free = [e]
            e = tt(at.ap, sg.ap, b2.ap, ALU.mult, e, k2, at.free)
            b2.free = [e]
            sg.free = [e]
            for t in range(0, NT, 2):
                b = banks.take()
                for q in range(2):
                    x = mm(b.ap[:, q * 256:(q + 1) * 256], at.ap[:, (t + q) * 128:(t + q + 1) * 128], wd, e, tk, b.free)
                for q in range(2):
                    sc = 1.0 if i == 16 else G[:, t + q, i:i + 1]
                    xa[t + q] = stt(X[:, t + q, :], b.ap[:, q * 256:(q + 1) * 256], sc, X[:, t + q, :],
                                    ALU.mult, ALU.add, x, xa[t + q], gtok[t + q])
                b.free = [xa[t + 1]]
            at.free = [x]
            s.free = [x]
            if i + NE < 17:
                load_expert(i + NE)
        s5 = now()
        if stage == 6:
            dump(X)
            return

        def load_l2a(*w):
            r, tok, at = {}, [], 0
            for n, kt, m in (("q", 2, 1024), ("kv", 2, 2048), ("o", 8, 256), ("g", 2, 16)):
                r[n], t = wload(WB, at, "L2a_" + n, kt, m, *w)
                at += kt * m
                tok.append(t)
            tok.append(col("L2a_w", 8, 2, *w)[1])
            r["tok"] = tok
            return r

        WL2a = load_l2a(s5)
        for e_ in (DV, AC, PO):
            e_.wait(*s5)
        ln = layernorm(X, 1e-5, s5)
        ht = turn(XN, ln, HT)
        S = [wview(WK, 4096 * i, 4096) for i in range(4)]
        CT = Ring([wview(WK, 16384 + 1024 * i, 1024, (2, 512)) for i in range(3)])
        CN = Ring([wview(WK, 19456 + 2048 * i, 2048, (8, 256)) for i in range(3)])
        PT4 = Ring([wview(WK, 25600 + 512 * i, 512) for i in range(4)])
        mxs = wview(WK, 27648, 64)
        for bb in range(2):
            ev = {0: [], 1: []}
            for c in range(8):
                ct = CT.take()
                src = D["ctxT"][:, bb * 4096 + c * 512:bb * 4096 + (c + 1) * 512].rearrange("(t p) n -> p t n", p=128)
                ld = Q.go(ct.ap, src, s5, ct.free)
                for q in range(2):
                    t = bb * 2 + q
                    b = banks.take()
                    for k in range(2):
                        x = mm(b.ap, HT[:, k, t * 128:(t + 1) * 128], ct.ap[:, k, :], ht, ld, b.free, start=k == 0, stop=k == 1)
                    m = red(mxs[:, t * 16 + c:t * 16 + c + 1], b.ap, ALU.max, x)
                    e = cp(S[t][:, c * 512:(c + 1) * 512], b.ap, m, E=AC)
                    b.free = [e, m]
                    ev[q] = [e, m]
                ct.free = [x]
            ex = []
            for q in range(2):
                t = bb * 2 + q
                m = red(mxs[:, t * 16 + 8:t * 16 + 9], mxs[:, t * 16:t * 16 + 8], ALU.max, ev[q], negate=True)
                e = act(S[t], S[t], ACT.Exp, m, ev[q], bias=mxs[:, t * 16 + 8:t * 16 + 9], scale=1.0,
                        accum_out=mxs[:, t * 16 + 9:t * 16 + 10])
                ex.append(e)
            acc = [banks.take(), banks.take()]
            pend = []

            def pvx(item):
                cn, ld, j0, pts = item
                for q in range(2):
                    pt, c = pts[q]
                    for j in range(4):
                        n = j0 + j
                        x = mm(acc[q].ap[:, 0:256], pt.ap[:, j * 128:(j + 1) * 128], cn.ap[:, n % 8, :], c, ld,
                               acc[q].free, start=n == 0, stop=n == 31, inc=j == 3)
                    pt.free = [x]
                cn.free = [x]
                return x
            TB = [bk for bk in banks.slots if bk not in acc]
            for g in range(8):
                if g % 2 == 0:
                    cn = CN.take()
                    r0 = bb * 4096 + g * 512
                    ld = Q.go(cn.ap, D["ctx"][r0:r0 + 1024, :].rearrange("(t p) n -> p t n", p=128), s5, cn.free)
                pts = []
                for q in range(2):
                    t = bb * 2 + q
                    b = TB[(g * 2 + q) % 6]
                    for j in range(4):
                        n = g * 4 + j
                        x = tr(b.ap[:, j * 128:(j + 1) * 128], S[t][:, n * 128:(n + 1) * 128], idf[:, :], ex[q], b.free)
                    pt = PT4.take()
                    c = cp(pt.ap, b.ap, x, pt.free, E=(DV, AC)[q])
                    b.free = [c]
                    pts.append((pt, c))
                pend.append((cn, ld, g * 4, pts))
                if len(pend) > 1:
                    x = pvx(pend.pop(0))
            x = pvx(pend.pop(0))
            for q in range(2):
                t = bb * 2 + q
                r = rec(mxs[:, t * 16 + 10:t * 16 + 11], mxs[:, t * 16 + 9:t * 16 + 10], ex[q])
                e = stt(X[:, t, :], acc[q].ap[:, 0:256], mxs[:, t * 16 + 10:t * 16 + 11], X[:, t, :], ALU.mult, ALU.add, x, r, ln)
                acc[q].free = [e]
        s6 = now()
        if stage == 7:
            dump(X)
            return

        def load_l2f(*w):
            r, tok = {}, []
            for i, n in enumerate("rkv"):
                r[n], t = wload(WA, 512 * i, "L2f_" + n, 2, 256, *w)
                tok.append(t)
            tok.append(col("L2f_mr", 48, 2, *w)[1])
            tok.append(col("L2f_mk", 50, 2, *w)[1])
            r["tok"] = tok
            return r

        WL2f = load_l2f(s6)
        for e_ in (DV, AC, PO):
            e_.wait(*s6)
        zh = zero_halves(s6)
        ln = layernorm(X, 1e-5, s6)
        W = WL2a
        a = []
        for t in range(NT):
            DV.wait(ln[t])
            a.append(DV.done(nc.vector.bn_stats(st[:, t, :], XN[:, t, :])))
        for t in range(NT):
            DV.wait(a[t])
            a[t] = DV.done(nc.vector.bn_aggr(mv[:, t, :], st[:, t, :]))
        e = tt(rs[:, :], mv[:, :, 0], mv[:, :, 0], ALU.mult, a[3])
        e = tt(rs[:, :], rs[:, :], mv[:, :, 1], ALU.add, e)
        e = rsqrt(rs[:, :], rs[:, :], float(np.finfo(np.float32).eps), ALU.add, e)
        xr = [ts(XR[:, t, :], XN[:, t, :], rs[:, t:t + 1], None, ALU.mult, None, e) for t in range(NT)]

        def scaled(f, src, dst, k):
            return ts(dst, src, sm[:, 8 + f:9 + f], None, ALU.mult, None, k, W["tok"])

        ht = turn(XR, xr, HT, scaled)
        qk = []
        for m in range(8):
            b, k = feat(W["q"], m * 128, 128, HT, 2, [ht, W["tok"]])
            qk.append(ts(QZ[0:64, 2 * m, :], b.ap[0:64, :], 0.125, None, ALU.mult, None, k))
            qk.append(ts(QZ[64:128, 2 * m + 1, :], b.ap[64:128, :], 0.125, None, ALU.mult, None, k))
            b.free = [qk[-1]]
            b, k = feat(W["kv"], m * 128, 128, HT, 2, [ht])
            qk.append(cp(KT[:, m, :], b.ap, k, E=AC))
            b.free = [qk[-1]]
        vt = vproj(HT, 2, W["kv"], 1024, [ht])
        gate = wview(WK, 31264, 64, (4, 16))
        ge = None
        for t in range(NT):
            b, k = tokp(HT, 2, t, W["g"], 0, 16, [ht])
            ge = act(gate[:, t, :], b.ap[:, 0:16], ACT.Sigmoid, k)
            b.free = [ge]
        o = attn64(16, [qk, vt, ge, zh], 0, gate=gate)
        add_out(OT, 8, W["o"], [o])
        s7 = now()
        if stage == 8:
            dump(X)
            return

        def load_l3x(*w):
            r, tok = {}, []
            for i, n in enumerate("qkvp"):
                r[n], t = wload(WB, 512 * i, "L3x_" + n, 2, 256, *w)
                tok.append(t)
            r["ff"] = sm[:, 52:53]
            tok.append(Q.go(sm[:, 52:53], D["L3x_ff"].rearrange("(a n) -> a n", a=1).to_broadcast([128, 1]), *w))
            r["tok"] = tok
            return r

        WL3x = load_l3x(s7)
        for e_ in (DV, AC, PO):
            e_.wait(*s7)
        W = WL2f
        ln = layernorm(X, 1e-5, s7)
        ht = turn(XN, ln, HT)
        XRK = [wview(WK, 1024 * i, 1024, (2, 512)) for i in range(2)]
        XD = wview(WK, 2048, 1024, (2, 512))
        KA = wview(WK, 3072, 1024, (2, 512))
        RR = wview(WK, 4096, 1024, (4, 256))
        d = []
        for f in range(2):
            hv = HT[:, f, :].rearrange("p (b t) -> p b t", b=2)
            dv = XD[:, f, :].rearrange("p (b t) -> p b t", b=2)
            e = tt(dv[:, :, 1:256], hv[:, :, 1:256], hv[:, :, 0:255], ALU.subtract, ht)
            e2 = cp(dv[:, :, 0:1], hv[:, :, 0:1], ht)
            for i in range(2):
                pv_ = XRK[i][:, f, :].rearrange("p (b t) -> p b t", b=2)
                mu = sm[:, 48 + 2 * i + f:49 + 2 * i + f]
                e3 = ts(rs[:, 0:1], mu, -1.0, 1.0, ALU.mult, ALU.add, W["tok"], now())
                e4 = ts(pv_, hv, mu, None, ALU.mult, None, e3)
                e5 = stt(pv_[:, :, 1:256], hv[:, :, 0:255], rs[:, 0:1], pv_[:, :, 1:256], ALU.mult, ALU.add, e3, e4)
                d.append(e5)
        ka = []
        for m in range(2):
            b, k = feat(W["k"], m * 128, 128, XRK[1], 2, [d, W["tok"]])
            e = ts(KA[:, m, :], b.ap, 0.0, None, ALU.max, None, k)
            b.free = [e]
            ka.append(tt(KA[:, m, :], KA[:, m, :], KA[:, m, :], ALU.mult, e))
        for t in range(NT):
            b, k = tokp(XRK[0], 2, t, W["r"], 0, 256, [d])
            e = act(RR[:, t, :], b.ap[:, 0:256], ACT.Sigmoid, k)
            b.free = [e]
            b, k = tokp(KA, 2, t, W["v"], 0, 256, [ka])
            e = tt(RR[:, t, :], b.ap[:, 0:256], RR[:, t, :], ALU.mult, e, k)
            b.free = [e]
            e = tt(X[:, t, :], X[:, t, :], RR[:, t, :], ALU.add, e)
        s8 = now()
        if stage == 9:
            dump(X)
            return

        def load_l3a(*w):
            r, tok, at = {}, [], 0
            for n, kt, m in (("q", 2, 256), ("k", 2, 256), ("v", 2, 512), ("o", 4, 256)):
                r[n], t = wload(WA, at, "L3a_" + n, kt, m, *w)
                at += kt * m
                tok.append(t)
            r["vb"] = WA[:, at:at + 512]
            tok.append(Q.go(r["vb"], D["L3a_vb"].rearrange("(a n) -> a n", a=1).to_broadcast([128, 512]), *w))
            r["ob"] = WA[:, at + 512:at + 768]
            tok.append(Q.go(r["ob"], D["L3a_ob"].rearrange("(a n) -> a n", a=1).to_broadcast([128, 256]), *w))
            tok.append(col("L3a_qb", 54, 2, *w)[1])
            tok.append(col("L3a_kb", 56, 2, *w)[1])
            r["tok"] = tok
            return r

        WL3a = load_l3a(s8)
        for e_ in (DV, AC, PO):
            e_.wait(*s8)
        W = WL3x
        ln = layernorm(X, 1e-5, s8)
        ht = turn(XN, ln, HT)
        NB = 4
        o_ = 0

        def part(n):
            nonlocal o_
            v = WK[:, o_:o_ + n]
            o_ += n
            return v

        CT = Ring([part(1024).rearrange("p (a b) -> p a b", a=2) for _ in range(3)])
        AXR = Ring([part(NB * 256).rearrange("p (a b) -> p a b", a=NB) for _ in range(2)])
        NPR = Ring([part(NB * 304).rearrange("p (a h c) -> p a h c", a=NB, h=16) for _ in range(2)])
        RPR = Ring([part(NB * 304).rearrange("p (a h c) -> p a h c", a=NB, h=16) for _ in range(2)])
        M8R = Ring([part(NB * 128).rearrange("p (a h c) -> p a h c", a=NB, h=16) for _ in range(2)])
        KHR = Ring([part(NB * 256).rearrange("p (a b) -> p a b", a=NB) for _ in range(2)])
        CNR = Ring([part(NB * 260).rearrange("p (a b) -> p a b", a=NB) for _ in range(4)])
        stR = Ring([part(32) for _ in range(5)])
        QH = part(1024).rearrange("p (a b) -> p a b", a=4)
        QHT = part(1024).rearrange("p (a b) -> p a b", a=2)
        GS = part(2 * 2 * 260).rearrange("p (b c n) -> p b c n", b=2, c=2)
        GTs = part(1024).rearrange("p (b f c) -> p b f c", b=2, f=2)
        KV = part(2 * 2 * 272).rearrange("p (b c n) -> p b c n", b=2, c=2)
        YY = part(1024).rearrange("p (a b) -> p a b", a=4)
        YYT = part(1024).rearrange("p (a b) -> p a b", a=2)
        epsc = part(1)
        t_eps = fill(epsc, 1e-6, s8)
        hm16 = part(32).rearrange("p (a b) -> p a b", a=2)
        t_hm = Q.go(hm16, D["c_hm16"].rearrange("(t p) n -> p t n", p=128), s8)
        assert o_ + 64 <= WKN, o_
        pad = []
        for s in NPR.slots:
            pad.append(fill(s.ap[:, :, :, 16:19], 5.0, s8))
        for s in CNR.slots:
            pad.append(fill(s.ap[:, :, 256:257], 1.0, s8))
        focR = Ring([PS[:, i, :] for i in range(4)])
        GB = [Slot(PS[:, 4 + i, :]) for i in range(2)]
        for s in focR.slots + GB:
            s.free = list(s8) + [PE.last(), DV.last(), AC.last()]

        def focus(lhs_of, Wm, wtok, dst):
            ax, npr, rpr, m8, sts = AXR.take(), NPR.take(), RPR.take(), M8R.take(), stR.take()
            axw, sw = ax.free, sts.free
            sv = sts.ap
            e1, bk2 = [], []
            for i in range(NB):
                if i % 2 == 0:
                    b = focR.take()
                    bk2.append(b)
                lhs, lt = lhs_of(i)
                for k in range(2):
                    x = mm(b.ap[:, (i % 2) * 256:(i % 2) * 256 + 256], lhs[k], Wm[:, k, 0:256], lt, wtok, b.free,
                           start=k == 0, stop=k == 1)
                if i % 2 == 1:
                    y0 = act(ax.ap[:, i - 1:i + 1, :].rearrange("p a b -> p (a b)"), b.ap, ACT.Copy, x, axw, scale=-0.01)
                    b.free = [y0]
            for j in range(NB):
                b = bk2[j // 2]
                e = stt(ax.ap[:, j, :], ax.ap[:, j, :], 1.0, b.ap[:, (j % 2) * 256:(j % 2) * 256 + 256],
                        ALU.mult, ALU.max, b.free, y0, sw, accum_out=sv[:, j:j + 1])
                e1.append(e)
                if j % 2 == 1:
                    b.free = [e]
            yield
            axf = ax.ap.rearrange("p a b -> p (a b)")
            l = act(axf, axf, ACT.Ln, e1, t_eps, bias=epsc[:, 0:1], scale=1.0)
            z = ts(axf, axf, W["ff"], None, ALU.mult, None, l, W["tok"])
            m = red(sv[:, 4:8], ax.ap, ALU.max, z, negate=True)
            yield
            e2 = []
            for i in range(NB):
                e2.append(act(ax.ap[:, i, :], ax.ap[:, i, :], ACT.Exp, m, bias=sv[:, 4 + i:5 + i], scale=1.0,
                              accum_out=sv[:, 8 + i:9 + i]))
            for i in range(NB):
                src = ax.ap[:, i, :].rearrange("p (h c) -> p h c", c=16)[:, :, ::-1]
                en = act(npr.ap[:, i, :, 0:16], src, ACT.Copy, e2[i], npr.free, pad, scale=-1.0)
            ax.free = [en]
            yield
            n1 = ts(sv[:, 12:16], sv[:, 0:4], 1.0 / 256, 1e-6, ALU.mult, ALU.add, e1[-1])
            r1 = rec(sv[:, 16:20], sv[:, 8:12], e2[-1])
            f = stt(sv[:, 20:24], sv[:, 12:16], -1.0, sv[:, 16:20], ALU.mult, ALU.mult, n1, r1)
            for i in range(NB):
                DV.wait(en, m8.free)
                for h in range(16):
                    x = DV.done(nc.vector.max(m8.ap[:, i, h, :], npr.ap[:, i, h, :]))
            yield
            qs = []
            for i in range(NB):
                DV.wait(x, rpr.free)
                for h in range(16):
                    q = DV.done(nc.vector.match_replace(rpr.ap[:, i, h, :], m8.ap[:, i, h, :], npr.ap[:, i, h, :], 0.0))
                qs.append(q)
            m8.free = [q]
            npr.free = [q]
            yield
            toks = []
            for i in range(NB):
                d_, dfree = dst(i)
                AC.wait(qs[i], f, dfree)
                o = act(d_.rearrange("p (h c) -> p h c", c=16), rpr.ap[:, i, :, 0:16][:, :, ::-1], ACT.Copy,
                        scale=sv[:, 20 + i:21 + i])
                toks.append(o)
            rpr.free = [o]
            sts.free = [o]
            yield toks

        gts, pend = [], []

        def gram(item):
            kh, cn, ld, toks, bb, g = item
            for i in range(NB):
                n = g * NB + i
                for c in range(2):
                    x = mm(GB[c].ap[:, 0:257], kh.ap[:, i, c * 128:(c + 1) * 128], cn.ap[:, i, 0:257], toks[i], ld,
                           GB[c].free, start=n == 0, stop=n == 31, inc=True)
            kh.free = [x]
            cn.free = [x]
            if g == 7:
                for c in range(2):
                    e = cp(GS[:, bb, c, 0:257], GB[c].ap[:, 0:257], x, E=AC)
                    GB[c].free = [e]
                    gts.append(e)

        def unit(u):
            if u == 0:
                f = focus(lambda i: ([HT[:, k, i * 128:(i + 1) * 128] for k in range(2)], ht), W["q"], W["tok"],
                          lambda i: (QH[:, i, :], None))
                next(f)
                return f, None
            bb, g = (u - 1) // 8, (u - 1) % 8
            ct = CT.take()
            src = D["ctxT"][:, bb * 4096 + g * 512:bb * 4096 + (g + 1) * 512].rearrange("(t p) n -> p t n", p=128)
            ld = Q.go(ct.ap, src, s8, ct.free)
            cn = CNR.take()
            r0 = bb * 4096 + g * 512
            ld2 = Q.go(cn.ap[:, :, 0:256], D["ctx"][r0:r0 + 512, :].rearrange("(t p) n -> p t n", p=128), s8, cn.free)
            kh = KHR.take()
            f = focus(lambda i: ([ct.ap[:, k, i * 128:(i + 1) * 128] for k in range(2)], ld), W["k"], W["tok"],
                      lambda i: (kh.ap[:, i, :], kh.free))
            next(f)
            ct.free = [PE.last()]
            return f, (kh, cn, [ld2, pad], bb, g)

        live = {}
        for u in range(17 + 4):
            if pend:
                gram(pend.pop(0))
            if u < 17:
                live[u] = unit(u)
            if 0 <= u - 3 < 17:
                f, rest = live.pop(u - 3)
                toks = next(f)
                if rest is None:
                    qh = toks
                else:
                    kh, cn, lds, bb, g = rest
                    pend.append((kh, cn, lds, toks, bb, g))
            if 0 <= u - 2 < 17:
                next(live[u - 2][0])
            if u < 17:
                next(live[u][0])
            if 0 <= u - 1 < 17:
                next(live[u - 1][0])
            if 0 <= u - 2 < 17:
                next(live[u - 2][0])
        while pend:
            gram(pend.pop(0))
        SB = [Slot(PS[:, 6 + i, :]) for i in range(2)]
        for s in SB:
            s.free = list(s8) + [PE.last(), DV.last(), AC.last()]
        qht = []
        for f in range(2):
            b = SB[f]
            for t in range(NT):
                k = tr(b.ap[:, t * 128:(t + 1) * 128], QH[:, t, f * 128:(f + 1) * 128], idf[:, :], qh[t], b.free)
            e = cp(QHT[:, f, :], b.ap, k)
            b.free = [e]
            qht.append(e)
        s8b = now()
        for bk in banks.slots:
            bk.free = list(s8b)
        yv_ = []
        for bb in range(2):
            gt = []
            for f in range(2):
                b = banks.take()
                for c in range(2):
                    k = tr(b.ap[:, c * 128:(c + 1) * 128], GS[:, bb, c, f * 128:(f + 1) * 128], idf[:, :], gts, b.free)
                e = cp(GTs[:, bb, f, :], b.ap[:, 0:256], k)
                b.free = [e]
                gt.append(e)
            kv = []
            for c in range(2):
                b = banks.take()
                for f in range(2):
                    x = mm(b.ap[:, 0:256], GTs[:, bb, f, c * 128:(c + 1) * 128], W["v"][:, f, :], gt, b.free,
                           start=f == 0, stop=f == 1)
                e = stt(KV[:, bb, c, 0:256], b.ap[:, 0:256], 1.0 / 256, bmask[:, c, :], ALU.mult, ALU.mult, x)
                b.free = [e]
                e2 = ts(KV[:, bb, c, 256:272], hm16[:, c, :], GS[:, bb, c, 256:257], 1.0 / 4096, ALU.mult, ALU.mult, t_hm, gts)
                kv += [e, e2]
            for q in range(2):
                t = bb * 2 + q
                b, x = tokp(QHT, 2, t, KV[:, bb, :, :], 0, 272, [kv, qht])
                z = YY[:, t, :]
                zi = mv_ = WK[:, o_ + 16 * t:o_ + 16 * t + 16]
                e = ts(zi, b.ap[:, 256:272], 1e-6, None, ALU.add, None, x)
                e = rec(zi, zi, e)
                e = tt(z.rearrange("p (h c) -> p h c", c=16), b.ap[:, 0:256].rearrange("p (h c) -> p h c", c=16),
                       zi.rearrange("p (h c) -> p h c", c=1).to_broadcast([128, 16, 16]), ALU.mult, e)
                b.free = [e]
                yv_.append(e)
        yt = turn(YY, yv_, YYT)
        add_out(YYT, 2, W["p"], [yt])
        s9 = now()
        if stage == 10:
            dump(X)
            return

        def load_l3f(l, t_, w):
            r, tok, at = {}, [], 0
            for n, kt, m in (("qkv", 2, 1536), ("o", 4, 256), ("w2", 6, 256)):
                r[n], t = wload(t_, at, f"L3f_{n}{l}", kt, m, w)
                at += kt * m
                tok.append(t)
            return r, tok, at

        WL3f, tk3, at3 = load_l3f(0, WB, s9)
        WL3f["w1"], t = wload(WB, at3, "L3f_w10", 2, 1536, s9)
        tk3.append(t)
        for e_ in (DV, AC, PO):
            e_.wait(*s9)
        W = WL3a
        ln = layernorm(X, 1e-5, s9)
        ht = turn(XN, ln, HT)
        o = attn16(W["q"], W["k"], W["v"], [ht, W["tok"]], 1.0 / 16, 1, qb=sm[:, 54:56], kb=sm[:, 56:58], vb=W["vb"])
        add_out(OT2, 4, W["o"], [o], extra=[(W["ob"], W["tok"])] * NT)
        s10 = now()
        if stage == 11:
            dump(X)
            return

        for e_ in (DV, AC, PO):
            e_.wait(*s10)
        ln = layernorm(X, 1e-5, s10)
        XL = XN
        xtok = ln
        tab = wview(WA, 0, 1024, (4, 256))
        ttab = Q.go(tab, D["L3f_tab"].rearrange("(t p) n -> p t n", p=128), s10)
        zrow = WA[:, 1024:1152]
        tz = fill(zrow, 0.0, s10)
        QT_ = wview(WK, 26112, 0) if False else None
        QN = wview(WK, 20480, 2048, (4, 512))
        QN2 = wview(WK, 22528, 2048, (4, 512))
        sq = Ring([wview(WK, 24576 + 512 * i, 512) for i in range(3)])
        XS = wview(WK, 30208, 1024, (4, 256))
        OT3 = wview(WK, 16384, 2048, (4, 512))
        for l in range(2):
            W = WL3f
            sl = now()
            for e_ in (DV, AC, PO):
                e_.wait(*sl)
            wx = [xtok, sl]
            small = [Q.go(WA[:, 1152 + 64 * i:1216 + 64 * i],
                          D[n][l:l + 1, :].to_broadcast([128, 64]), sl)
                     for i, n in enumerate(("L3f_qs", "L3f_ks"))]
            small.append(Q.go(WA[:, 1280:1536], D["L3f_b2"][l:l + 1, :].to_broadcast([128, 256]), sl))
            small.append(Q.go(sm[:, 64:76], D["L3f_b1"][l], sl))
            small.append(Q.go(sm[:, 76:78], D["L3f_lg"][l], sl))
            small.append(Q.go(sm[:, 78:80], D["L3f_lb"][l], sl))
            zh = zero_halves(sl)
            zz = fill(HT[:, 1, :].rearrange("p (b t) -> p b t", b=2)[:, :, 0:1], 0.0, sl)

            def shifted(f, src, dst, k):
                if f == 0:
                    return cp(dst, src, k)
                sv = src.rearrange("p (b t) -> p b t", b=2)
                dv = dst.rearrange("p (b t) -> p b t", b=2)
                return cp(dv[:, :, 1:256], sv[:, :, 0:255], k, zz)

            ht = turn(XL, [xtok] * NT, HT, shifted)
            fin = []
            for which in range(2):
                QQ = (QN, QN2)[which]
                s_ = WA[:, 1152 + 64 * which:1216 + 64 * which]
                qq = []
                for t in range(NT):
                    b, k = tokp(HT, 2, t, W["qkv"], 512 * which, 512, [ht, zz, tk3])
                    s = sq.take()
                    e = act(s.ap, b.ap, ACT.Square, k, s.free, sl)
                    rr = rs2 = wview(WK, 31300 + (which * 4 + t) * 16, 8)
                    e = red(rr, s.ap.rearrange("p (h d) -> p h d", d=64), ALU.add, e)
                    s.free = [e]
                    e = rsqrt(rr, rr, 1e-24, ALU.max, e)
                    q3 = QQ[:, t, :].rearrange("p (h d) -> p h d", d=64)
                    e = tt(q3, b.ap.rearrange("p (h d) -> p h d", d=64),
                           rr.rearrange("p (h d) -> p h d", d=1).to_broadcast([128, 8, 64]), ALU.mult, e)
                    b.free = [e]
                    e = tt(q3, q3, s_.rearrange("p (h d) -> p h d", h=1).to_broadcast([128, 8, 64]), ALU.mult, e, small)
                    C = tab[:, t, 0:64] if which == 0 else tab[:, t, 128:192]
                    Sn = tab[:, t, 64:128] if which == 0 else tab[:, t, 192:256]
                    s = sq.take()
                    s3 = s.ap.rearrange("p (h d) -> p h d", d=64)
                    Sb = Sn.rearrange("p (h d) -> p h d", h=1)
                    e2 = tt(s3[:, :, 0:32], q3[:, :, 32:64], Sb[:, :, 0:32].to_broadcast([128, 8, 32]), ALU.mult, e, s.free, ttab, E=PO)
                    e2 = tt(s3[:, :, 32:64], q3[:, :, 0:32], Sb[:, :, 32:64].to_broadcast([128, 8, 32]), ALU.mult, e, E=PO)
                    e = tt(q3, q3, C.rearrange("p (h d) -> p h d", h=1).to_broadcast([128, 8, 64]), ALU.mult, e, e2, ttab)
                    e = tt(QQ[:, t, :], QQ[:, t, :], s.ap, ALU.add, e, e2)
                    s.free = [e]
                    qq.append(e)
                for m in range(4):
                    b = banks.take()
                    for t in range(NT):
                        k = tr(b.ap[:, t * 128:(t + 1) * 128], QQ[:, t, m * 128:(m + 1) * 128], idf[:, :], qq[t], b.free)
                    if which == 0:
                        e = cp(QZ[0:64, 2 * m, :], b.ap[0:64, :], k, zh, E=DV)
                        e2 = cp(QZ[64:128, 2 * m + 1, :], b.ap[64:128, :], k, zh, E=AC)
                        b.free = [e, e2]
                        fin += [e, e2]
                    else:
                        e = cp(KT[:, m, :], b.ap, k, E=AC)
                        b.free = [e]
                        fin.append(e)
            vt = vproj(HT, 2, W["qkv"], 1024, [ht, zz, tk3], n=512)
            o = attn64(8, [fin, vt, zh, now()], 2, OTv=OT3)
            e = add_out(OT3, 4, W["o"], [o], dst=XL)
            sh = []
            for t in range(NT):
                sh.append(Q.go(XS[1:128, t, 128:256], XL[0:127, t, 128:256], e))
                if t % 2 == 0:
                    sh.append(Q.go(XS[0:1, t, 128:256], zrow[0:1, 0:128], tz, e))
                else:
                    sh.append(Q.go(XS[0:1, t, 128:256], XL[127:128, t - 1, 128:256], e))
                sh.append(cp(XS[:, t, 0:128], XL[:, t, 0:128], e, E=PO))
            ln = layernorm(XS, 1e-5, sh, dst=XS)
            ht = turn(XS, ln, HT, affine(sm[:, 76:78], sm[:, 78:80], small))
            if l == 0:
                sw = now()
                nxt, tkn = {}, []
                for n, kt, m, at in (("qkv", 2, 1536, 0), ("o", 4, 256, 3072)):
                    nxt[n], t = wload(WB, at, f"L3f_{n}1", kt, m, sw)
                    tkn.append(t)
            AG = wview(WK, 0, 3072, (6, 512))
            GG = Ring([wview(WK, 3072 + 512 * i, 512) for i in range(3)])
            sA = now()
            ag = []
            for m in range(6):
                b, k = feat(W["w1"], m * 128, 128, HT, 2, [ht, tk3])
                b2, k2 = feat(W["w1"], 768 + m * 128, 128, HT, 2, [ht])
                g = GG.take()
                e = act(g.ap, b2.ap, ACT.Gelu, k2, small, g.free, sA, bias=sm[:, 70 + m:71 + m], scale=1.0)
                b2.free = [e]
                e = stt(AG[:, m, :], b.ap, sm[:, 64 + m:65 + m], g.ap, ALU.add, ALU.mult, e, k, small)
                b.free = [e]
                g.free = [e]
                ag.append(e)
            e = add_out(AG, 6, W["w2"] if l == 0 else W["w2"], [ag], extra=[(WA[:, 1280:1536], small)] * NT, dst=XL)
            xtok = e
            if l == 0:
                sw = now()
                nxt["w1"], t = wload(WB, 5632, "L3f_w11", 2, 1536, sw)
                nxt["w2"], t2 = wload(WB, 4096, "L3f_w21", 6, 256, sw)
                WL3f = nxt
                tk3 = tkn + [t, t2]
        for t in range(NT):
            e = tt(X[:, t, :], X[:, t, :], XL[:, t, :], ALU.add, xtok)
        dump(X)


def host_arrays(v):
    f = np.float32

    def T(a):
        return np.ascontiguousarray(np.asarray(a).T)

    def C(a):
        return np.ascontiguousarray(np.asarray(a))

    def headpad(a, n=16, hd=16, to=32):
        a = np.asarray(a)
        o = np.zeros(a.shape[:-1] + (n, to), a.dtype)
        o[..., :hd] = a.reshape(a.shape[:-1] + (n, hd))
        return np.ascontiguousarray(o.reshape(a.shape[:-1] + (n * to,)))

    A = {}
    A["x"] = C(v["x"]).reshape(512, 256)
    ctx = C(v["ctx_1024"]).reshape(8192, 256)
    A["ctx"] = ctx
    A["ctxT"] = T(ctx)
    A["mask_BxS2_ik0"] = C(v["mask_BxS2_ik0"])
    for n in "qkv":
        A["L0x_" + n] = T(v[f"L0_xattn_{n}_w"])
    A["L0x_qb"] = C(v["L0_xattn_q_b"])
    A["L0x_kb"] = C(v["L0_xattn_k_b"])
    A["L0x_vb"] = C(v["L0_xattn_v_b"])
    A["L0a_dq"], A["L0a_dkv"] = T(v["L0_attn_w_down_q"]), T(v["L0_attn_w_down_kv"])
    swap = np.arange(1024) ^ 1
    for n, w in (("uq", "q"), ("uk", "k"), ("uv", "v")):
        A["L0a_" + n] = T(v["L0_attn_w_up_" + w])
    A["L0a_uqs"] = C(T(v["L0_attn_w_up_q"])[:, swap])
    A["L0a_uks"] = C(T(v["L0_attn_w_up_k"])[:, swap])
    A["L0a_o"] = T(v["L0_attn_w_out"])
    A["L0a_g"], A["L0a_b"] = C(v["L0_attn_ln_scale"]), C(v["L0_attn_ln_bias"])
    inv = 1.0 / 10000.0 ** (np.arange(0, 64, 2, dtype=f) / 64)
    fr = np.outer(np.arange(256, dtype=f), inv)
    cos = np.concatenate([np.cos(fr), np.cos(fr)], -1)[:, ::2]
    sin = np.concatenate([np.sin(fr), np.sin(fr)], -1)[:, ::2]
    ct = np.repeat(cos.T, 2, axis=0)
    sg = np.where(np.arange(64) % 2 == 0, -1.0, 1.0).astype(f)
    stb = np.repeat(sin.T, 2, axis=0) * sg[:, None]
    A["L0a_C"] = np.tile(ct, (2, 2)).astype(f)
    A["L0a_S"] = np.tile(stb, (2, 2)).astype(f)
    A["L0f_w1"] = T(v["L0_ffn_w1"])
    A["L0f_w2"] = T(v["L0_ffn_w2"])
    A["L0f_cv"] = C(np.concatenate([np.asarray(v["L0_ffn_conv_w"]).reshape(1024, 3), np.asarray(v["L0_ffn_conv_b"])[:, None]], 1))
    for n in "qkvo":
        A["L1x_" + n] = C(v["L1_xattn_W" + n])
    A["L1a_q"], A["L1a_k"] = T(v["L1_attn_Wq"]), T(v["L1_attn_Wk"])
    A["L1a_v"] = headpad(T(v["L1_attn_Wv"]))
    A["L1a_u"] = T(headpad(v["L1_attn_Wu"]))
    A["L1a_bu"] = C(v["L1_attn_bu"])
    A["L1f_gate"], A["L1f_gb"] = C(v["L1_ffn_gate_w"]), C(v["L1_ffn_gate_b"])
    for n, a, b in (("g", "wg", "shared_wg"), ("u", "wu", "shared_wu"), ("d", "wd", "shared_wd")):
        A["L1f_" + n] = np.concatenate([np.asarray(v["L1_ffn_experts_" + a]), np.asarray(v["L1_ffn_" + b])[None]], 0)
    A["L2a_q"], A["L2a_kv"], A["L2a_o"], A["L2a_g"] = (C(v["L2_attn_" + n]) for n in ("Wq", "Wkv", "Wout", "Wg"))
    A["L2a_w"] = C(v["L2_attn_norm_w"])
    for n in "rkv":
        A["L2f_" + n] = T(v["L2_ffn_W_" + n])
    A["L2f_mr"], A["L2f_mk"] = C(v["L2_ffn_mu_r"]), C(v["L2_ffn_mu_k"])
    for n in "qkvp":
        A["L3x_" + n] = T(v["L3_xattn_W" + n])
    A["L3x_ff"] = C(v["L3_xattn_focusing_factor"]).reshape(1)
    w = C(v["L3_attn_Wqkv"])
    bq = C(v["L3_attn_bqkv"])
    A["L3a_q"], A["L3a_k"], A["L3a_v"] = C(w[:, 0:256]), C(w[:, 256:512]), headpad(w[:, 512:768])
    A["L3a_qb"], A["L3a_kb"], A["L3a_vb"] = C(bq[0:256]), C(bq[256:512]), headpad(bq[512:768])
    A["L3a_o"] = T(headpad(T(v["L3_attn_Wout"])))
    A["L3a_ob"] = C(v["L3_attn_bout"])
    for l in range(2):
        A[f"L3f_qkv{l}"] = C(np.asarray(v["L3_ffn_wqkv"])[l])
        A[f"L3f_o{l}"] = C(np.asarray(v["L3_ffn_wo"])[l])
        w1 = np.asarray(v["L3_ffn_w1"])[l]
        p = np.zeros((256, 2, 768), w1.dtype)
        p[:, :, :HID] = w1.reshape(256, 2, HID)
        A[f"L3f_w1{l}"] = p.reshape(256, 1536)
        w2 = np.asarray(v["L3_ffn_w2"])[l]
        p = np.zeros((768, 256), w2.dtype)
        p[:HID] = w2
        A[f"L3f_w2{l}"] = p
    b1 = np.asarray(v["L3_ffn_b1"])
    p = np.zeros((2, 2, 768), b1.dtype)
    p[:, :, :HID] = b1.reshape(2, 2, HID)
    A["L3f_b1"] = p.reshape(2, 1536)
    A["L3f_b2"], A["L3f_lg"], A["L3f_lb"] = C(v["L3_ffn_b2"]), C(v["L3_ffn_ln_g"]), C(v["L3_ffn_ln_b"])
    A["L3f_qs"], A["L3f_ks"] = C(v["L3_ffn_q_scale"]), C(v["L3_ffn_k_scale"])
    half = np.arange(0, 64, 2, dtype=f)
    invf = 1.0 / 10000.0 ** (half / 64)
    t = np.arange(256, dtype=f)
    fr = t[:, None] * invf[None, :]
    fr = np.concatenate([fr, fr], -1)
    base = (half + 0.4 * 64) / (1.4 * 64)
    sc = base[None, :] ** ((t - 128) / 64.0)[:, None]
    sc = np.concatenate([sc, sc], -1)
    cs, sn = np.cos(fr), np.sin(fr)
    sgn = np.where(np.arange(64) < 32, -1.0, 1.0)
    tab = np.concatenate([cs * sc * 8.0, sn * sc * 8.0 * sgn, cs / sc, sn / sc * sgn], 1).astype(f)
    A["L3f_tab"] = np.ascontiguousarray(np.tile(tab, (2, 1)))
    for n in ("L0x_qb", "L0x_kb", "L0a_g", "L0a_b", "L2a_w", "L2f_mr", "L2f_mk", "L3a_qb", "L3a_kb"):
        A[n] = T(A[n].reshape(-1, 128))
    for n in ("L3f_b1", "L3f_lg", "L3f_lb"):
        A[n] = np.ascontiguousarray(A[n].reshape(2, -1, 128).transpose(0, 2, 1))
    A["c_id"] = np.eye(128, dtype=f)
    i, j = np.arange(256)[:, None], np.arange(256)[None, :]
    ms = [j > i, np.abs(i - j) > 128, (i < j) | (i > j + 128)]
    ms = [np.where(m, -BIG, 0.0).astype(f).reshape(2, 128, 256).transpose(1, 0, 2).reshape(128, 512) for m in ms]
    A["c_msk"] = np.ascontiguousarray(np.concatenate(ms, 1))
    s = np.zeros((128, 17), f)
    for q in range(4):
        s[32 * q:32 * q + 17] = np.eye(17, dtype=f)
    A["c_sel"] = s
    A["c_hm8"] = np.repeat(np.eye(8, dtype=f), 16, axis=0)
    hm = np.repeat(np.eye(16, dtype=f), 16, axis=0)
    A["c_hm16"] = hm
    A["c_bmask"] = np.ascontiguousarray(np.repeat(hm, 16, axis=1))
    lo = (np.arange(16)[None, :] < np.arange(16)[:, None]).astype(f)
    A["c_lower"] = np.ascontiguousarray(np.broadcast_to(lo.reshape(1, 256), (128, 256)))
    return A


def program(nc, arrays, stage=12):
    D = {n: nc.dram_tensor("in_" + n, a.shape, mybir.dt.from_np(a.dtype), kind="ExternalInput").ap()
         for n, a in arrays.items()}
    D["scr"] = nc.dram_tensor("scratch_mask", [2, 8192], BF, kind="Internal").ap()
    D["scrq"] = nc.dram_tensor("scratch_q", [3, 256, 512], BF, kind="Internal").ap()
    out = nc.dram_tensor("out_0", [512, 256], F, kind="ExternalOutput").ap()
    build(nc, D, out, stage)


def kernel(**inputs):
    import concourse.bacc as _bacc
    from concourse.bass_utils import run_bass_kernel_spmd as _run

    arrays = host_arrays(inputs)
    nc = _bacc.Bacc("TRN2", target_bir_lowering=False, num_devices=1)
    program(nc, arrays)
    r = _run(nc, [{"in_" + n: a for n, a in arrays.items()}], core_ids=[0])
    return np.asarray(r.results[0]["out_0"]).reshape(2, 256, 256)
```

```python
from contextlib import ExitStack

import numpy as np
import concourse.bass as bass
from concourse import mybir

F = mybir.dt.float32
R32 = mybir.dt.float32r
BF = mybir.dt.bfloat16
I32 = mybir.dt.int32
ALU = mybir.AluOpType
ACT = mybir.ActivationFunctionType
AX = mybir.AxisListType.X
BIG = float(2.0 ** 100)
MAGIC = 12582912.0
NT = 4
QAT = 2
HID = 682
WKN = 34432


class Engine:

    def __init__(self, eng, sem):
        self.eng, self.sem, self.n, self.seen = eng, sem, 0, {}
        self.serial = False

    def wait(self, *tokens):
        if self.serial and self.n > self.seen.get(id(self), 0):
            self.eng.wait_ge(self.sem, self.n)
            self.seen[id(self)] = self.n
        for t in tokens:
            if t is None:
                continue
            if isinstance(t, list):
                self.wait(*t)
                continue
            sem, key, value = t
            if self.seen.get(key, 0) < value:
                self.eng.wait_ge(sem, value)
                self.seen[key] = value

    def done(self, ins):
        self.n += 1
        ins.then_inc(self.sem, 1)
        return (self.sem, id(self), self.n)

    def last(self):
        return (self.sem, id(self), self.n) if self.n else None


class Queue:

    def __init__(self, engine, sems):
        self.engine, self.sems, self.count, self.i = engine, sems, [0] * len(sems), 0

    def go(self, out, src, *waits):
        i = self.i
        self.i = (i + 1) % len(self.sems)
        if self.count[i]:
            self.engine.wait((self.sems[i], (id(self), i), self.count[i]))
        self.engine.wait(*waits)
        self.count[i] += 16
        self.engine.eng.dma_start(out, src).then_inc(self.sems[i], 16)
        return (self.sems[i], (id(self), i), self.count[i])


class Slot:

    def __init__(self, ap):
        self.ap, self.free = ap, []


class Ring:
    def __init__(self, aps):
        self.slots, self.i = [Slot(a) for a in aps], 0

    def take(self):
        s = self.slots[self.i]
        self.i = (self.i + 1) % len(self.slots)
        return s


def build(nc, D, out, stage=12):
    ctx = ExitStack()
    with ctx:
        def sb(name, shape, dt=F):
            return ctx.enter_context(nc.sbuf_tensor(name, shape, dt))

        def sem(name):
            return ctx.enter_context(nc.semaphore(name))

        PE = Engine(nc.tensor, sem("s_pe"))
        DV = Engine(nc.vector, sem("s_dve"))
        AC = Engine(nc.scalar, sem("s_act"))
        PO = Engine(nc.gpsimd, sem("s_pool"))
        SP = Engine(nc.sync, sem("s_sp"))
        PO.serial = True
        Q = Queue(SP, [sem(f"s_d{i}") for i in range(100)])

        def now():
            return [PE.last(), DV.last(), AC.last(), PO.last()]

        def mm(o, l, r, *w, start=True, stop=True, inc=None, cols=False):
            PE.wait(*w)
            i = nc.tensor.matmul(o, l, r, start=start, stop=stop, skip_group_check=cols)
            return PE.done(i) if (stop if inc is None else inc) else None

        def tr(o, x, ident, *w):
            PE.wait(*w)
            return PE.done(nc.tensor.transpose(o, x, ident))

        def act(o, x, f, *w, **k):
            AC.wait(*w)
            return AC.done(nc.scalar.activation(o, x, f, **k))

        def ts(o, x, a, b, op0, op1, *w, E=DV, **k):
            E.wait(*w)
            if b is None:
                return E.done(E.eng.tensor_scalar(o, x, a, None, op0, **k))
            return E.done(E.eng.tensor_scalar(o, x, a, b, op0, op1, **k))

        def tt(o, x, y, op, *w, E=DV):
            E.wait(*w)
            return E.done(E.eng.tensor_tensor(o, x, y, op))

        def stt(o, x, s, y, op0, op1, *w, **k):
            DV.wait(*w)
            return DV.done(nc.vector.scalar_tensor_tensor(out=o, in0=x, scalar=s, in1=y, op0=op0, op1=op1, **k))

        def red(o, x, op, *w, **k):
            DV.wait(*w)
            return DV.done(nc.vector.tensor_reduce(o, x, AX, op, **k))

        def cp(o, x, *w, E=DV):
            E.wait(*w)
            if E is AC:
                return E.done(nc.scalar.activation(o, x, ACT.Copy))
            if E is PO:
                return E.done(nc.gpsimd.tensor_scalar(o, x, 1.0, None, ALU.mult))
            return E.done(E.eng.tensor_copy(o, x))

        def rec(o, x, *w):
            DV.wait(*w)
            return DV.done(nc.vector.reciprocal(o, x))

        def fill(o, v, *w, E=PO):
            E.wait(*w)
            return E.done(E.eng.memset(o, v))

        def rsqrt(o, x, c, op, *w):
            a = ts(o, x, c, None, op, None, *w)
            a = act(o, o, ACT.Sqrt, a)
            return rec(o, o, a)

        X = sb("X", [128, NT, 256])
        XN = sb("XN", [128, NT, 256])
        HT = sb("HT", [128, 2, 512])
        WA = sb("WA", [128, 4096])
        WB = sb("WB", [128, 8704])
        WK = sb("WK", [128, WKN])
        idf = sb("idf", [128, 128])
        idb = sb("idb", [128, 128], BF)
        msk = sb("msk", [128, 3, 512], BF)
        hm8 = sb("hm8", [128, 8])
        bmask = sb("bmask", [128, 2, 256])
        onesf = sb("onesf", [128, 128])
        XR0 = sb("XR0", [128, 1])
        st = sb("st", [128, NT, 6])
        mv = sb("mv", [128, NT, 2])
        rs = sb("rs", [128, NT])
        sm = sb("sm", [128, 256])
        PS = ctx.enter_context(nc.psum_tensor("PS", [128, 8, 512], F))
        banks = Ring([PS[:, i, :] for i in range(8)])

        def wview(t, a, n, shape=None):
            v = t[:, a:a + n]
            if shape and len(shape) == 2:
                return v.rearrange("p (a b) -> p a b", a=shape[0])
            if shape and len(shape) == 3:
                return v.rearrange("p (a b c) -> p a b c", a=shape[0], b=shape[1])
            return v

        def wload(t, at, name, kt, n, *w, rows=None):
            v = wview(t, at, kt * n, (kt, n))
            src = D[name] if rows is None else rows
            tok = Q.go(v, src.rearrange("(t p) n -> p t n", p=128), *w)
            return v, tok

        def col(name, at, n, *w):
            v = sm[:, at:at + n]
            return v, Q.go(v, D[name], *w)

        def ctx_chunk(slot, bb, c, *w):
            src = D["ctxT"][:, bb * 4096 + c * 512:bb * 4096 + (c + 1) * 512]
            return slot, Q.go(slot.ap, src.rearrange("(t p) n -> p t n", p=128), *w)

        def ctx_slots(lay):
            at = [WK[:, a:a + 1024] for a in (WKN - 2048, WKN - 1024)]
            at += [WB[:, a:a + 1024] for a in ((6880, 0, 1024), (6880,))[lay]]
            return [Slot(v.rearrange("p (a b) -> p a b", a=2)) for v in at]

        k0 = wload(WA, 512, "L0x_k", 2, 256)
        cs0 = ctx_slots(0)
        ch0 = [ctx_chunk(cs0[0], 0, 0)]
        v0 = wload(WA, 1024, "L0x_v", 2, 256)
        kb0 = col("L0x_kb", 2, 2)[1]
        ch0.append(ctx_chunk(cs0[1], 0, 1))
        cl = [Q.go(idf[:, :], D["c_id"]), Q.go(hm8[:, :], D["c_hm8"]),
              Q.go(bmask[:, :, :], D["c_bmask"].rearrange("(t p) n -> p t n", p=128)),
              Q.go(WK[:, 0:1536], D["c_msk"])]
        xl = Q.go(X[:, :, :], D["x"].rearrange("(t p) n -> p t n", p=128))
        ch0 += [ctx_chunk(cs0[c], 0, c) for c in range(2, 5)]
        t_ones = fill(onesf[:, :], 1.0)
        cst = [cp(idb[:, :], idf[:, :], cl), cp(msk[:, :, :].rearrange("p a b -> p (a b)"), WK[:, 0:1536], cl), t_ones]
        PE.wait(cst[0], t_ones)

        def layernorm(src, eps, *w, dst=None, E2=PO):
            dst = XN if dst is None else dst
            a = [None] * NT
            for t in range(NT):
                DV.wait(*w)
                a[t] = DV.done(nc.vector.bn_stats(st[:, t, :], src[:, t, :]))
            for t in range(NT):
                DV.wait(a[t])
                a[t] = DV.done(nc.vector.bn_aggr(mv[:, t, :], st[:, t, :]))
            r = rsqrt(rs[:, :], mv[:, :, 1], eps, ALU.add, a[3])
            return [ts(dst[:, t, :], src[:, t, :], mv[:, t, 0:1], rs[:, t:t + 1], ALU.subtract, ALU.mult, r)
                    for t in range(NT)]

        def turn(src, toks, dst, evac=None, n=2, *w):
            o = []
            for f in range(n):
                b = banks.take()
                for t in range(NT):
                    k = tr(b.ap[:, t * 128:(t + 1) * 128], src[:, t, f * 128:(f + 1) * 128], idf[:, :], toks[t], b.free)
                if evac is None:
                    e = cp(dst[:, f, :], b.ap, k, *w, E=(DV, AC)[f % 2])
                else:
                    e = evac(f, b.ap, dst[:, f, :], k)
                b.free = [e]
                o.append(e)
            return o

        def feat(Wt, c0, m, rhs, kt, toks):
            b = banks.take()
            for k in range(kt):
                t = mm(b.ap[0:m, :], Wt[:, k, c0:c0 + m], rhs[:, k, :], toks, b.free, start=k == 0, stop=k == kt - 1)
            return b, t

        def tokp(lhs, kt, t, Wt, c0, n, toks, bank=None, at=0):
            b = bank or banks.take()
            for k in range(kt):
                x = mm(b.ap[:, at:at + n], lhs[:, k, t * 128:(t + 1) * 128], Wt[:, k, c0:c0 + n], toks, b.free,
                       start=k == 0, stop=k == kt - 1)
            return b, x

        def selfattn(units, group, P, Pn, PT, rsum):
            n = len(units)
            S0, S1, S2 = {}, {}, {}
            ringP, ringN, ringT = Ring(P), Ring(Pn), Ring(PT)
            out = []

            def first(i):
                u = units[i]
                b = banks.take()
                for q in range(2):
                    o = b.ap[:, q * 256:(q + 1) * 256]
                    s = True
                    if u["mask"] is not None:
                        mm(o, idb[:, :], msk[:, u["mask"], q * 256:(q + 1) * 256], b.free, start=True, stop=False)
                        s = False
                    k = mm(o, u["q"][:, q * 128:(q + 1) * 128], u["k"], u["w"], b.free, start=s, stop=True)
                j = i % 4
                nm = rsum[:, j * 8:j * 8 + 2]
                m = red(nm, b.ap.rearrange("p (a b) -> p a b", a=2), ALU.max, k, u_free.get(j), negate=True)
                p = ringP.take()
                ss = rsum[:, j * 8 + 2:j * 8 + 4]
                for q in range(2):
                    e = act(p.ap[:, q * 256:(q + 1) * 256], b.ap[:, q * 256:(q + 1) * 256], ACT.Exp, m, p.free,
                            bias=nm[:, q:q + 1], scale=1.0, accum_out=ss[:, q:q + 1])
                b.free = [e, m]
                S0[i] = (p, ss, e)

            def norm(i):
                u, j = units[i], i % 4
                p, ss, e = S0.pop(i)
                r = rec(rsum[:, j * 8 + 4:j * 8 + 6], ss, e)
                rr = rsum[:, j * 8 + 4:j * 8 + 6]
                if u["gate"] is not None:
                    r = tt(rr, rr, u["gate"], ALU.mult, r)
                pn = ringN.take()
                for q in range(2):
                    z = ts(pn.ap[:, q * 256:(q + 1) * 256], p.ap[:, q * 256:(q + 1) * 256], rr[:, q:q + 1], None,
                           ALU.mult, None, r, pn.free)
                p.free = [z]
                u_free[j] = z
                S1[i] = (pn, z)

            def second(i):
                pn, z = S1.pop(i)
                b = banks.take()
                for k in range(2):
                    for q in range(2):
                        t = tr(b.ap[:, k * 256 + q * 128:k * 256 + (q + 1) * 128],
                               pn.ap[:, q * 256 + k * 128:q * 256 + (k + 1) * 128], idf[:, :], z, b.free)
                pn.free = [t]
                pt = ringT.take()
                c = cp(pt.ap, b.ap, t, pt.free, E=(DV, AC)[i % 2])
                b.free = [c]
                S2[i] = (pt, c)

            def third(i):
                if i % group == group - 1:
                    its = [S2.pop(j) for j in range(i - group + 1, i + 1)]
                    x = units[i]["pv"](its)
                    for pt, c in its:
                        pt.free = [x]

            u_free = {}
            for i in range(n + 5):
                if i < n:
                    first(i)
                if 0 <= i - 1 < n:
                    norm(i - 1)
                if 0 <= i - 3 < n:
                    second(i - 3)
                if 0 <= i - 5 < n:
                    third(i - 5)

        def add_out(src, kt, Wt, toks, extra=None, dst=None):
            dst = X if dst is None else dst
            o = []
            for t in range(NT):
                b, k = tokp(src, kt, t, Wt, 0, 256, toks)
                e = tt(dst[:, t, :], b.ap[:, 0:256], dst[:, t, :], ALU.add, k)
                b.free = [e]
                if extra is not None:
                    e = tt(dst[:, t, :], dst[:, t, :], extra[t][0], ALU.add, e, extra[t][1])
                o.append(e)
            return o

        scr = D["scr"]
        mi = WA[:, 2048:2176].bitcast(I32)
        mf = WA[:, 2176:2304]
        ml = Q.go(mi[0:64, :], D["mask_BxS2_ik0"].rearrange("b (t p) -> (b t) p", p=128))
        a = cp(mf[0:64, :], mi[0:64, :], ml)
        mrow = WA[:, 2304:2432].bitcast(BF)
        m0 = ts(mrow[0:64, 0:128], mf[0:64, :], 0.0, -BIG, ALU.is_gt, ALU.mult, a)
        m1a = ts(mf[0:64, :], mf[0:64, :], -1.0, 1.0, ALU.mult, ALU.add, a, m0)
        m1 = ts(mrow[0:64, 128:256], mf[0:64, :], -BIG, None, ALU.mult, None, m1a)
        md = [Q.go(scr[l:l + 1, :].rearrange("a (t p) -> (a t) p", p=128), mrow[0:64, l * 128:(l + 1) * 128], [m0, m1][l])
              for l in range(2)]
        anyk = sb("anyk", [128, 2])
        mn = WA[:, 2440:2456]

        def anykeys():
            a = red(mn[0:64, 0:1], mf[0:64, :], ALU.min, m1)
            b = banks.take()
            a = tr(b.ap[0:1, 0:64], mn[0:64, 0:1], idf[0:64, 0:64], a, b.free)
            e = red(mn[0:1, 4:6], b.ap[0:1, 0:64].rearrange("p (a b) -> p a b", a=2), ALU.min, a)
            b.free = [e]
            e = ts(mn[0:1, 6:8], mn[0:1, 4:6], 1.0, None, ALU.is_lt, None, e)
            b = banks.take()
            a = mm(b.ap[:, 0:2], onesf[0:1, :], mn[0:1, 6:8], e, b.free)
            t = cp(anyk[:, :], b.ap[:, 0:2], a)
            b.free = [t]
            return t

        flag = {}

        def load_l0x(*w):
            q = wload(WA, 0, "L0x_q", 2, 256, *w)
            c = col("L0x_qb", 0, 2, *w)[1]
            return dict(q=q[0], k=k0[0], v=v0[0], tok=[k0[1], v0[1], kb0], qtok=[q[1], c], qb=sm[:, 0:2], kb=sm[:, 2:4])

        def load_l1x(*w):
            r = {}
            tok = []
            for i, n in enumerate("qkvo"):
                r[n], t = wload(WB, 512 * i, "L1x_" + n, 2, 256, *w)
                tok.append(t)
            r["tok"] = tok
            r["qtok"] = tok
            return r

        def crossattn(W, lay, prep, later, slots, ch):
            start = now()
            o = 0

            def part(n, dt=F):
                nonlocal o
                v = WK[:, o:o + n]
                o += n
                return v if dt is F else v.bitcast(dt)

            KF = [part(2048) for _ in range(4)]
            KS = [k.bitcast(BF) for k in KF]
            KH, KM, KL = part(2048, BF), part(2048, BF), part(2048, BF)
            CT, more = Ring([]), slots[2:]
            CT.slots = slots[0:2]
            K32 = Ring([part(512) for _ in range(2)])
            V = [v.rearrange("p (a b) -> p a b", a=32) for v in (part(4832), part(4832), WB[:, 2048:6880])]
            PR = Ring([part(512) for _ in range(5)])
            QF = part(4096)
            QS = QF.bitcast(BF).rearrange("p (h t) -> p h t", h=16)
            PV = Ring([part(256) for _ in range(1)])
            mx = part(64)
            mxb = part(16, BF)
            mxr = part(16)
            rd = Ring([part(36) for _ in range(2)])
            assert o <= WKN - 2048, o
            qx = V[1][:, :, :].rearrange("p a b -> p (a b)")
            q32 = qx[:, 0:1024].rearrange("p (a b) -> p a b", a=2)
            qp = [qx[:, 1024 + 512 * i:1536 + 512 * i].bitcast(BF).rearrange("p (a b) -> p a b", a=2) for i in range(3)]
            qr = qx[:, 2560:3584].rearrange("p (a b) -> p a b", a=2)
            kst = [Q.go(KF[s][96:99, :], D["c_krows"], start) for s in range(4)]
            z2 = Q.go(QF[96:100, :], D["c_qrows"], start)
            vc = [None, None, None]

            def vconst(s, *w):
                vv = V[s]
                vc[s] = [fill(vv[:, :, 136:151], 0.0, *w, E=PO),
                         fill(vv[:, :, 0:136].rearrange("p a (h c) -> p a h c", c=17)[:, :, :, 16], 1.0, *w, E=PO)]

            vconst(0, start)
            vconst(2, start)
            vbuf = (0, 2, 0, 1)
            ko = (0, 0, 0, 1, 1, 2)
            kparts = (KH, KM, KL)
            kfree, vfree = [], [[], [], []]
            ktok, vtok, stk, mtok = {}, {}, {}, {}
            kstfree, mxfree = [[] for _ in range(4)], [[], []]
            PJ, P1, ST = Ring([]), Ring([]), Ring([])
            ST.slots, P1.slots, PJ.slots = banks.slots[0:3], banks.slots[3:5], banks.slots[0:3] + banks.slots[6:8]
            PVB = banks.slots[5]
            PE.wait(*start)
            AC.wait(*start)
            def keys(g, c, ct, ld):
                m = g % 2
                b = PJ.take()
                for k in range(2):
                    x = mm(b.ap, W["k"][:, k, m * 128:(m + 1) * 128], ct.ap[:, k, :], ld, b.free, W["tok"],
                           start=k == 0, stop=k == 1)
                    if k == 0:
                        yield
                k32 = K32.take()
                sl = slice(c * 512, (c + 1) * 512)
                if lay == 0:
                    e = act(k32.ap, b.ap, ACT.Identity, x, k32.free, bias=W["kb"][:, m:m + 1], scale=1.0)
                    h = act(KH[:, sl], b.ap, ACT.Identity, kfree, bias=W["kb"][:, m:m + 1], scale=1.0)
                else:
                    e = act(k32.ap, b.ap, ACT.Copy, x, k32.free)
                    h = act(KH[:, sl], b.ap, ACT.Copy, kfree)
                b.free = [h]
                ct.free = ct.free + [x]
                r = tt(k32.ap, k32.ap, KH[:, sl], ALU.subtract, e, h, E=PO)
                m1 = cp(KM[:, sl], k32.ap, r, kfree, E=DV)
                l = tt(KL[:, sl], k32.ap, KM[:, sl], ALU.subtract, m1, kfree, E=PO)
                k32.free = [l]
                ktok.setdefault(g, []).append(l)
                yield

            def values(bb, c, ct, ld):
                for u in range(2):
                    b = PJ.take()
                    for t in range(2):
                        for k in range(2):
                            tk = u * 2 + t
                            x = mm(b.ap[:, t * 256:(t + 1) * 256], ct.ap[:, k, tk * 128:(tk + 1) * 128],
                                   W["v"][:, k, :], ld, b.free, W["tok"], start=k == 0, stop=k == 1)
                            if t * 2 + k < 3:
                                yield
                    bv = b.ap.rearrange("p (a m h c) -> p a m h c", a=2, m=2, h=8)
                    for m in range(2):
                        vb = vbuf[2 * bb + m]
                        at = c * 4 + u * 2
                        dst = V[vb][:, at:at + 2, 0:136].rearrange("p a (h c) -> p a h c", c=17)[:, :, :, 0:16]
                        e = cp(dst, bv[:, :, m], x, vfree[vb], vc[vb], E=AC)
                        vtok.setdefault(2 * bb + m, []).append(e)
                    b.free = [e]
                    if u == 0:
                        yield
                ct.free = ct.free + [x]
                yield

            def work(items):
                def load(it):
                    r = ctx_chunk(CT.take(), it[1] // 2 if it[0] is keys else it[1], it[2], CT.slots[CT.i - 1].free)
                    r[0].free = []
                    return r

                def run(nxt):
                    for n, it in enumerate(items):
                        cur = nxt
                        if n + 1 < len(items):
                            nxt = load(items[n + 1])
                        yield from it[0](it[1], it[2], *cur)

                return run(load(items[0]))

            def stack(s, part=None):
                g, hh = s // 8, s % 8
                ks = KS[s % 4]
                sl = slice(0, 4096) if part is None else slice(part * 2048, part * 2048 + 2048)
                kt = ktok[g] if part is None else ktok[g][part * 4:part * 4 + 4]
                d = []
                for j, pn in enumerate(ko):
                    d.append(Q.go(ks[16 * j:16 * j + 16, sl], kparts[pn][16 * hh:16 * hh + 16, sl], kt,
                                  kstfree[s % 4], kst[s % 4]))
                if not part:
                    d.append(Q.go(ks[99:100, :], scr[lay:lay + 1, (g // 2) * 4096:(g // 2) * 4096 + 4096], md[lay],
                                  kstfree[s % 4]))
                stk[s] = [d, d] if part is None else [d, None] if part == 0 else [stk[s][0], d]
                if hh == 7:
                    kfree[:] = d

            def where(s):
                g, hh = s // 8, s % 8
                return g, hh, g // 2, (g % 2) * 8 + hh

            state = {}

            def rowmax(s):
                g, hh, bb, h = where(s)
                ks = KS[s % 4]
                mt = mx[:, (s % 2) * 32:(s % 2) * 32 + 32]
                for c in range(8):
                    for q in range(2):
                        b = P1.take()
                        x = mm(b.ap, QS[0:100, h, bb * 256 + q * 128:bb * 256 + (q + 1) * 128],
                               ks[0:100, c * 512:(c + 1) * 512], stk[s][c // 4], qd, z2, b.free)
                        e = red(mt[:, q * 8 + c:q * 8 + c + 1], b.ap, ALU.max, x, mxfree[s % 2])
                        b.free = [e]
                        if q + 2 * c < 15:
                            yield
                state["p1"] = x
                nm = mxr[:, (s % 2) * 8:(s % 2) * 8 + 2]
                r1 = mxr[:, (s % 2) * 8 + 2:(s % 2) * 8 + 4]
                nb = mxb[:, (s % 2) * 8:(s % 2) * 8 + 8].rearrange("p (q c) -> p q c", c=4)
                a = red(nm, mt[:, 0:16].rearrange("p (a b) -> p a b", a=2), ALU.max, e, mxfree[s % 2], negate=True)
                h1 = cp(nb[:, :, 0], nm, a)
                r = tt(r1, nm, nb[:, :, 0], ALU.subtract, h1)
                h2 = cp(nb[:, :, 1], r1, r)
                h3 = tt(nb[:, :, 2], r1, nb[:, :, 1], ALU.subtract, h2)
                mtok[s] = (nb, [h1, h2, h3])
                yield

            def maxrow(s):
                g, hh, bb, h = where(s)
                nb, w = mtok[s]
                b = P1.take()
                bv = b.ap.bitcast(BF)
                for q in range(2):
                    PE.wait(w, b.free)
                    x = PE.done(nc.tensor.transpose(bv[96:99, q * 128:(q + 1) * 128], nb[:, q, 0:3], idb[:, :]))
                e = cp(QS[96:99, h, bb * 256:bb * 256 + 256], bv[96:99, 0:256], x, state["p1"])
                b.free = [e]
                mxfree[s % 2] = [x]
                state["mrow"] = e

            def finish(s, part):
                g, hh, bb, h = where(s)
                if part == 0:
                    pv = PV.take()
                    e = cp(pv.ap, PVB.ap[:, 0:256], state["pvt"], pv.free)
                    PVB.free = [e]
                    state["pvs"] = (pv, e)
                    return
                pv, e = state["pvs"]
                b = P1.take()
                for q in range(2):
                    x = tr(b.ap[:, q * 128:(q + 1) * 128], pv.ap[:, q * 128:(q + 1) * 128], idf[:, :], e, b.free)
                pv.free = [x]
                r_ = rd.take()
                sm_ = r_.ap[:, 0:34].rearrange("p (a b) -> p a b", a=2)
                e = red(sm_, b.ap[:, 0:256].rearrange("p (a j c) -> p a c j", a=2, j=4)[:, :, 0:17, :], ALU.add, x, r_.free)
                b.free = [e]
                r = rec(r_.ap[:, 34:36], sm_[:, :, 16], e)
                for q in range(2):
                    t = 2 * bb + q
                    if lay == 0:
                        e = stt(X[:, t, 16 * h:16 * h + 16], sm_[:, q, 0:16], r_.ap[:, 34 + q:35 + q],
                                X[:, t, 16 * h:16 * h + 16], ALU.mult, ALU.add, r)
                    else:
                        e = ts(XN[:, t, 16 * h:16 * h + 16], sm_[:, q, 0:16], r_.ap[:, 34 + q:35 + q], None,
                               ALU.mult, None, r)
                r_.free = [e]
                return e

            def drain(it):
                for _ in it:
                    pass

            def queries():
                xn_tok = prep()
                qt = []
                for m in range(2):
                    b, k = feat(W["q"], m * 128, 128, HT, 2, [xn_tok, W["qtok"]])
                    if lay == 0:
                        e = ts(q32[:, m, :], b.ap, W["qb"][:, m:m + 1], 0.25, ALU.add, ALU.mult, k, W["qtok"], start)
                    else:
                        for bb in range(2):
                            e = ts(q32[:, m, bb * 256:(bb + 1) * 256], b.ap[:, bb * 256:(bb + 1) * 256],
                                   anyk[:, bb:bb + 1], 0.25, ALU.mult, ALU.mult, k, flag["any"], start)
                    b.free = [e]
                    h = cp(qp[0][:, m, :], q32[:, m, :], e)
                    r = tt(qr[:, m, :], q32[:, m, :], qp[0][:, m, :], ALU.subtract, h)
                    l = cp(qp[1][:, m, :], qr[:, m, :], r)
                    l2 = tt(qp[2][:, m, :], qr[:, m, :], qp[1][:, m, :], ALU.subtract, l)
                    qt += [h, l, l2]
                sq_ = D["scrq"]
                qw = [Q.go(sq_[s].rearrange("(m p) t -> p m t", p=128), qp[s], qt, start) for s in range(3)]
                r = [Q.go(QS[16 * j:16 * j + 16, :, :], sq_[s].rearrange("(h p) t -> p h t", p=16), qw[s], start)
                     for j, s in enumerate((0, 1, 2, 0, 1, 0))]
                vconst(1, qw)
                return r

            NS = 32
            for c in range(8):
                drain(keys(0, c, *ch[c]))
                if c == QAT:
                    qd = queries()
                if c == 5:
                    stack(0, 0)
                if c > 0:
                    drain(values(0, c - 1, *ch[c - 1]))
                    n = len(ch)
                    if n < 8:
                        sl = slots[n % len(slots)]
                        ch.append(ctx_chunk(sl, 0, n, sl.free))
                        sl.free = []
            stack(0, 1)
            for s in range(1, 4):
                stack(s)
            A = rowmax(0)
            for _ in values(0, 7, *ch[7]):
                next(A, None)
            drain(A)
            A = rowmax(1)
            for n in range(8):
                next(A, None)
                if n == 3:
                    maxrow(0)
            B = iter(())
            PJ.slots, PJ.i = banks.slots[6:8], 0
            CT.i = 0
            extra = [iter(())] * 4
            prev = None
            for s in range(NS):
                g, hh, bb, h = where(s)
                if s == 17:
                    later([vfree[2], [m_.free for m_ in more]])
                if s == 7:
                    extra[1] = work([(values, 1, c) for c in range(5)] + [(keys, 2, c) for c in range(8)]
                                    + [(values, 1, c) for c in range(5, 8)])
                if hh == 4 and g in (0, 2):
                    extra[g] = work([(keys, g + 1, c) for c in range(8)])
                ks = KS[s % 4]
                V_ = V[vbuf[g]]
                mrow = state["mrow"]
                pend = []

                def flush(c, items):
                    for j in range(4):
                        pr, e = items[j // 2]
                        x = mm(PVB.ap[32 * j:32 * j + 32, 0:256], V_[:, c * 4 + j, 17 * hh:17 * hh + 32],
                               pr.ap[:, (j % 2) * 256:(j % 2) * 256 + 256], e, PVB.free, vtok[g], start=c == 0,
                               stop=c == 7, inc=(j == 3), cols=True)
                    for pr, e in items:
                        pr.free = [x]
                    state["pvt"] = x

                for i in range(16):
                    sT = ST.take()
                    for j in range(2):
                        kt = i * 2 + j
                        x = mm(sT.ap[:, j * 256:j * 256 + 256], ks[0:100, kt * 128:(kt + 1) * 128],
                               QS[0:100, h, bb * 256:bb * 256 + 256], mrow, sT.free)
                    pr = PR.take()
                    e = act(pr.ap, sT.ap, ACT.Exp, x, pr.free)
                    sT.free = [e]
                    lastS = x
                    pend.append((pr, e))
                    if i == 8 and s + 2 < NS:
                        B = rowmax(s + 2)
                    next(A if i < 8 else B, None)
                    if i == 11 and s + 1 < NS:
                        maxrow(s + 1)
                    if i == 0 and prev is not None:
                        finish(prev, 0)
                    if i == 2 and prev is not None:
                        finish(prev, 1)
                    if i % 2 == 1 and i >= 3:
                        flush((i - 3) // 2, [pend.pop(0), pend.pop(0)])
                    if g < 3 and ((hh == 4 and i >= 6) or (hh == 5 and i < 12 and i % 2 == 0)):
                        next(extra[g], None)
                    if g == 1 and ((hh < 4 and i % 8 < 5) or (hh > 5 and i % 4 < 3)):
                        next(extra[1], None)
                    if g < 3 and hh == 5 and i == 12:
                        while len(ktok.get(g + 1, [])) < 8:
                            next(extra[g])
                        stack(s + 3)
                A, B = B, iter(())
                flush(7, [pend.pop(0), pend.pop(0)])
                kstfree[s % 4] = [lastS]
                if hh == 7:
                    drain(extra[g])
                    vfree[vbuf[g]] = [state["pvt"]]
                if s + 4 < NS and hh != 4:
                    stack(s + 4)
                prev = s
            finish(prev, 0)
            return finish(prev, 1)

        W = load_l0x()
        def prep0():
            r = turn(XN, layernorm(X, 1e-5, xl), HT)
            flag["any"] = anykeys()
            return r

        def load_l0a(*w):
            r, tok = {}, []
            at = 0
            for n, kt, m in (("dq", 2, 128), ("dkv", 2, 128), ("uq", 1, 1024), ("uqs", 1, 1024), ("uk", 1, 1024),
                             ("uks", 1, 1024), ("uv", 1, 1024), ("o", 8, 256), ("C", 1, 512), ("S", 1, 512)):
                r[n], t = wload(WB, at, "L0a_" + n, kt, m, *w)
                at += kt * m
                tok.append(t)
            tok.append(col("L0a_g", 4, 2, *w)[1])
            tok.append(col("L0a_b", 6, 2, *w)[1])
            r["tok"] = tok
            return r

        vbt = WA[:, 1536:1792]
        late = {}

        def later0(w):
            late["a"] = load_l0a(w)
            late["vb"] = Q.go(vbt, D["L0x_vb"].rearrange("(a n) -> a n", a=1).to_broadcast([128, 256]))

        if "fake0" in D:
            e = Q.go(X[:, :, :], D["fake0"].rearrange("(t p) n -> p t n", p=128), now(), prep0())
            cp(XR0[:, :], X[:, 0, 0:1], e)
            later0([])
        else:
            e = crossattn(W, 0, prep0, later0, cs0, ch0)
            for t in range(NT):
                tt(X[:, t, :], X[:, t, :], vbt, ALU.add, e, late["vb"])
        WL0a = late["a"]
        s0 = now() + [late["vb"]]

        def dump(src):
            o = []
            for t in range(NT):
                o.append(Q.go(out.rearrange("(t p) n -> p t n", p=128)[:, t, :], src[:, t, :], *now()))
            SP.wait(*o)

        if stage == 1:
            dump(X)
            return

        for bk in banks.slots:
            bk.free = list(s0)

        WL0f = [wload(WA, 0, "L0f_w1", 2, 1024, s0), wload(WA, 2048, "L0f_w2", 8, 256, s0)]
        cv = sm[:, 16:48].rearrange("p (a b) -> p a b", a=8)
        WL0f.append((None, Q.go(cv, D["L0f_cv"].rearrange("(t p) n -> p t n", p=128), s0)))

        def heads64(k2, base):
            QZ = wview(WK, 0, 8192, (16, 512))
            return QZ

        QZ = wview(WK, 0, 8192, (16, 512))
        KT = wview(WK, 8192, 4096, (8, 512))
        VT = wview(WK, 12288, 4096, (4, 1024))
        OT = wview(WK, 16384, 4096, (8, 512))
        PP = [wview(WK, 20480 + 512 * i, 512) for i in range(4)]
        PN = [wview(WK, 22528 + 512 * i, 512) for i in range(4)]
        PTT = [wview(WK, 24576 + 512 * i, 512) for i in range(3)] + [wview(WK, 31744 + 512 * i, 512) for i in range(5)]
        TMP = Ring([wview(WK, 26112 + 512 * i, 512) for i in range(6)])
        CQ = wview(WK, 29184, 1024, (2, 512))
        XR = wview(WK, 30208, 1024, (4, 256))
        RS = wview(WK, 31232, 32)

        def zero_halves(w):
            a = fill(QZ[64:128, 0:16:2, :], 0.0, w, E=PO)
            b = fill(QZ[0:64, 1:16:2, :], 0.0, w, E=PO)
            return [a, b]

        zh = zero_halves(s0)
        ln = layernorm(X, 1e-5, s0)
        ln2 = layernorm(XN, 1e-5, ln, dst=XR)
        g_, b_ = sm[:, 4:6], sm[:, 6:8]
        W = WL0a

        def affine(g, bb, tok):
            def ev(f, src, dst, k):
                return ts(dst, src, g[:, f:f + 1], bb[:, f:f + 1], ALU.mult, ALU.add, k, tok)
            return ev

        ht = turn(XR, ln2, HT, affine(g_, b_, W["tok"]))
        cc = []
        for i, n in enumerate(("dq", "dkv")):
            b, k = feat(W[n], 0, 128, HT, 2, [ht, W["tok"]])
            e = cp(CQ[:, i, :], b.ap, k, E=(DV, AC)[i])
            b.free = [e]
            cc.append(e)

        def rope(n, ns, src, m, dsts, sc):
            b, k = feat(W[n], m * 128, 128, src, 1, cc)
            b2, k2 = feat(W[ns], m * 128, 128, src, 1, cc)
            u, v = TMP.take(), TMP.take()
            e1 = stt(u.ap, b.ap, sc, W["C"][:, 0, :], ALU.mult, ALU.mult, k, u.free, W["tok"])
            e2 = stt(v.ap, b2.ap, sc, W["S"][:, 0, :], ALU.mult, ALU.mult, k2, v.free)
            b.free, b2.free = [e1], [e2]
            o = [tt(d, u.ap[p0:p1, :], v.ap[p0:p1, :], ALU.add, e1, e2, E=PO) for d, p0, p1 in dsts]
            u.free = v.free = o
            return o

        qk = []
        for m in range(8):
            qk += rope("uq", "uqs", CQ[:, 0:1, :], m, [(QZ[0:64, 2 * m, :], 0, 64), (QZ[64:128, 2 * m + 1, :], 64, 128)], 0.125)
            qk += rope("uk", "uks", CQ[:, 1:2, :], m, [(KT[:, m, :], 0, 128)], 1.0)
        vt = []

        def vproj(lhs, kt, Wv, c0, toks, dst=None, n=1024):
            o = []
            for t in range(NT):
                for c in range(0, n, 512):
                    b, k = tokp(lhs, kt, t, Wv, c0 + c, 512, toks)
                    e = cp((VT if dst is None else dst)[:, t, c:c + 512], b.ap, k, E=AC)
                    b.free = [e]
                    o.append(e)
            return o

        vt = vproj(CQ[:, 1:2, :], 1, W["uv"], 0, cc)

        def attn64(nh, wts, mask, gate=None, gtok=None, OTv=None):
            OTv = OT if OTv is None else OTv
            units, held = [], {}
            for bb in range(2):
                for h in range(nh):
                    def pv(its, bb=bb, h=h):
                        b = banks.take()
                        for k in range(2):
                            for j, (pt, c) in enumerate(its):
                                hh = h - 1 + j
                                x = mm(b.ap[64 * j:64 * j + 64, 0:256], VT[:, bb * 2 + k, hh * 64:(hh + 1) * 64],
                                       pt.ap[:, k * 256:(k + 1) * 256], c, wts, b.free, start=k == 0, stop=k == 1, cols=True)
                        e = cp(OTv[:, h // 2, bb * 256:(bb + 1) * 256], b.ap[:, 0:256], x, E=AC)
                        b.free = [e]
                        held["o"] = e
                        return x
                    units.append(dict(q=QZ[:, h, bb * 256:(bb + 1) * 256], k=KT[:, h // 2, bb * 256:(bb + 1) * 256],
                                      w=wts, mask=mask, pv=pv,
                                      gate=None if gate is None else gate[:, 2 * bb:2 * bb + 2, h]))
            selfattn(units, 2, PP, PN, PTT, RS)
            return held["o"]

        w1, w2 = WL0f[0][0], WL0f[1][0]
        wt = [x[1] for x in WL0f]
        wst = sb("wst", [128, 64])

        def wquant(wap, n, at):
            flat = wap.rearrange("p a b -> p (a b)")
            DV.wait(*wt)
            a = DV.done(nc.vector.tensor_reduce(wst[:, at:at + 1], flat, AX, ALU.add, apply_absolute_value=True))
            b = banks.take()
            x = mm(b.ap[:, 0:1], onesf[:, :], wst[:, at:at + 1], a, b.free)
            e = ts(wst[:, at + 1:at + 2], b.ap[:, 0:1], 1.0 / n, 1e-5, ALU.mult, ALU.max, x)
            b.free = [e]
            r = rec(wst[:, at + 2:at + 3], wst[:, at + 1:at + 2], e)
            q = ts(flat, flat, wst[:, at + 2:at + 3], MAGIC, ALU.mult, ALU.add, r, E=PO)
            q = ts(flat, flat, MAGIC, -1.0, ALU.subtract, ALU.max, q, E=PO)
            q = ts(flat, flat, 1.0, None, ALU.min, None, q, E=PO)
            return q, wst[:, at + 1:at + 2]

        q1, sw1 = wquant(w1, 262144, 0)
        q2, sw2 = wquant(w2, 262144, 4)
        o = attn64(16, [qk[-1], vt[-1], zh], None)
        e = add_out(OT, 8, W["o"], [o], extra=[(XN[:, t, :], None) for t in range(NT)])
        s1 = now()
        if stage == 2:
            dump(X)
            return

        WL1x = load_l1x(s1)
        cs1 = ctx_slots(1)
        ch1 = [ctx_chunk(cs1[c], 0, c, s1) for c in range(3)]
        ln = layernorm(X, 1e-5, s1)
        WQ1 = w1
        WQ2 = wview(WK, 2048, 1024).bitcast(BF).rearrange("p (a b) -> p a b", a=8)
        XQ = wview(WK, 5120, 1024, (4, 256))
        HB = wview(WK, 6144, 4128).rearrange("p (m b t) -> p m b t", m=8, b=2)
        Y = Ring([wview(WK, 10272 + 512 * i, 512) for i in range(3)])
        YT = wview(WK, 11808, 4096, (8, 512))
        HK = wview(WK, 15904, 4096, (4, 1024))
        HQ = wview(WK, 20000, 2048).bitcast(BF).rearrange("p (t n) -> p t n", t=4)
        HQT = wview(WK, 22048, 2048).bitcast(BF).rearrange("p (m t) -> p m t", m=8)
        hq1 = wview(WK, 24096, 2048, (2, 1024))
        q2 = cp(WQ2.rearrange("p a b -> p (a b)"), w2.rearrange("p a b -> p (a b)"), q2, s1, E=AC)

        def aquant(src, t, n, dst, tmp, at, w, back):
            DV.wait(w)
            c = wst[:, at + 3 * t:at + 3 * t + 1]
            c1 = wst[:, at + 3 * t + 1:at + 3 * t + 2]
            c2 = wst[:, at + 3 * t + 2:at + 3 * t + 3]
            a = DV.done(nc.vector.tensor_reduce(c, src, AX, ALU.max, apply_absolute_value=True))
            a = ts(c, c, 1e-5, None, ALU.max, None, a)
            r = rec(c1, c, a)
            i1 = ts(c1, c1, 127.0, None, ALU.mult, None, r)
            i2 = ts(c2, c, 1.0 / 127.0, None, ALU.mult, None, a)
            q = ts(tmp, src, c1, MAGIC, ALU.mult, ALU.add, i1)
            q = ts(tmp, tmp, MAGIC, 127.0, ALU.subtract, ALU.min, q)
            if back:
                return ts(dst, tmp, -128.0, c2, ALU.max, ALU.mult, q, i2), c2
            return ts(dst, tmp, -128.0, None, ALU.max, None, q), c2

        xq = [aquant(XN[:, t, :], t, 256, XQ[:, t, :], hq1[:, 0, t * 256:(t + 1) * 256], 16, ln[t], True)[0] for t in range(NT)]
        ht = turn(XQ, xq, HT)
        z = [fill(HB[:, :, :, 0:1], 0.0, s1), fill(HB[:, :, :, 257:258], 0.0, s1)]
        yt = []
        for m in range(8):
            b, k = feat(WQ1, m * 128, 128, HT, 2, [ht, q1])
            e = act(HB[:, m, :, 1:257], b.ap.rearrange("p (b t) -> p b t", b=2), ACT.Copy, k, z, s1, scale=sw1)
            b.free = [e]
            y = Y.take()
            yv = y.ap.rearrange("p (b t) -> p b t", b=2)
            a = ts(yv, HB[:, m, :, 1:257], cv[:, m, 1:2], cv[:, m, 3:4], ALU.mult, ALU.add, e, y.free)
            a = stt(yv, HB[:, m, :, 0:256], cv[:, m, 0:1], yv, ALU.mult, ALU.add, a)
            a = stt(yv, HB[:, m, :, 2:258], cv[:, m, 2:3], yv, ALU.mult, ALU.add, a)
            e = act(YT[:, m, :], y.ap, ACT.Silu, a)
            y.free = [e]
            yt.append(e)
        hk = []
        for t in range(NT):
            hs = []
            for g in range(2):
                b = banks.take()
                for j in range(4):
                    m = g * 4 + j
                    k = tr(b.ap[:, j * 128:(j + 1) * 128], YT[:, m, t * 128:(t + 1) * 128], idf[:, :], yt[m], b.free)
                e = cp(HK[:, t, g * 512:(g + 1) * 512], b.ap, k, E=AC)
                b.free = [e]
                hs.append(e)
            hk.append(aquant(HK[:, t, :], t, 1024, HQ[:, t, :], hq1[:, t % 2, :], 32, hs, False))
        tq = []
        for m in range(8):
            b = banks.take()
            bv = b.ap.bitcast(BF)
            for t in range(NT):
                k = tr(bv[:, t * 128:(t + 1) * 128], HQ[:, t, m * 128:(m + 1) * 128], idb[:, :], hk[t][0], b.free)
            e = cp(HQT[:, m, :], bv[:, 0:512], k, E=AC)
            b.free = [e]
            tq.append(e)
        for t in range(NT):
            b, k = tokp(HQT, 8, t, WQ2, 0, 256, [tq, q2])
            a = ts(wst[:, 48 + t:49 + t], hk[t][1], sw2, None, ALU.mult, None, hk[t][0], q2)
            e = stt(X[:, t, :], b.ap[:, 0:256], wst[:, 48 + t:49 + t], X[:, t, :], ALU.mult, ALU.add, k, a)
            b.free = [e]
        s2 = now()
        if stage == 3:
            dump(X)
            return

        def load_l1a(*w):
            r, tok, at = {}, [], 0
            for n, kt, m in (("q", 2, 256), ("k", 2, 256), ("v", 2, 512), ("u", 4, 256)):
                r[n], t = wload(WA, at, "L1a_" + n, kt, m, *w)
                at += kt * m
                tok.append(t)
            r["bu"] = WA[:, at:at + 256]
            tok.append(Q.go(WA[:, at:at + 256], D["L1a_bu"].rearrange("(a n) -> a n", a=1).to_broadcast([128, 256]), *w))
            r["tok"] = tok
            return r

        def later1(w):
            late["l1a"] = load_l1a(s2)

        W = WL1x

        def prep1():
            return turn(XN, layernorm(X, 1e-5, s2), HT)

        if "fake1" in D:
            e = Q.go(X[:, :, :], D["fake1"].rearrange("(t p) n -> p t n", p=128), now(), prep1())
            cp(XR0[:, :], X[:, 0, 0:1], e)
            later1([])
        else:
            e = crossattn(W, 1, prep1, later1, cs1, ch1)
            s3 = now()
            for bk in banks.slots:
                bk.free = list(s3)
            ht = turn(XN, [e] * NT, HT)
            add_out(HT, 2, W["o"], [ht])
        WL1a = late["l1a"]
        s3 = now()
        if stage == 4:
            dump(X)
            return

        NE = 11
        exp_slots = Ring([WB[:, 768 * i:768 * (i + 1)] for i in range(NE)])
        exq = {}

        def load_expert(i, *w):
            s = exp_slots.take()
            g = s.ap[:, 0:256].rearrange("p (a b) -> p a b", a=2)
            u = s.ap[:, 256:512].rearrange("p (a b) -> p a b", a=2)
            d = s.ap[:, 512:768]
            tk = [Q.go(g, D["L1f_g"][i].rearrange("(t p) n -> p t n", p=128), s.free, *w),
                  Q.go(u, D["L1f_u"][i].rearrange("(t p) n -> p t n", p=128), s.free, *w),
                  Q.go(d, D["L1f_d"][i], s.free, *w)]
            exq[i] = (s, g, u, d, tk)

        for i in range(NE):
            load_expert(i, s3)
        ln = layernorm(X, 1e-5, s3)
        ht = turn(XN, ln, HT)
        KT2 = wview(WK, 8192, 1024, (2, 512))
        VT2 = wview(WK, 12288, 2048, (4, 512))
        OT2 = wview(WK, 16384, 2048, (4, 512))
        hmask = hm8

        def attn16(Wq, Wk, Wv, toks, sc, mask, qb=None, kb=None, vb=None):
            qk, vt = [], []
            for m in range(2):
                b, k = feat(Wq, m * 128, 128, HT, 2, toks)
                u = TMP.take()
                if qb is None:
                    e0 = ts(u.ap, b.ap, sc, None, ALU.mult, None, k, u.free)
                else:
                    e0 = ts(u.ap, b.ap, qb[:, m:m + 1], sc, ALU.add, ALU.mult, k, u.free)
                b.free = [e0]
                for j in range(8):
                    if j % 2:
                        e = ts(QZ[:, m * 8 + j, :], u.ap, hm8[:, j:j + 1], None, ALU.mult, None, e0, E=PO)
                    else:
                        e = act(QZ[:, m * 8 + j, :], u.ap, ACT.Copy, e0, scale=hm8[:, j:j + 1])
                    qk.append(e)
                u.free = qk[-2:]
                b, k = feat(Wk, m * 128, 128, HT, 2, toks)
                if kb is None:
                    e = cp(KT2[:, m, :], b.ap, k, E=DV)
                else:
                    e = ts(KT2[:, m, :], b.ap, kb[:, m:m + 1], None, ALU.add, None, k)
                b.free = [e]
                qk.append(e)
            for t in range(NT):
                b, k = tokp(HT, 2, t, Wv, 0, 512, toks)
                if vb is None:
                    e = cp(VT2[:, t, :], b.ap, k, E=AC)
                else:
                    e = tt(VT2[:, t, :], b.ap, vb, ALU.add, k)
                b.free = [e]
                vt.append(e)
            units, held = [], {}
            wts = qk + vt
            for bb in range(2):
                for h in range(16):
                    def pv(its, bb=bb, h=h):
                        b = banks.take()
                        for k in range(2):
                            for j, (pt, c) in enumerate(its):
                                hh = h - 3 + j
                                x = mm(b.ap[32 * j:32 * j + 32, 0:256], VT2[:, bb * 2 + k, hh * 32:(hh + 1) * 32],
                                       pt.ap[:, k * 256:(k + 1) * 256], c, wts, b.free, start=k == 0, stop=k == 1, cols=True)
                        e = cp(OT2[:, h // 4, bb * 256:(bb + 1) * 256], b.ap[:, 0:256], x, E=AC)
                        b.free = [e]
                        held["o"] = e
                        return x
                    units.append(dict(q=QZ[:, h, bb * 256:(bb + 1) * 256], k=KT2[:, h // 8, bb * 256:(bb + 1) * 256],
                                      w=wts, mask=mask, pv=pv, gate=None))
            selfattn(units, 4, PP, PN, PTT, RS)
            return held["o"]

        W = WL1a
        PO.wait(*s3)
        AC.wait(*s3)
        DV.wait(*s3)
        o = attn16(W["q"], W["k"], W["v"], [ht, W["tok"]], 1.0 / 16, None)
        add_out(OT2, 4, W["u"], [o], extra=[(W["bu"], W["tok"])] * NT)
        s4 = now()
        if stage == 5:
            dump(X)
            return

        gw, gt = wload(WA, 0, "L1f_gate", 2, 16, s4)
        gb = WA[:, 32:48]
        gt2 = Q.go(gb, D["L1f_gb"].rearrange("(a n) -> a n", a=1).to_broadcast([128, 16]), s4)
        ll = WA[:, 64:320].rearrange("p (a b) -> p a b", a=16)
        gt3 = Q.go(WA[:, 64:320], D["c_lower"], s4)
        DV.wait(*s4)
        AC.wait(*s4)
        PO.wait(*s4)
        ln = layernorm(X, 1e-5, s4)
        ht = turn(XN, ln, HT)
        G = wview(WK, 0, 64, (4, 16))
        Gr = wview(WK, 64, 64, (4, 16))
        gs = wview(WK, 128, 8)
        cmpA = wview(WK, 256, 256, (16, 16))
        cmpB = wview(WK, 512, 256, (16, 16))
        AT = Ring([wview(WK, 1024 + 512 * i, 512) for i in range(3)])
        SG = Ring([wview(WK, 3072 + 512 * i, 512) for i in range(3)])
        gtok = []
        for t in range(NT):
            b, k = tokp(HT, 2, t, gw, 0, 16, [ht, gt])
            g = G[:, t, :]
            e = tt(g, b.ap[:, 0:16], gb, ALU.add, k, gt2)
            b.free = [e]
            e = act(g, g, ACT.Sigmoid, e)
            gj = g.rearrange("p (a b) -> p a b", a=1).to_broadcast([128, 16, 16])
            gi = g.rearrange("p (a b) -> p a b", b=1).to_broadcast([128, 16, 16])
            c1 = tt(cmpA, gj, gi, ALU.is_equal, e)
            c2 = tt(cmpB, gj, gi, ALU.is_gt, e)
            c1 = tt(cmpA, cmpA, ll, ALU.mult, c1, gt3)
            c1 = tt(cmpA, cmpA, cmpB, ALU.add, c1, c2)
            r = red(Gr[:, t, :], cmpA, ALU.add, c1)
            r = stt(Gr[:, t, :], Gr[:, t, :], 2.0, g, ALU.is_lt, ALU.mult, r)
            e = red(gs[:, t:t + 1], Gr[:, t, :], ALU.add, r)
            e = rec(gs[:, t:t + 1], gs[:, t:t + 1], e)
            gtok.append(ts(g, Gr[:, t, :], gs[:, t:t + 1], None, ALU.mult, None, e))
        xa = [tt(X[:, t, :], X[:, t, :], XN[:, t, :], ALU.add, ln, E=PO) for t in range(NT)]
        def up(i):
            s, wg, wu, wd, tk = exq.pop(i)
            b, k = feat(wg, 0, 128, HT, 2, [ht, tk])
            b2, k2 = feat(wu, 0, 128, HT, 2, [ht, tk])
            sg, at = SG.take(), AT.take()
            e = act(sg.ap, b.ap, ACT.Silu, k, sg.free)
            b.free = [e]
            e = tt(at.ap, sg.ap, b2.ap, ALU.mult, e, k2, at.free)
            b2.free = [e]
            sg.free = [e]
            return i, s, wd, tk, at, e

        def down(i, s, wd, tk, at, e):
            for t in range(0, NT, 2):
                b = banks.take()
                for q in range(2):
                    x = mm(b.ap[:, q * 256:(q + 1) * 256], at.ap[:, (t + q) * 128:(t + q + 1) * 128], wd, e, tk, b.free)
                for q in range(2):
                    sc = 1.0 if i == 16 else G[:, t + q, i:i + 1]
                    xa[t + q] = stt(X[:, t + q, :], b.ap[:, q * 256:(q + 1) * 256], sc, X[:, t + q, :],
                                    ALU.mult, ALU.add, x, xa[t + q], gtok[t + q])
                b.free = [xa[t + 1]]
            at.free = [x]
            s.free = [x]
            if i + NE < 17:
                load_expert(i + NE)

        held_ = None
        for i in list(range(17)) + [None]:
            nxt_ = None if i is None else up(i)
            if held_ is not None:
                down(*held_)
            held_ = nxt_
        s5 = now()
        if stage == 6:
            dump(X)
            return

        def load_l2a(*w):
            r, tok, at = {}, [], 0
            for n, kt, m in (("q", 2, 1024), ("kv", 2, 2048), ("o", 8, 256), ("g", 2, 16)):
                r[n], t = wload(WB, at, "L2a_" + n, kt, m, *w)
                at += kt * m
                tok.append(t)
            tok.append(col("L2a_w", 8, 2, *w)[1])
            r["tok"] = tok
            return r

        WL2a = load_l2a(s5)
        for e_ in (DV, AC, PO):
            e_.wait(*s5)
        ln = layernorm(X, 1e-5, s5)
        ht = turn(XN, ln, HT)
        S = [wview(WK, 4096 * i, 4096) for i in range(4)]
        CT = Ring([wview(WK, 16384 + 1024 * i, 1024, (2, 512)) for i in range(3)])
        CN = Ring([wview(WK, 19456 + 2048 * i, 2048, (8, 256)) for i in range(3)])
        PT4 = Ring([wview(WK, 25600 + 512 * i, 512) for i in range(4)])
        mxs = wview(WK, 27648, 64)
        evs, exs = {}, {}

        def qkx(bb):
            ev = {0: [], 1: []}
            for c in range(8):
                ct = CT.take()
                src = D["ctxT"][:, bb * 4096 + c * 512:bb * 4096 + (c + 1) * 512].rearrange("(t p) n -> p t n", p=128)
                ld = Q.go(ct.ap, src, s5, ct.free)
                for q in range(2):
                    t = bb * 2 + q
                    b = banks.take()
                    for k in range(2):
                        x = mm(b.ap, HT[:, k, t * 128:(t + 1) * 128], ct.ap[:, k, :], ht, ld, b.free, start=k == 0, stop=k == 1)
                    m = red(mxs[:, t * 16 + c:t * 16 + c + 1], b.ap, ALU.max, x)
                    e = cp(S[t][:, c * 512:(c + 1) * 512], b.ap, m, E=AC)
                    b.free = [e, m]
                    ev[q] = [e, m]
                ct.free = [x]
            evs[bb] = ev

        def expx(bb):
            ev = evs[bb]
            ex = []
            for q in range(2):
                t = bb * 2 + q
                m = red(mxs[:, t * 16 + 8:t * 16 + 9], mxs[:, t * 16:t * 16 + 8], ALU.max, ev[q], negate=True)
                e = act(S[t], S[t], ACT.Exp, m, ev[q], bias=mxs[:, t * 16 + 8:t * 16 + 9], scale=1.0,
                        accum_out=mxs[:, t * 16 + 9:t * 16 + 10])
                ex.append(e)
            exs[bb] = ex

        qkx(0)
        expx(0)
        qkx(1)
        for bb in range(2):
            ex = exs[bb]
            acc = [banks.take(), banks.take()]
            pend = []

            def pvx(item):
                cn, ld, j0, pts = item
                for q in range(2):
                    pt, c = pts[q]
                    for j in range(4):
                        n = j0 + j
                        x = mm(acc[q].ap[:, 0:256], pt.ap[:, j * 128:(j + 1) * 128], cn.ap[:, n % 8, :], c, ld,
                               acc[q].free, start=n == 0, stop=n == 31, inc=j == 3)
                    pt.free = [x]
                cn.free = [x]
                return x
            TB = [bk for bk in banks.slots if bk not in acc]
            for g in range(8):
                if g % 2 == 0:
                    cn = CN.take()
                    r0 = bb * 4096 + g * 512
                    ld = Q.go(cn.ap, D["ctx"][r0:r0 + 1024, :].rearrange("(t p) n -> p t n", p=128), s5, cn.free)
                pts = []
                for q in range(2):
                    t = bb * 2 + q
                    b = TB[(g * 2 + q) % 6]
                    for j in range(4):
                        n = g * 4 + j
                        x = tr(b.ap[:, j * 128:(j + 1) * 128], S[t][:, n * 128:(n + 1) * 128], idf[:, :], ex[q], b.free)
                    pt = PT4.take()
                    c = cp(pt.ap, b.ap, x, pt.free, E=(DV, AC)[q])
                    b.free = [c]
                    pts.append((pt, c))
                pend.append((cn, ld, g * 4, pts))
                if len(pend) > 1:
                    x = pvx(pend.pop(0))
            x = pvx(pend.pop(0))
            for q in range(2):
                t = bb * 2 + q
                r = rec(mxs[:, t * 16 + 10:t * 16 + 11], mxs[:, t * 16 + 9:t * 16 + 10], ex[q])
                e = stt(X[:, t, :], acc[q].ap[:, 0:256], mxs[:, t * 16 + 10:t * 16 + 11], X[:, t, :], ALU.mult, ALU.add, x, r, ln)
                acc[q].free = [e]
            if bb == 0:
                expx(1)
        s6 = now()
        if stage == 7:
            dump(X)
            return

        def load_l2f(*w):
            r, tok = {}, []
            for i, n in enumerate("rkv"):
                r[n], t = wload(WA, 512 * i, "L2f_" + n, 2, 256, *w)
                tok.append(t)
            tok.append(col("L2f_mr", 48, 2, *w)[1])
            tok.append(col("L2f_mk", 50, 2, *w)[1])
            r["tok"] = tok
            return r

        WL2f = load_l2f(s6)
        for e_ in (DV, AC, PO):
            e_.wait(*s6)
        zh = zero_halves(s6)
        ln = layernorm(X, 1e-5, s6)
        W = WL2a
        a = []
        for t in range(NT):
            DV.wait(ln[t])
            a.append(DV.done(nc.vector.bn_stats(st[:, t, :], XN[:, t, :])))
        for t in range(NT):
            DV.wait(a[t])
            a[t] = DV.done(nc.vector.bn_aggr(mv[:, t, :], st[:, t, :]))
        e = tt(rs[:, :], mv[:, :, 0], mv[:, :, 0], ALU.mult, a[3])
        e = tt(rs[:, :], rs[:, :], mv[:, :, 1], ALU.add, e)
        e = rsqrt(rs[:, :], rs[:, :], float(np.finfo(np.float32).eps), ALU.add, e)
        xr = [ts(XR[:, t, :], XN[:, t, :], rs[:, t:t + 1], None, ALU.mult, None, e) for t in range(NT)]

        def scaled(f, src, dst, k):
            return ts(dst, src, sm[:, 8 + f:9 + f], None, ALU.mult, None, k, W["tok"])

        ht = turn(XR, xr, HT, scaled)
        qk = []
        for m in range(8):
            b, k = feat(W["q"], m * 128, 128, HT, 2, [ht, W["tok"]])
            qk.append(ts(QZ[0:64, 2 * m, :], b.ap[0:64, :], 0.125, None, ALU.mult, None, k))
            qk.append(ts(QZ[64:128, 2 * m + 1, :], b.ap[64:128, :], 0.125, None, ALU.mult, None, k))
            b.free = [qk[-1]]
            b, k = feat(W["kv"], m * 128, 128, HT, 2, [ht])
            qk.append(cp(KT[:, m, :], b.ap, k, E=AC))
            b.free = [qk[-1]]
        vt = vproj(HT, 2, W["kv"], 1024, [ht])
        gate = wview(WK, 31264, 64, (4, 16))
        ge = None
        for t in range(NT):
            b, k = tokp(HT, 2, t, W["g"], 0, 16, [ht])
            ge = act(gate[:, t, :], b.ap[:, 0:16], ACT.Sigmoid, k)
            b.free = [ge]
        o = attn64(16, [qk, vt, ge, zh], 0, gate=gate)
        add_out(OT, 8, W["o"], [o])
        s7 = now()
        if stage == 8:
            dump(X)
            return

        def load_l3x(*w):
            r, tok = {}, []
            for i, n in enumerate("qkvp"):
                r[n], t = wload(WB, 512 * i, "L3x_" + n, 2, 256, *w)
                tok.append(t)
            r["ff"] = sm[:, 52:53]
            tok.append(Q.go(sm[:, 52:53], D["L3x_ff"].rearrange("(a n) -> a n", a=1).to_broadcast([128, 1]), *w))
            r["tok"] = tok
            return r

        WL3x = load_l3x(s7)
        for e_ in (DV, AC, PO):
            e_.wait(*s7)
        W = WL2f
        ln = layernorm(X, 1e-5, s7)
        ht = turn(XN, ln, HT)
        XRK = [wview(WK, 1024 * i, 1024, (2, 512)) for i in range(2)]
        XD = wview(WK, 2048, 1024, (2, 512))
        KA = wview(WK, 3072, 1024, (2, 512))
        RR = wview(WK, 4096, 1024, (4, 256))
        d = []
        for f in range(2):
            hv = HT[:, f, :].rearrange("p (b t) -> p b t", b=2)
            dv = XD[:, f, :].rearrange("p (b t) -> p b t", b=2)
            e = tt(dv[:, :, 1:256], hv[:, :, 1:256], hv[:, :, 0:255], ALU.subtract, ht)
            e2 = cp(dv[:, :, 0:1], hv[:, :, 0:1], ht)
            for i in range(2):
                pv_ = XRK[i][:, f, :].rearrange("p (b t) -> p b t", b=2)
                mu = sm[:, 48 + 2 * i + f:49 + 2 * i + f]
                e3 = ts(rs[:, 0:1], mu, -1.0, 1.0, ALU.mult, ALU.add, W["tok"], now())
                e4 = ts(pv_, hv, mu, None, ALU.mult, None, e3)
                e5 = stt(pv_[:, :, 1:256], hv[:, :, 0:255], rs[:, 0:1], pv_[:, :, 1:256], ALU.mult, ALU.add, e3, e4)
                d.append(e5)
        ka = []
        for m in range(2):
            b, k = feat(W["k"], m * 128, 128, XRK[1], 2, [d, W["tok"]])
            e = ts(KA[:, m, :], b.ap, 0.0, None, ALU.max, None, k)
            b.free = [e]
            ka.append(tt(KA[:, m, :], KA[:, m, :], KA[:, m, :], ALU.mult, e))
        for t in range(NT):
            b, k = tokp(XRK[0], 2, t, W["r"], 0, 256, [d])
            e = act(RR[:, t, :], b.ap[:, 0:256], ACT.Sigmoid, k)
            b.free = [e]
            b, k = tokp(KA, 2, t, W["v"], 0, 256, [ka])
            e = tt(RR[:, t, :], b.ap[:, 0:256], RR[:, t, :], ALU.mult, e, k)
            b.free = [e]
            e = tt(X[:, t, :], X[:, t, :], RR[:, t, :], ALU.add, e)
        s8 = now()
        if stage == 9:
            dump(X)
            return

        def load_l3a(*w):
            r, tok, at = {}, [], 0
            for n, kt, m in (("q", 2, 256), ("k", 2, 256), ("v", 2, 512), ("o", 4, 256)):
                r[n], t = wload(WA, at, "L3a_" + n, kt, m, *w)
                at += kt * m
                tok.append(t)
            r["vb"] = WA[:, at:at + 512]
            tok.append(Q.go(r["vb"], D["L3a_vb"].rearrange("(a n) -> a n", a=1).to_broadcast([128, 512]), *w))
            r["ob"] = WA[:, at + 512:at + 768]
            tok.append(Q.go(r["ob"], D["L3a_ob"].rearrange("(a n) -> a n", a=1).to_broadcast([128, 256]), *w))
            tok.append(col("L3a_qb", 54, 2, *w)[1])
            tok.append(col("L3a_kb", 56, 2, *w)[1])
            r["tok"] = tok
            return r

        WL3a = load_l3a(s8)
        for e_ in (DV, AC, PO):
            e_.wait(*s8)
        W = WL3x
        ln = layernorm(X, 1e-5, s8)
        ht = turn(XN, ln, HT)
        NB = 4
        o_ = 0

        def part(n):
            nonlocal o_
            v = WK[:, o_:o_ + n]
            o_ += n
            return v

        CT = Ring([part(1024).rearrange("p (a b) -> p a b", a=2) for _ in range(3)])
        AXR = Ring([part(NB * 256).rearrange("p (a b) -> p a b", a=NB) for _ in range(2)])
        NPR = Ring([part(NB * 304).rearrange("p (a h c) -> p a h c", a=NB, h=16) for _ in range(2)])
        RPR = Ring([part(NB * 304).rearrange("p (a h c) -> p a h c", a=NB, h=16) for _ in range(2)])
        M8R = Ring([part(NB * 128).rearrange("p (a h c) -> p a h c", a=NB, h=16) for _ in range(2)])
        KHR = Ring([part(NB * 256).rearrange("p (a b) -> p a b", a=NB) for _ in range(2)])
        CNR = Ring([part(NB * 260).rearrange("p (a b) -> p a b", a=NB) for _ in range(4)])
        stR = Ring([part(32) for _ in range(5)])
        QH = part(1024).rearrange("p (a b) -> p a b", a=4)
        QHT = part(1024).rearrange("p (a b) -> p a b", a=2)
        GS = part(2 * 2 * 260).rearrange("p (b c n) -> p b c n", b=2, c=2)
        GTs = part(1024).rearrange("p (b f c) -> p b f c", b=2, f=2)
        KV = part(2 * 2 * 272).rearrange("p (b c n) -> p b c n", b=2, c=2)
        YY = part(1024).rearrange("p (a b) -> p a b", a=4)
        YYT = part(1024).rearrange("p (a b) -> p a b", a=2)
        epsc = part(1)
        t_eps = fill(epsc, 1e-6, s8)
        hm16 = part(32).rearrange("p (a b) -> p a b", a=2)
        t_hm = Q.go(hm16, D["c_hm16"].rearrange("(t p) n -> p t n", p=128), s8)
        assert o_ + 64 <= WKN, o_
        pad = []
        for s in NPR.slots:
            pad.append(fill(s.ap[:, :, :, 16:19], 5.0, s8))
        for s in CNR.slots:
            pad.append(fill(s.ap[:, :, 256:257], 1.0, s8))
        focR = Ring([PS[:, i, :] for i in range(4)])
        GB = [Slot(PS[:, 4 + i, :]) for i in range(2)]
        for s in focR.slots + GB:
            s.free = list(s8) + [PE.last(), DV.last(), AC.last()]

        def focus(lhs_of, Wm, wtok, dst):
            ax, npr, rpr, m8, sts = AXR.take(), NPR.take(), RPR.take(), M8R.take(), stR.take()
            axw, sw = ax.free, sts.free
            sv = sts.ap
            e1, bk2 = [], []
            for i in range(NB):
                if i % 2 == 0:
                    b = focR.take()
                    bk2.append(b)
                lhs, lt = lhs_of(i)
                for k in range(2):
                    x = mm(b.ap[:, (i % 2) * 256:(i % 2) * 256 + 256], lhs[k], Wm[:, k, 0:256], lt, wtok, b.free,
                           start=k == 0, stop=k == 1)
                if i % 2 == 1:
                    y0 = act(ax.ap[:, i - 1:i + 1, :].rearrange("p a b -> p (a b)"), b.ap, ACT.Copy, x, axw, scale=-0.01)
                    b.free = [y0]
            for j in range(NB):
                b = bk2[j // 2]
                e = stt(ax.ap[:, j, :], ax.ap[:, j, :], 1.0, b.ap[:, (j % 2) * 256:(j % 2) * 256 + 256],
                        ALU.mult, ALU.max, b.free, y0, sw, accum_out=sv[:, j:j + 1])
                e1.append(e)
                if j % 2 == 1:
                    b.free = [e]
            yield
            axf = ax.ap.rearrange("p a b -> p (a b)")
            l = act(axf, axf, ACT.Ln, e1, t_eps, bias=epsc[:, 0:1], scale=1.0)
            z = ts(axf, axf, W["ff"], None, ALU.mult, None, l, W["tok"])
            m = red(sv[:, 4:8], ax.ap, ALU.max, z, negate=True)
            yield
            e2 = []
            for i in range(NB):
                e2.append(act(ax.ap[:, i, :], ax.ap[:, i, :], ACT.Exp, m, bias=sv[:, 4 + i:5 + i], scale=1.0,
                              accum_out=sv[:, 8 + i:9 + i]))
            for i in range(NB):
                src = ax.ap[:, i, :].rearrange("p (h c) -> p h c", c=16)[:, :, ::-1]
                en = act(npr.ap[:, i, :, 0:16], src, ACT.Copy, e2[i], npr.free, pad, scale=-1.0)
            ax.free = [en]
            yield
            n1 = ts(sv[:, 12:16], sv[:, 0:4], 1.0 / 256, 1e-6, ALU.mult, ALU.add, e1[-1])
            r1 = rec(sv[:, 16:20], sv[:, 8:12], e2[-1])
            f = stt(sv[:, 20:24], sv[:, 12:16], -1.0, sv[:, 16:20], ALU.mult, ALU.mult, n1, r1)
            for i in range(NB):
                DV.wait(en, m8.free)
                for h in range(16):
                    x = DV.done(nc.vector.max(m8.ap[:, i, h, :], npr.ap[:, i, h, :]))
            yield
            qs = []
            for i in range(NB):
                DV.wait(x, rpr.free)
                for h in range(16):
                    q = DV.done(nc.vector.match_replace(rpr.ap[:, i, h, :], m8.ap[:, i, h, :], npr.ap[:, i, h, :], 0.0))
                qs.append(q)
            m8.free = [q]
            npr.free = [q]
            yield
            toks = []
            for i in range(NB):
                d_, dfree = dst(i)
                AC.wait(qs[i], f, dfree)
                o = act(d_.rearrange("p (h c) -> p h c", c=16), rpr.ap[:, i, :, 0:16][:, :, ::-1], ACT.Copy,
                        scale=sv[:, 20 + i:21 + i])
                toks.append(o)
            rpr.free = [o]
            sts.free = [o]
            yield toks

        gts, pend = [], []

        def gram(item):
            kh, cn, ld, toks, bb, g = item
            for i in range(NB):
                n = g * NB + i
                for c in range(2):
                    x = mm(GB[c].ap[:, 0:257], kh.ap[:, i, c * 128:(c + 1) * 128], cn.ap[:, i, 0:257], toks[i], ld,
                           GB[c].free, start=n == 0, stop=n == 31, inc=True)
            kh.free = [x]
            cn.free = [x]
            if g == 7:
                for c in range(2):
                    e = cp(GS[:, bb, c, 0:257], GB[c].ap[:, 0:257], x, E=AC)
                    GB[c].free = [e]
                    gts.append(e)

        def unit(u):
            if u == 0:
                f = focus(lambda i: ([HT[:, k, i * 128:(i + 1) * 128] for k in range(2)], ht), W["q"], W["tok"],
                          lambda i: (QH[:, i, :], None))
                next(f)
                return f, None
            bb, g = (u - 1) // 8, (u - 1) % 8
            ct = CT.take()
            src = D["ctxT"][:, bb * 4096 + g * 512:bb * 4096 + (g + 1) * 512].rearrange("(t p) n -> p t n", p=128)
            ld = Q.go(ct.ap, src, s8, ct.free)
            cn = CNR.take()
            r0 = bb * 4096 + g * 512
            ld2 = Q.go(cn.ap[:, :, 0:256], D["ctx"][r0:r0 + 512, :].rearrange("(t p) n -> p t n", p=128), s8, cn.free)
            kh = KHR.take()
            f = focus(lambda i: ([ct.ap[:, k, i * 128:(i + 1) * 128] for k in range(2)], ld), W["k"], W["tok"],
                      lambda i: (kh.ap[:, i, :], kh.free))
            next(f)
            ct.free = [PE.last()]
            return f, (kh, cn, [ld2, pad], bb, g)

        live = {}
        for u in range(17 + 4):
            if pend:
                gram(pend.pop(0))
            if u < 17:
                live[u] = unit(u)
            if 0 <= u - 3 < 17:
                f, rest = live.pop(u - 3)
                toks = next(f)
                if rest is None:
                    qh = toks
                else:
                    kh, cn, lds, bb, g = rest
                    pend.append((kh, cn, lds, toks, bb, g))
            if 0 <= u - 2 < 17:
                next(live[u - 2][0])
            if u < 17:
                next(live[u][0])
            if 0 <= u - 1 < 17:
                next(live[u - 1][0])
            if 0 <= u - 2 < 17:
                next(live[u - 2][0])
        while pend:
            gram(pend.pop(0))
        SB = [Slot(PS[:, 6 + i, :]) for i in range(2)]
        for s in SB:
            s.free = list(s8) + [PE.last(), DV.last(), AC.last()]
        qht = []
        for f in range(2):
            b = SB[f]
            for t in range(NT):
                k = tr(b.ap[:, t * 128:(t + 1) * 128], QH[:, t, f * 128:(f + 1) * 128], idf[:, :], qh[t], b.free)
            e = cp(QHT[:, f, :], b.ap, k)
            b.free = [e]
            qht.append(e)
        s8b = now()
        for bk in banks.slots:
            bk.free = list(s8b)
        yv_ = []
        for bb in range(2):
            gt = []
            for f in range(2):
                b = banks.take()
                for c in range(2):
                    k = tr(b.ap[:, c * 128:(c + 1) * 128], GS[:, bb, c, f * 128:(f + 1) * 128], idf[:, :], gts, b.free)
                e = cp(GTs[:, bb, f, :], b.ap[:, 0:256], k)
                b.free = [e]
                gt.append(e)
            kv = []
            for c in range(2):
                b = banks.take()
                for f in range(2):
                    x = mm(b.ap[:, 0:256], GTs[:, bb, f, c * 128:(c + 1) * 128], W["v"][:, f, :], gt, b.free,
                           start=f == 0, stop=f == 1)
                e = stt(KV[:, bb, c, 0:256], b.ap[:, 0:256], 1.0 / 256, bmask[:, c, :], ALU.mult, ALU.mult, x)
                b.free = [e]
                e2 = ts(KV[:, bb, c, 256:272], hm16[:, c, :], GS[:, bb, c, 256:257], 1.0 / 4096, ALU.mult, ALU.mult, t_hm, gts)
                kv += [e, e2]
            for q in range(2):
                t = bb * 2 + q
                b, x = tokp(QHT, 2, t, KV[:, bb, :, :], 0, 272, [kv, qht])
                z = YY[:, t, :]
                zi = mv_ = WK[:, o_ + 16 * t:o_ + 16 * t + 16]
                e = ts(zi, b.ap[:, 256:272], 1e-6, None, ALU.add, None, x)
                e = rec(zi, zi, e)
                e = tt(z.rearrange("p (h c) -> p h c", c=16), b.ap[:, 0:256].rearrange("p (h c) -> p h c", c=16),
                       zi.rearrange("p (h c) -> p h c", c=1).to_broadcast([128, 16, 16]), ALU.mult, e)
                b.free = [e]
                yv_.append(e)
        yt = turn(YY, yv_, YYT)
        add_out(YYT, 2, W["p"], [yt])
        s9 = now()
        if stage == 10:
            dump(X)
            return

        def load_l3f(l, t_, w):
            r, tok, at = {}, [], 0
            for n, kt, m in (("qkv", 2, 1536), ("o", 4, 256), ("w2", 6, 256)):
                r[n], t = wload(t_, at, f"L3f_{n}{l}", kt, m, w)
                at += kt * m
                tok.append(t)
            return r, tok, at

        WL3f, tk3, at3 = load_l3f(0, WB, s9)
        WL3f["w1"], t = wload(WB, at3, "L3f_w10", 2, 1536, s9)
        tk3.append(t)
        for e_ in (DV, AC, PO):
            e_.wait(*s9)
        W = WL3a
        ln = layernorm(X, 1e-5, s9)
        ht = turn(XN, ln, HT)
        o = attn16(W["q"], W["k"], W["v"], [ht, W["tok"]], 1.0 / 16, 1, qb=sm[:, 54:56], kb=sm[:, 56:58], vb=W["vb"])
        add_out(OT2, 4, W["o"], [o], extra=[(W["ob"], W["tok"])] * NT)
        s10 = now()
        if stage == 11:
            dump(X)
            return

        for e_ in (DV, AC, PO):
            e_.wait(*s10)
        ln = layernorm(X, 1e-5, s10)
        XL = XN
        xtok = ln
        tab = wview(WA, 0, 1024, (4, 256))
        ttab = Q.go(tab, D["L3f_tab"].rearrange("(t p) n -> p t n", p=128), s10)
        zrow = WA[:, 1024:1152]
        tz = fill(zrow, 0.0, s10)
        QT_ = wview(WK, 26112, 0) if False else None
        QN = wview(WK, 20480, 2048, (4, 512))
        QN2 = wview(WK, 22528, 2048, (4, 512))
        sq = Ring([wview(WK, 24576 + 512 * i, 512) for i in range(8)])
        XS = wview(WK, 30208, 1024, (4, 256))
        OT3 = wview(WK, 16384, 2048, (4, 512))
        for l in range(2):
            W = WL3f
            sl = now()
            for e_ in (DV, AC, PO):
                e_.wait(*sl)
            wx = [xtok, sl]
            small = [Q.go(WA[:, 1152 + 64 * i:1216 + 64 * i],
                          D[n][l:l + 1, :].to_broadcast([128, 64]), sl)
                     for i, n in enumerate(("L3f_qs", "L3f_ks"))]
            small.append(Q.go(WA[:, 1280:1536], D["L3f_b2"][l:l + 1, :].to_broadcast([128, 256]), sl))
            small.append(Q.go(sm[:, 64:76], D["L3f_b1"][l], sl))
            small.append(Q.go(sm[:, 76:78], D["L3f_lg"][l], sl))
            small.append(Q.go(sm[:, 78:80], D["L3f_lb"][l], sl))
            zh = zero_halves(sl)
            zz = fill(HT[:, 1, :].rearrange("p (b t) -> p b t", b=2)[:, :, 0:1], 0.0, sl)

            def shifted(f, src, dst, k):
                if f == 0:
                    return cp(dst, src, k)
                sv = src.rearrange("p (b t) -> p b t", b=2)
                dv = dst.rearrange("p (b t) -> p b t", b=2)
                return cp(dv[:, :, 1:256], sv[:, :, 0:255], k, zz)

            ht = turn(XL, [xtok] * NT, HT, shifted)
            fin = []
            RN = wview(WK, 31300, 64, (8, 8))
            pb, er, eq = [], [], []
            for n in range(8):
                which, t = n // 4, n % 4
                b, k = tokp(HT, 2, t, W["qkv"], 512 * which, 512, [ht, zz, tk3])
                s = sq.take()
                e = act(s.ap, b.ap, ACT.Square, k, s.free, sl)
                e = red(RN[:, n, :], s.ap.rearrange("p (h d) -> p h d", d=64), ALU.add, e, sl)
                s.free = [e]
                pb.append((b, k))
                er.append(e)
            en = rsqrt(RN[:, :, :], RN[:, :, :], 1e-24, ALU.max, er[-1])
            for n in range(8):
                which, t = n // 4, n % 4
                QQ = (QN, QN2)[which]
                b, k = pb[n]
                q3 = QQ[:, t, :].rearrange("p (h d) -> p h d", d=64)
                e = tt(q3, b.ap.rearrange("p (h d) -> p h d", d=64),
                       RN[:, n, :].rearrange("p (h d) -> p h d", d=1).to_broadcast([128, 8, 64]), ALU.mult, en, er[n])
                b.free = [e]
                eq.append(e)
            ep, ec = [], []
            for n in range(8):
                which, t = n // 4, n % 4
                q3 = (QN, QN2)[which][:, t, :].rearrange("p (h d) -> p h d", d=64)
                s_ = WA[:, 1152 + 64 * which:1216 + 64 * which]
                e = tt(q3, q3, s_.rearrange("p (h d) -> p h d", h=1).to_broadcast([128, 8, 64]), ALU.mult, eq[n], small)
                s = sq.take()
                s3 = s.ap.rearrange("p (h d) -> p h d", d=64)
                Sb = tab[:, t, 64 + 128 * which:128 + 128 * which].rearrange("p (h d) -> p h d", h=1)
                PE_ = PO if n % 2 else DV
                e2 = tt(s3[:, :, 0:32], q3[:, :, 32:64], Sb[:, :, 0:32].to_broadcast([128, 8, 32]), ALU.mult, e, s.free, ttab, E=PE_)
                e3 = tt(s3[:, :, 32:64], q3[:, :, 0:32], Sb[:, :, 32:64].to_broadcast([128, 8, 32]), ALU.mult, e, E=PE_)
                ep.append((s, [e2, e3], e))
            for n in range(8):
                which, t = n // 4, n % 4
                q3 = (QN, QN2)[which][:, t, :].rearrange("p (h d) -> p h d", d=64)
                C = tab[:, t, 128 * which:64 + 128 * which]
                ec.append(tt(q3, q3, C.rearrange("p (h d) -> p h d", h=1).to_broadcast([128, 8, 64]), ALU.mult, ep[n][1], ttab))
            ef = []
            for n in range(8):
                which, t = n // 4, n % 4
                QQ = (QN, QN2)[which]
                s = ep[n][0]
                e = tt(QQ[:, t, :], QQ[:, t, :], s.ap, ALU.add, ec[n])
                s.free = [e]
                ef.append(e)
            for which in range(2):
                QQ, qq = (QN, QN2)[which], ef[4 * which:4 * which + 4]
                for m in range(4):
                    b = banks.take()
                    for t in range(NT):
                        k = tr(b.ap[:, t * 128:(t + 1) * 128], QQ[:, t, m * 128:(m + 1) * 128], idf[:, :], qq[t], b.free)
                    if which == 0:
                        e = cp(QZ[0:64, 2 * m, :], b.ap[0:64, :], k, zh, E=DV)
                        e2 = cp(QZ[64:128, 2 * m + 1, :], b.ap[64:128, :], k, zh, E=AC)
                        b.free = [e, e2]
                        fin += [e, e2]
                    else:
                        e = cp(KT[:, m, :], b.ap, k, E=AC)
                        b.free = [e]
                        fin.append(e)
            vt = vproj(HT, 2, W["qkv"], 1024, [ht, zz, tk3], n=512)
            o = attn64(8, [fin, vt, zh, now()], 2, OTv=OT3)
            e = add_out(OT3, 4, W["o"], [o], dst=XL)
            sh = []
            for t in range(NT):
                sh.append(Q.go(XS[1:128, t, 128:256], XL[0:127, t, 128:256], e))
                if t % 2 == 0:
                    sh.append(Q.go(XS[0:1, t, 128:256], zrow[0:1, 0:128], tz, e))
                else:
                    sh.append(Q.go(XS[0:1, t, 128:256], XL[127:128, t - 1, 128:256], e))
                sh.append(cp(XS[:, t, 0:128], XL[:, t, 0:128], e, E=PO))
            ln = layernorm(XS, 1e-5, sh, dst=XS)
            ht = turn(XS, ln, HT, affine(sm[:, 76:78], sm[:, 78:80], small))
            if l == 0:
                sw = now()
                nxt, tkn = {}, []
                for n, kt, m, at in (("qkv", 2, 1536, 0), ("o", 4, 256, 3072)):
                    nxt[n], t = wload(WB, at, f"L3f_{n}1", kt, m, sw)
                    tkn.append(t)
            AG = wview(WK, 0, 3072, (6, 512))
            GG = Ring([wview(WK, 3072 + 512 * i, 512) for i in range(3)])
            sA = now()
            ag = []
            for m in range(6):
                b, k = feat(W["w1"], m * 128, 128, HT, 2, [ht, tk3])
                b2, k2 = feat(W["w1"], 768 + m * 128, 128, HT, 2, [ht])
                g = GG.take()
                e = act(g.ap, b2.ap, ACT.Gelu, k2, small, g.free, sA, bias=sm[:, 70 + m:71 + m], scale=1.0)
                b2.free = [e]
                e = stt(AG[:, m, :], b.ap, sm[:, 64 + m:65 + m], g.ap, ALU.add, ALU.mult, e, k, small)
                b.free = [e]
                g.free = [e]
                ag.append(e)
            e = add_out(AG, 6, W["w2"] if l == 0 else W["w2"], [ag], extra=[(WA[:, 1280:1536], small)] * NT, dst=XL)
            xtok = e
            if l == 0:
                sw = now()
                nxt["w1"], t = wload(WB, 5632, "L3f_w11", 2, 1536, sw)
                nxt["w2"], t2 = wload(WB, 4096, "L3f_w21", 6, 256, sw)
                WL3f = nxt
                tk3 = tkn + [t, t2]
        for t in range(NT):
            e = tt(X[:, t, :], X[:, t, :], XL[:, t, :], ALU.add, xtok)
        dump(X)


def host_arrays(v):
    f = np.float32

    def T(a):
        return np.ascontiguousarray(np.asarray(a).T)

    def C(a):
        return np.ascontiguousarray(np.asarray(a))

    def headpad(a, n=16, hd=16, to=32):
        a = np.asarray(a)
        o = np.zeros(a.shape[:-1] + (n, to), a.dtype)
        o[..., :hd] = a.reshape(a.shape[:-1] + (n, hd))
        return np.ascontiguousarray(o.reshape(a.shape[:-1] + (n * to,)))

    A = {}
    A["x"] = C(v["x"]).reshape(512, 256)
    ctx = C(v["ctx_1024"]).reshape(8192, 256)
    A["ctx"] = ctx
    A["ctxT"] = T(ctx)
    A["mask_BxS2_ik0"] = C(v["mask_BxS2_ik0"])
    for n in "qkv":
        A["L0x_" + n] = T(v[f"L0_xattn_{n}_w"])
    A["L0x_qb"] = C(v["L0_xattn_q_b"])
    A["L0x_kb"] = C(v["L0_xattn_k_b"])
    A["L0x_vb"] = C(v["L0_xattn_v_b"])
    A["L0a_dq"], A["L0a_dkv"] = T(v["L0_attn_w_down_q"]), T(v["L0_attn_w_down_kv"])
    swap = np.arange(1024) ^ 1
    for n, w in (("uq", "q"), ("uk", "k"), ("uv", "v")):
        A["L0a_" + n] = T(v["L0_attn_w_up_" + w])
    A["L0a_uqs"] = C(T(v["L0_attn_w_up_q"])[:, swap])
    A["L0a_uks"] = C(T(v["L0_attn_w_up_k"])[:, swap])
    A["L0a_o"] = T(v["L0_attn_w_out"])
    A["L0a_g"], A["L0a_b"] = C(v["L0_attn_ln_scale"]), C(v["L0_attn_ln_bias"])
    inv = 1.0 / 10000.0 ** (np.arange(0, 64, 2, dtype=f) / 64)
    fr = np.outer(np.arange(256, dtype=f), inv)
    cos = np.concatenate([np.cos(fr), np.cos(fr)], -1)[:, ::2]
    sin = np.concatenate([np.sin(fr), np.sin(fr)], -1)[:, ::2]
    ct = np.repeat(cos.T, 2, axis=0)
    sg = np.where(np.arange(64) % 2 == 0, -1.0, 1.0).astype(f)
    stb = np.repeat(sin.T, 2, axis=0) * sg[:, None]
    A["L0a_C"] = np.tile(ct, (2, 2)).astype(f)
    A["L0a_S"] = np.tile(stb, (2, 2)).astype(f)
    A["L0f_w1"] = T(v["L0_ffn_w1"])
    A["L0f_w2"] = T(v["L0_ffn_w2"])
    A["L0f_cv"] = C(np.concatenate([np.asarray(v["L0_ffn_conv_w"]).reshape(1024, 3), np.asarray(v["L0_ffn_conv_b"])[:, None]], 1))
    for n in "qkvo":
        A["L1x_" + n] = C(v["L1_xattn_W" + n])
    A["L1a_q"], A["L1a_k"] = T(v["L1_attn_Wq"]), T(v["L1_attn_Wk"])
    A["L1a_v"] = headpad(T(v["L1_attn_Wv"]))
    A["L1a_u"] = T(headpad(v["L1_attn_Wu"]))
    A["L1a_bu"] = C(v["L1_attn_bu"])
    A["L1f_gate"], A["L1f_gb"] = C(v["L1_ffn_gate_w"]), C(v["L1_ffn_gate_b"])
    for n, a, b in (("g", "wg", "shared_wg"), ("u", "wu", "shared_wu"), ("d", "wd", "shared_wd")):
        A["L1f_" + n] = np.concatenate([np.asarray(v["L1_ffn_experts_" + a]), np.asarray(v["L1_ffn_" + b])[None]], 0)
    A["L2a_q"], A["L2a_kv"], A["L2a_o"], A["L2a_g"] = (C(v["L2_attn_" + n]) for n in ("Wq", "Wkv", "Wout", "Wg"))
    A["L2a_w"] = C(v["L2_attn_norm_w"])
    for n in "rkv":
        A["L2f_" + n] = T(v["L2_ffn_W_" + n])
    A["L2f_mr"], A["L2f_mk"] = C(v["L2_ffn_mu_r"]), C(v["L2_ffn_mu_k"])
    for n in "qkvp":
        A["L3x_" + n] = T(v["L3_xattn_W" + n])
    A["L3x_ff"] = C(v["L3_xattn_focusing_factor"]).reshape(1)
    w = C(v["L3_attn_Wqkv"])
    bq = C(v["L3_attn_bqkv"])
    A["L3a_q"], A["L3a_k"], A["L3a_v"] = C(w[:, 0:256]), C(w[:, 256:512]), headpad(w[:, 512:768])
    A["L3a_qb"], A["L3a_kb"], A["L3a_vb"] = C(bq[0:256]), C(bq[256:512]), headpad(bq[512:768])
    A["L3a_o"] = T(headpad(T(v["L3_attn_Wout"])))
    A["L3a_ob"] = C(v["L3_attn_bout"])
    for l in range(2):
        A[f"L3f_qkv{l}"] = C(np.asarray(v["L3_ffn_wqkv"])[l])
        A[f"L3f_o{l}"] = C(np.asarray(v["L3_ffn_wo"])[l])
        w1 = np.asarray(v["L3_ffn_w1"])[l]
        p = np.zeros((256, 2, 768), w1.dtype)
        p[:, :, :HID] = w1.reshape(256, 2, HID)
        A[f"L3f_w1{l}"] = p.reshape(256, 1536)
        w2 = np.asarray(v["L3_ffn_w2"])[l]
        p = np.zeros((768, 256), w2.dtype)
        p[:HID] = w2
        A[f"L3f_w2{l}"] = p
    b1 = np.asarray(v["L3_ffn_b1"])
    p = np.zeros((2, 2, 768), b1.dtype)
    p[:, :, :HID] = b1.reshape(2, 2, HID)
    A["L3f_b1"] = p.reshape(2, 1536)
    A["L3f_b2"], A["L3f_lg"], A["L3f_lb"] = C(v["L3_ffn_b2"]), C(v["L3_ffn_ln_g"]), C(v["L3_ffn_ln_b"])
    A["L3f_qs"], A["L3f_ks"] = C(v["L3_ffn_q_scale"]), C(v["L3_ffn_k_scale"])
    half = np.arange(0, 64, 2, dtype=f)
    invf = 1.0 / 10000.0 ** (half / 64)
    t = np.arange(256, dtype=f)
    fr = t[:, None] * invf[None, :]
    fr = np.concatenate([fr, fr], -1)
    base = (half + 0.4 * 64) / (1.4 * 64)
    sc = base[None, :] ** ((t - 128) / 64.0)[:, None]
    sc = np.concatenate([sc, sc], -1)
    cs, sn = np.cos(fr), np.sin(fr)
    sgn = np.where(np.arange(64) < 32, -1.0, 1.0)
    tab = np.concatenate([cs * sc * 8.0, sn * sc * 8.0 * sgn, cs / sc, sn / sc * sgn], 1).astype(f)
    A["L3f_tab"] = np.ascontiguousarray(np.tile(tab, (2, 1)))
    for n in ("L0x_qb", "L0x_kb", "L0a_g", "L0a_b", "L2a_w", "L2f_mr", "L2f_mk", "L3a_qb", "L3a_kb"):
        A[n] = T(A[n].reshape(-1, 128))
    for n in ("L3f_b1", "L3f_lg", "L3f_lb"):
        A[n] = np.ascontiguousarray(A[n].reshape(2, -1, 128).transpose(0, 2, 1))
    one = np.full((1, 4096), 0x3F803F80, np.uint32).view(f)
    A["c_krows"] = np.repeat(one[:, :2048], 3, axis=0)
    A["c_qrows"] = np.concatenate([np.zeros((3, 4096), f), one], 0)
    A["c_id"] = np.eye(128, dtype=f)
    i, j = np.arange(256)[:, None], np.arange(256)[None, :]
    ms = [j > i, np.abs(i - j) > 128, (i < j) | (i > j + 128)]
    ms = [np.where(m, -BIG, 0.0).astype(f).reshape(2, 128, 256).transpose(1, 0, 2).reshape(128, 512) for m in ms]
    A["c_msk"] = np.ascontiguousarray(np.concatenate(ms, 1))
    s = np.zeros((128, 17), f)
    for q in range(4):
        s[32 * q:32 * q + 17] = np.eye(17, dtype=f)
    A["c_hm8"] = np.repeat(np.eye(8, dtype=f), 16, axis=0)
    hm = np.repeat(np.eye(16, dtype=f), 16, axis=0)
    A["c_hm16"] = hm
    A["c_bmask"] = np.ascontiguousarray(np.repeat(hm, 16, axis=1))
    lo = (np.arange(16)[None, :] < np.arange(16)[:, None]).astype(f)
    A["c_lower"] = np.ascontiguousarray(np.broadcast_to(lo.reshape(1, 256), (128, 256)))
    return A


def program(nc, arrays, stage=12):
    D = {n: nc.dram_tensor("in_" + n, a.shape, mybir.dt.from_np(a.dtype), kind="ExternalInput").ap()
         for n, a in arrays.items()}
    D["scr"] = nc.dram_tensor("scratch_mask", [2, 8192], BF, kind="Internal").ap()
    D["scrq"] = nc.dram_tensor("scratch_q", [3, 256, 512], BF, kind="Internal").ap()
    out = nc.dram_tensor("out_0", [512, 256], F, kind="ExternalOutput").ap()
    build(nc, D, out, stage)


def kernel(**inputs):
    import concourse.bacc as _bacc
    from concourse.bass_utils import run_bass_kernel_spmd as _run

    arrays = host_arrays(inputs)
    nc = _bacc.Bacc("TRN2", target_bir_lowering=False, num_devices=1)
    program(nc, arrays)
    r = _run(nc, [{"in_" + n: a for n, a in arrays.items()}], core_ids=[0])
    return np.asarray(r.results[0]["out_0"]).reshape(2, 256, 256)
```
